# Optimizing a Trainium2 kernel written in Bass

```python
import numpy as np
import jax
import jax.numpy as jnp

def _softmax(x, axis=-1):
    return jax.nn.softmax(x, axis=axis)

def _gelu(x):
    return jax.nn.gelu(x, approximate=True)

def _silu(x):
    return jax.nn.silu(x)

def _sigmoid(x):
    return jax.nn.sigmoid(x)

def _layernorm(x, axis=-1, eps=1e-05):
    m = jnp.mean(x, axis=axis, keepdims=True)
    v = jnp.var(x, axis=axis, keepdims=True)
    return (x - m) / jnp.sqrt(v + eps)

def _scatter_add(tgt, idx, src, axis=0):
    return tgt.at[idx].add(src)

def _segment_sum(src, seg, n):
    return jax.ops.segment_sum(src, seg, n)
kernel_name = 'mk_seq_postln_d2_jaxref_r8_30b169'

def setup_inputs(seed: int=0):
    np.random.seed(seed)
    _w = jnp.asarray

    def _L0_attn_setup():
        import jax, jax.numpy as jnp
        import numpy as np
        D_IN = 128
        D_OUT = 128
        NUM_HEADS = 16
        HEAD_DIM = D_OUT // NUM_HEADS
        CLIP = 16
        key = jax.random.key(seed)
        ks = jax.random.split(key, 7)
        x = jax.random.normal(ks[0], (4, 128, D_IN), dtype=jnp.float32)
        s = 0.02
        W_q = jax.random.normal(ks[1], (D_IN, D_OUT), dtype=jnp.float32) * s
        W_k = jax.random.normal(ks[2], (D_IN, D_OUT), dtype=jnp.float32) * s
        W_v = jax.random.normal(ks[3], (D_IN, D_OUT), dtype=jnp.float32) * s
        W_o = jax.random.normal(ks[4], (D_OUT, D_OUT), dtype=jnp.float32) * s
        b_o = jnp.zeros((D_OUT,), dtype=jnp.float32)
        rel_k = jax.random.normal(ks[5], (2 * CLIP + 1, HEAD_DIM), dtype=jnp.float32)
        rel_v = jax.random.normal(ks[6], (2 * CLIP + 1, HEAD_DIM), dtype=jnp.float32)
        return {'x': x, 'W_q': W_q, 'W_k': W_k, 'W_v': W_v, 'W_o': W_o, 'b_o': b_o, 'rel_k': rel_k, 'rel_v': rel_v}
    _L0_attn_in = _L0_attn_setup()

    def _L0_ffn_setup():
        import jax, jax.numpy as jnp
        import numpy as np
        DIM = 128

        def _reference_tuple_inner(x, W_r, W_k, W_v, mu_r, mu_k):
            B, T, C = x.shape
            x_prev = jnp.concatenate([jnp.zeros((B, 1, C), x.dtype), x[:, :-1, :]], axis=1)
            xr = mu_r * x + (1.0 - mu_r) * x_prev
            xk = mu_k * x + (1.0 - mu_k) * x_prev
            r = jax.nn.sigmoid(jnp.einsum('btc,dc->btd', xr, W_r))
            k = jnp.einsum('btc,dc->btd', xk, W_k)
            k_act = jnp.square(jax.nn.relu(k))
            out = r * jnp.einsum('btc,dc->btd', k_act, W_v)
            new_state = x[:, -1, :]
            return (out, new_state)
        key = jax.random.key(seed)
        ks = jax.random.split(key, 6)
        B, T, C = (8, 256, DIM)
        x = jax.random.normal(ks[0], (B, T, C), dtype=jnp.float32)
        s = 1.0 / np.sqrt(C)
        W_r = jax.random.uniform(ks[1], (C, C), jnp.float32, -s, s)
        W_k = jax.random.uniform(ks[2], (C, C), jnp.float32, -s, s)
        W_v = jax.random.uniform(ks[3], (C, C), jnp.float32, -s, s)
        mu_r = jax.random.uniform(ks[4], (C,), jnp.float32)
        mu_k = jax.random.uniform(ks[5], (C,), jnp.float32)
        return {'x': x, 'W_r': W_r, 'W_k': W_k, 'W_v': W_v, 'mu_r': mu_r, 'mu_k': mu_k}
    _L0_ffn_in = _L0_ffn_setup()

    def _L1_attn_setup():
        import jax, jax.numpy as jnp
        import numpy as np
        B, T, E = (4, 256, 128)
        H, D = (8, 128)

        def sinusoidal_pe(length, dim, dtype=jnp.float32):
            pos = jnp.arange(length, dtype=jnp.float32)[:, None]
            inv_freq = jnp.exp(-jnp.log(jnp.float32(10000.0)) * (jnp.arange(0, dim, 2, dtype=jnp.float32) / dim))
            ang = pos * inv_freq[None, :]
            pe = jnp.zeros((length, dim), dtype=jnp.float32)
            pe = pe.at[:, 0::2].set(jnp.sin(ang)).at[:, 1::2].set(jnp.cos(ang))
            return pe.astype(dtype)
        key = jax.random.key(seed)
        kx, kq, kk, kv, ko = jax.random.split(key, 5)
        s = 0.02
        return {'x': jax.random.normal(kx, (B, T, E), dtype=jnp.float32), 'Wq': jax.random.normal(kq, (H * D, E), dtype=jnp.float32) * s, 'Wk': jax.random.normal(kk, (D, E), dtype=jnp.float32) * s, 'Wv': jax.random.normal(kv, (D, E), dtype=jnp.float32) * s, 'Wo': jax.random.normal(ko, (E, H * D), dtype=jnp.float32) * s}
    _L1_attn_in = _L1_attn_setup()

    def _L1_ffn_setup():
        import jax, jax.numpy as jnp
        import numpy as np
        E = 8
        TOPK = 2

        def _moe_forward(x, Wg, W1, W2, W3):
            B, S, D = x.shape
            xt = x.reshape(-1, D)
            T = xt.shape[0]
            logits = xt @ Wg.T
            scores = jax.nn.softmax(logits, axis=-1)
            w, idx = jax.lax.top_k(scores, TOPK)
            w = w / (w.sum(axis=-1, keepdims=True) + 1e-20)
            cw = jnp.zeros((T, E), xt.dtype).at[jnp.arange(T)[:, None], idx].add(w)
            h = jax.nn.silu(jnp.einsum('td,ehd->teh', xt, W1)) * jnp.einsum('td,ehd->teh', xt, W3)
            out = jnp.einsum('teh,edh->ted', h, W2)
            y = jnp.einsum('te,ted->td', cw, out)
            return y.reshape(B, S, D)
        key = jax.random.key(seed)
        k0, k1, k2, k3, k4 = jax.random.split(key, 5)
        B, S, D, H = (1, 256, 128, 352)
        scale = 0.02
        x = jax.random.normal(k0, (B, S, D), jnp.float32)
        Wg = jax.random.normal(k1, (E, D), jnp.float32) * scale
        W1 = jax.random.normal(k2, (E, H, D), jnp.float32) * scale
        W2 = jax.random.normal(k3, (E, D, H), jnp.float32) * scale
        W3 = jax.random.normal(k4, (E, H, D), jnp.float32) * scale
        return {'x': x, 'Wg': Wg, 'W1': W1, 'W2': W2, 'W3': W3}
    _L1_ffn_in = _L1_ffn_setup()
    _d = {'L0_attn_x': _L0_attn_in['x'], 'L0_attn_W_q': _L0_attn_in['W_q'], 'L0_attn_W_k': _L0_attn_in['W_k'], 'L0_attn_W_v': _L0_attn_in['W_v'], 'L0_attn_W_o': _L0_attn_in['W_o'], 'L0_attn_b_o': _L0_attn_in['b_o'], 'L0_attn_rel_k': _L0_attn_in['rel_k'], 'L0_attn_rel_v': _L0_attn_in['rel_v'], 'L0_ffn_W_r': _L0_ffn_in['W_r'], 'L0_ffn_W_k': _L0_ffn_in['W_k'], 'L0_ffn_W_v': _L0_ffn_in['W_v'], 'L0_ffn_mu_r': _L0_ffn_in['mu_r'], 'L0_ffn_mu_k': _L0_ffn_in['mu_k'], 'L1_attn_Wq': _L1_attn_in['Wq'], 'L1_attn_Wk': _L1_attn_in['Wk'], 'L1_attn_Wv': _L1_attn_in['Wv'], 'L1_attn_Wo': _L1_attn_in['Wo'], 'L1_ffn_Wg': _L1_ffn_in['Wg'], 'L1_ffn_W1': _L1_ffn_in['W1'], 'L1_ffn_W2': _L1_ffn_in['W2'], 'L1_ffn_W3': _L1_ffn_in['W3']}
    _x0 = _d['L0_attn_x']
    _d['L0_attn_x'] = jax.random.normal(jax.random.fold_in(jax.random.key(seed), 1), (8, 512, 128), dtype=_x0.dtype)
    del _x0
    return _d

def reference(L0_attn_x, L0_attn_W_q, L0_attn_W_k, L0_attn_W_v, L0_attn_W_o, L0_attn_b_o, L0_attn_rel_k, L0_attn_rel_v, L0_ffn_W_r, L0_ffn_W_k, L0_ffn_W_v, L0_ffn_mu_r, L0_ffn_mu_k, L1_attn_Wq, L1_attn_Wk, L1_attn_Wv, L1_attn_Wo, L1_ffn_Wg, L1_ffn_W1, L1_ffn_W2, L1_ffn_W3):

    def _L0_attn_ref(x, W_q, W_k, W_v, W_o, b_o, rel_k, rel_v):
        import jax, jax.numpy as jnp
        import numpy as np
        D_IN = 128
        D_OUT = 128
        NUM_HEADS = 16
        HEAD_DIM = D_OUT // NUM_HEADS
        CLIP = 16
        b, n, _ = x.shape
        h, d = (NUM_HEADS, HEAD_DIM)
        q = (x @ W_q).reshape(b, n, h, d).transpose(0, 2, 1, 3)
        k = (x @ W_k).reshape(b, n, h, d).transpose(0, 2, 1, 3)
        v = (x @ W_v).reshape(b, n, h, d).transpose(0, 2, 1, 3)
        r = jnp.arange(n)
        rel_idx = jnp.clip(r[None, :] - r[:, None], -CLIP, CLIP) + CLIP
        a_k = rel_k[rel_idx]
        a_v = rel_v[rel_idx]
        scores = jnp.einsum('bhid,bhjd->bhij', q, k) + jnp.einsum('bhid,ijd->bhij', q, a_k)
        causal = jnp.triu(jnp.ones((n, n), dtype=bool), k=1)
        scores = jnp.where(causal[None, None], -jnp.inf, scores)
        attn = jax.nn.softmax(scores / jnp.sqrt(jnp.float32(d)), axis=-1)
        ctx = jnp.einsum('bhij,bhjd->bhid', attn, v) + jnp.einsum('bhij,ijd->bhid', attn, a_v)
        ctx = ctx.transpose(0, 2, 1, 3).reshape(b, n, h * d)
        return ctx @ W_o + b_o

    def _L0_ffn_ref(x, W_r, W_k, W_v, mu_r, mu_k):
        import jax, jax.numpy as jnp
        import numpy as np
        DIM = 128

        def _reference_tuple_inner(x, W_r, W_k, W_v, mu_r, mu_k):
            B, T, C = x.shape
            x_prev = jnp.concatenate([jnp.zeros((B, 1, C), x.dtype), x[:, :-1, :]], axis=1)
            xr = mu_r * x + (1.0 - mu_r) * x_prev
            xk = mu_k * x + (1.0 - mu_k) * x_prev
            r = jax.nn.sigmoid(jnp.einsum('btc,dc->btd', xr, W_r))
            k = jnp.einsum('btc,dc->btd', xk, W_k)
            k_act = jnp.square(jax.nn.relu(k))
            out = r * jnp.einsum('btc,dc->btd', k_act, W_v)
            new_state = x[:, -1, :]
            return (out, new_state)
        return _reference_tuple_inner(x, W_r, W_k, W_v, mu_r, mu_k)[0]

    def _L1_attn_ref(x, Wq, Wk, Wv, Wo):
        import jax, jax.numpy as jnp
        import numpy as np
        B, T, E = (4, 256, 128)
        H, D = (8, 128)

        def sinusoidal_pe(length, dim, dtype=jnp.float32):
            pos = jnp.arange(length, dtype=jnp.float32)[:, None]
            inv_freq = jnp.exp(-jnp.log(jnp.float32(10000.0)) * (jnp.arange(0, dim, 2, dtype=jnp.float32) / dim))
            ang = pos * inv_freq[None, :]
            pe = jnp.zeros((length, dim), dtype=jnp.float32)
            pe = pe.at[:, 0::2].set(jnp.sin(ang)).at[:, 1::2].set(jnp.cos(ang))
            return pe.astype(dtype)
        Bv, Tv, Ev = x.shape
        scale = 1.0 / jnp.sqrt(jnp.float32(D)).astype(x.dtype)
        q = (x @ Wq.T).reshape(Bv, Tv, H, D)
        k = (x @ Wk.T).reshape(Bv, Tv, 1, D)
        v = (x @ Wv.T).reshape(Bv, Tv, 1, D)
        k = k + sinusoidal_pe(1, D, k.dtype)
        q = jnp.transpose(q, (0, 2, 1, 3))
        k1 = k[:, :, 0, :]
        v1 = v[:, :, 0, :]
        q = q + sinusoidal_pe(Tv, D, q.dtype)[None, None]
        scores = jnp.einsum('bhtd,bsd->bhts', q, k1) * scale
        causal = jnp.tril(jnp.ones((Tv, Tv), dtype=bool))
        scores = jnp.where(causal[None, None], scores, jnp.finfo(scores.dtype).min)
        probs = jax.nn.softmax(scores, axis=-1)
        attn = jnp.einsum('bhts,bsd->bhtd', probs, v1)
        out = jnp.transpose(attn, (0, 2, 1, 3)).reshape(Bv, Tv, H * D)
        return out @ Wo.T

    def _L1_ffn_ref(x, Wg, W1, W2, W3):
        import jax, jax.numpy as jnp
        import numpy as np
        E = 8
        TOPK = 2

        def _moe_forward(x, Wg, W1, W2, W3):
            B, S, D = x.shape
            xt = x.reshape(-1, D)
            T = xt.shape[0]
            logits = xt @ Wg.T
            scores = jax.nn.softmax(logits, axis=-1)
            w, idx = jax.lax.top_k(scores, TOPK)
            w = w / (w.sum(axis=-1, keepdims=True) + 1e-20)
            cw = jnp.zeros((T, E), xt.dtype).at[jnp.arange(T)[:, None], idx].add(w)
            h = jax.nn.silu(jnp.einsum('td,ehd->teh', xt, W1)) * jnp.einsum('td,ehd->teh', xt, W3)
            out = jnp.einsum('teh,edh->ted', h, W2)
            y = jnp.einsum('te,ted->td', cw, out)
            return y.reshape(B, S, D)
        return _moe_forward(x, Wg, W1, W2, W3)
    x = L0_attn_x
    x = _layernorm(x + _L0_attn_ref(x, L0_attn_W_q, L0_attn_W_k, L0_attn_W_v, L0_attn_W_o, L0_attn_b_o, L0_attn_rel_k, L0_attn_rel_v), axis=-1)
    x = _layernorm(x + _L0_ffn_ref(x, L0_ffn_W_r, L0_ffn_W_k, L0_ffn_W_v, L0_ffn_mu_r, L0_ffn_mu_k), axis=-1)
    x = _layernorm(x + _L1_attn_ref(x, L1_attn_Wq, L1_attn_Wk, L1_attn_Wv, L1_attn_Wo), axis=-1)
    x = _layernorm(x + _L1_ffn_ref(x, L1_ffn_Wg, L1_ffn_W1, L1_ffn_W2, L1_ffn_W3), axis=-1)
    return x

_drawn_inputs = setup_inputs


def setup_inputs(seed=0):
    import zlib

    import numpy as np

    out = dict(_drawn_inputs(seed))
    spreads = {'L0_attn_b_o': (0.0, 0.1)}
    factors = {'L0_attn_W_q': 8.0,
     'L0_attn_W_k': 8.0,
     'L0_attn_W_v': 8.0,
     'L0_attn_rel_k': 8.0,
     'L0_ffn_W_r': 3.151,
     'L0_ffn_mu_r': 6.349,
     'L1_attn_Wq': 8.0,
     'L1_attn_Wk': 8.0,
     'L1_ffn_Wg': 8.0,
     'L1_ffn_W1': 8.0,
     'L1_ffn_W2': 8.0,
     'L1_ffn_W3': 8.0}
    for name, (base, spread) in spreads.items():
        noise = np.random.default_rng([zlib.crc32(name.encode()), seed]).standard_normal(out[name].shape)
        drawn = base * np.exp(spread * noise) if base else spread * noise
        out[name] = jnp.asarray(drawn.astype(out[name].dtype))
    for name, factor in factors.items():
        out[name] = (out[name] * factor).astype(out[name].dtype)
    return out
```

```python
from contextlib import ExitStack

import concourse.bass as bass
import concourse.mybir as mybir
import numpy as np

ALU = mybir.AluOpType
ACT = mybir.ActivationFunctionType
AX = mybir.AxisListType
F32 = mybir.dt.float32
BF16 = mybir.dt.bfloat16

P = 128
NB, N, C = 8, 512, 128
TT = N // P
H0, D0, CLIP = 16, 8, 16
HG = 4
G0 = H0 // HG
STRIP = P // HG
R = CLIP
WIN = P + R
WG = WIN // R
HALF = 2
HH = H0 // HALF
H1 = 8
E, HF = 8, 352
KT = [(0, 128), (128, 128), (256, 96)]
EPS = 1e-5
SC0 = float(1.0 / np.sqrt(np.float32(D0)))
SC1 = float(1.0 / np.sqrt(np.float32(C)))
NEG = -1.0e30
U0 = G0 * TT
NSTEP = 6
NGATE = 22
U1 = H1 * TT


def build(nc, x, wq0, wk0, wv0, wo0, bo, relk, relv, wr, wkf, wvf, mur, muk,
          wq1, wk1, wv1, wo1, wg, w1, w2, w3, c_ident, c_near, c_causal, c_head, c_pe, c_pe0, out):
    ctx = ExitStack()
    with ctx:
        ctx.enter_context(nc.allow_non_contiguous_dma(reason="small tables laid out once"))

        def sb(name, shape, dt=F32):
            return ctx.enter_context(nc.sbuf_tensor(name, shape, dt))

        def sem(name):
            return ctx.enter_context(nc.semaphore(name))

        ident = sb("ident", [P, P])
        near = sb("near", [P, WG, R])
        causal = sb("causal", [P, P], BF16)
        causal_f = sb("causal_f", [P, P])
        ident_b = sb("ident_b", [P, P], BF16)
        headmask = sb("headmask", [P, H0])
        wq_sb = sb("wq_sb", [P, C])
        wv_sb = sb("wv_sb", [P, C])
        wo_sb = sb("wo_sb", [P, C])
        wqg = sb("wqg", [P, G0, HG, STRIP])
        wkg = sb("wkg", [P, G0, HG, STRIP])
        bo_sb = sb("bo_sb", [P, C])
        relk0 = sb("relk0", [P, 1])
        relv0 = sb("relv0", [P, 1])
        reltab = sb("reltab", [P, 2, R + 1])
        reld = sb("reld", [P, 2, 2, R])
        rotk = sb("rotk", [P, R, H0, R])
        rotv_src = sb("rotv_src", [P, 2, H0, R])
        rotv = sb("rotv", [P, R, HALF, P])
        wr_sb = sb("wr_sb", [P, C])
        wkf_sb = sb("wkf_sb", [P, C])
        wvf_sb = sb("wvf_sb", [P, C])
        mu = sb("mu", [P, 2])
        omu = sb("omu", [P, 2])
        wq1_sb = sb("wq1_sb", [P, H1, C])
        wk1_sb = sb("wk1_sb", [P, C])
        wv1_sb = sb("wv1_sb", [P, C])
        wo1_sb = sb("wo1_sb", [P, H1, C])
        wg_sb = sb("wg_sb", [P, E])
        w1_sb = sb("w1_sb", [P, E, HF])
        w3_sb = sb("w3_sb", [P, E, HF])
        w2_sb = sb("w2_sb", [P, E, len(KT), C])
        pe_sb = sb("pe_sb", [P, N])
        pe0_sb = sb("pe0_sb", [P, 1])
        eps_sb = sb("eps_sb", [P, 1])

        x_sb = sb("x_sb", [P, TT, C])
        xb = sb("xb", [P, TT, C])
        xT = sb("xT", [P, N])
        qT = sb("qT", [P, N])
        qg = sb("qg", [P, G0, N])
        kg = sb("kg", [P, G0, N])
        vp = sb("vp", [P, TT, H0, STRIP])
        cT = sb("cT", [P, HALF, N])
        cN = sb("cN", [P, TT, H0, R])
        corr = sb("corr", [P, 2, HG, WG, R])
        prob = sb("prob", [P, 2, HG, N])
        pwin = sb("pwin", [P, 2, HG, WG, R])
        band = sb("band", [P, TT, H0, R])
        probT = sb("probT", [P, 2, HG, TT, P])
        negmax = sb("negmax", [P, U0, HG])
        rowsum = sb("rowsum", [P, TT, H0])
        rinv = sb("rinv", [P, TT, H0])
        ctxs = sb("ctxs", [P, 2, P])
        ctxn = sb("ctxn", [P, TT, H0, D0])
        bandT = sb("bandT", [P, HALF, N])
        crel = sb("crel", [P, N])
        ctxT = sb("ctxT", [P, N])
        res = sb("res", [P, TT, C])
        xn = sb("xn", [P, TT, C])
        stats = sb("stats", [P, TT, 6])
        mv = sb("mv", [P, TT, 2])
        lnv = sb("lnv", [P, TT])
        rstd = sb("rstd", [P, TT])
        nwt = sb("nwt", [P, 2, TT])
        xsh = sb("xsh", [P, N + 1])
        mix = sb("mix", [P, 2, N])
        nm1 = sb("nm1", [P, U1])
        rs1 = sb("rs1", [P, U1])
        ri1 = sb("ri1", [P, U1])
        gsm = sb("gsm", [P, 12, TT, E])
        g1 = sb("g1", [P, 8, TT])
        top = sb("top", [P, TT, 8])
        cw = sb("cw", [P, TT, E])
        y = sb("y", [P, TT, C])

        q1 = prob[:].rearrange("p a h n -> p (a h) n")
        a1 = probT[:].rearrange("p a h j i -> p (a h) (j i)")
        hT = prob[:].rearrange("p a h n -> p (a h) n")[:, 0:2 * len(KT), :].rearrange("p (a k) n -> p a k n", a=2)
        k1 = qg[:, 0, :]
        v1 = qg[:, 1, :].rearrange("p (t c) -> p t c", c=C)
        er, kr = qg[:, 2, :], qg[:, 3, :]
        ksq, rv = kg[:, 0, :], kg[:, 1, :]
        p1 = kg[:, 2:4, :]
        p1T = cT[:].rearrange("p a (j i) -> p a j i", i=P)
        sg = bandT
        mixp = cN[:].rearrange("p t h r -> p (t h r)").rearrange("p (a n) -> p a n", a=2)

        ps_s = ctx.enter_context(nc.psum_tensor("ps_s", [P, HG, N], F32))
        ps_t = ctx.enter_context(nc.psum_tensor("ps_t", [P, 2, N], F32))
        ps_a = ctx.enter_context(nc.psum_tensor("ps_a", [P, 2, N], F32))

        loads = sem("loads")
        setup_zero = sem("setup_zero")
        setup_v = sem("setup_v")
        setup_t_mm, setup_t, reld_ready = sem("setup_t_mm"), sem("setup_t"), sem("reld_ready")
        x_in = sem("x_in")
        x_free = sem("x_free")
        ln_s, ln_n, gate_s = sem("ln_s"), sem("ln_n"), sem("gate_s")
        turn = sem("turn")
        y_free = sem("y_free")
        xT_mm, xT_ev = sem("xT_mm"), sem("xT_ev")
        proj_mm, q_ev, kv_ev = sem("proj_mm"), sem("q_ev"), sem("kv_ev")
        c_mm, cT_ev_a, cT_ev_v, cN_ev = sem("c_mm"), sem("cT_ev_a"), sem("cT_ev_v"), sem("cN_ev")
        corr_ready = sem("corr_ready")
        score_mm, near_added, max_ready, exp_done = sem("score_mm"), sem("near_added"), sem("max_ready"), sem("exp_done")
        pT_mm, pT_ev_a, pT_ev_v = sem("pT_mm"), sem("pT_ev_a"), sem("pT_ev_v")
        pwin_ready, band_ready = sem("pwin_ready"), sem("band_ready")
        ctx_mm, ctx_ev, ctxt_mm, ctxn_ready, rinv_ready = sem("ctx_mm"), sem("ctx_ev"), sem("ctxt_mm"), sem("ctxn_ready"), sem("rinv_ready")
        bandn_ready, bandT_mm, bandT_ev_a, bandT_ev_v = sem("bandn_ready"), sem("bandT_mm"), sem("bandT_ev_a"), sem("bandT_ev_v")
        crel_mm, crel_ev, ctxT_mm, ctxT_ready, wo_mm = sem("crel_mm"), sem("crel_ev"), sem("ctxT_mm"), sem("ctxT_ready"), sem("wo_mm")
        xb_ready = sem("xb_ready")
        ln_v, ln_a, xn_ready = sem("ln_v"), sem("ln_a"), sem("xn_ready")
        mix_v, ffn_mm, ffn_a, ksq_ready = sem("mix_v"), sem("ffn_mm"), sem("ffn_a"), sem("ksq_ready")
        proj1_mm, kv1_ev, q1_ev = sem("proj1_mm"), sem("kv1_ev"), sem("q1_ev")
        s1_mm, m1_ready, e1_done, r1_ready, n1_ready = sem("s1_mm"), sem("m1_ready"), sem("e1_done"), sem("r1_ready"), sem("n1_ready")
        t1_mm, t1_ev_a, t1_ev_v, a1_mm, a1_ev, o1_mm = sem("t1_mm"), sem("t1_ev_a"), sem("t1_ev_v"), sem("a1_mm"), sem("a1_ev"), sem("o1_mm")
        gate_mm, gate_v, gate_a, cw_ready = sem("gate_mm"), sem("gate_v"), sem("gate_a"), sem("cw_ready")
        h_mm, silu_done, hT_ready, y_mm, y_added = sem("h_mm"), sem("silu_done"), sem("hT_ready"), sem("y_mm"), sem("y_added")
        step_v = sem("step_v")

        SETUP = [
            (ident[:], c_ident), (near[:], c_near), (causal_f[:], c_causal), (headmask[:], c_head),
            (wq_sb[:], wq0), (wv_sb[:], wv0), (wo_sb[:], wo0), (bo_sb[:], bo.partition_broadcast(P)),
            (wr_sb[:], wr), (wkf_sb[:], wkf), (wvf_sb[:], wvf),
            (mu[:, 0:1], mur), (mu[:, 1:2], muk),
            (wq1_sb[:], wq1), (wk1_sb[:], wk1), (wv1_sb[:], wv1), (wo1_sb[:], wo1), (wg_sb[:], wg),
            (pe_sb[:], c_pe),
            (w1_sb[:], w1), (w3_sb[:], w3),
            (w2_sb[:, :, 0, :], w2[0:128]), (w2_sb[:, :, 1, :], w2[128:256]), (w2_sb[0:96, :, 2, :], w2[256:352]),
        ]
        SETUP += [(reltab[D0 * h:D0 * h + D0, k, :], t[0:R + 1, :].rearrange("t c -> c t"))
                  for h in range(H0) for k, t in enumerate((relk, relv))]
        PADDED = [(wqg[:, g, :, 0:D0], wq0[:, 32 * g:32 * g + 32].rearrange("p (h c) -> p h c", h=HG)) for g in range(G0)]
        PADDED += [(wkg[:, g, :, 0:D0], wk0[:, 32 * g:32 * g + 32].rearrange("p (h c) -> p h c", h=HG)) for g in range(G0)]
        PADDED += [(relk0[STRIP * h:STRIP * h + D0, :], relk[0:1, :].rearrange("t c -> c t")) for h in range(HG)]
        NLOAD = 16 * (len(SETUP) + len(PADDED))

        def units(b, per, k):
            return b * per + k

        block = ctx.enter_context(nc.Block())

        @block.sync
        def _(sp):
            sp.dma_start(x_sb[:], x[0:1].rearrange("b (t p) c -> p (b t) c", p=P)).then_inc(x_in, 16)
            sp.dma_start(pe0_sb[:], c_pe0).then_inc(y_free, 16)
            for dst, src in SETUP:
                sp.dma_start(dst, src).then_inc(loads, 16)
            sp.wait_ge(setup_zero, 3)
            for dst, src in PADDED:
                sp.dma_start(dst, src).then_inc(loads, 16)
            with sp.Fori(1, NB) as b:
                sp.wait_ge(x_free, b)
                sp.wait_ge(xT_mm, 4 * b - 3)
                sp.dma_start(x_sb[:], x[bass.ds(b, 1)].rearrange("b (t p) c -> p (b t) c", p=P)).then_inc(x_in, 16)
                sp.wait_ge(turn, TT * b + 1)
                sp.dma_start(out[bass.ds(b - 1, 1)].rearrange("b (t p) c -> p (b t) c", p=P), y[:]).then_inc(y_free, 16)
            sp.wait_ge(turn, TT * NB + 1)
            sp.dma_start(out[NB - 1:NB].rearrange("b (t p) c -> p (b t) c", p=P), y[:]).then_inc(y_free, 16)
            sp.wait_ge(y_free, 16 * NB + 16)

        @block.gpsimd
        def _(pool):
            pool.memset(wqg[:], 0.0).then_inc(setup_zero, 1)
            pool.memset(wkg[:], 0.0).then_inc(setup_zero, 1)
            pool.memset(relk0[:], 0.0).then_inc(setup_zero, 1)
            pool.memset(vp[:], 0.0).then_inc(setup_zero, 1)
            pool.memset(xsh[:], 0.0).then_inc(setup_zero, 1)
            pool.wait_ge(loads, NLOAD)

            def spread(b, u):
                g, t = u // TT, u % TT
                w0 = 0 if t else 1
                if u >= 2:
                    pool.wait_ge(near_added, units(b, U0, u - 1))
                pool.tensor_tensor(
                    corr[:, u % 2, :, w0:WG, :],
                    cN[:, t, HG * g:HG * g + HG, :].unsqueeze(2).broadcast_to([P, HG, WG - w0, R]),
                    near[:, w0:WG, :].unsqueeze(1).broadcast_to([P, HG, WG - w0, R]),
                    ALU.mult).then_inc(corr_ready, 1)

            def window(b, u):
                t = u % TT
                w0 = 0 if t else 1
                pool.wait_ge(exp_done, units(b, HG * U0, HG * (u + 1)))
                if u >= 2:
                    pool.wait_ge(band_ready, units(b, U0, u - 1))
                base = (t - 1) * P + P - R + w0 * R
                pool.tensor_tensor(
                    pwin[:, u % 2, :, w0:WG, :],
                    prob[:, u % 2, :, base:base + (WG - w0) * R].rearrange("p h (w r) -> p h w r", r=R),
                    near[:, w0:WG, :].unsqueeze(1).broadcast_to([P, HG, WG - w0, R]),
                    ALU.mult).then_inc(pwin_ready, 1)

            with pool.Fori(0, NB) as b:
                pool.wait_ge(turn, TT * b + 1)
                pool.wait_ge(x_in, 16 * b + 16)
                pool.tensor_tensor(xb[:], x_sb[:], bo_sb[:].unsqueeze(1).broadcast_to([P, TT, C]),
                                   ALU.add).then_inc(x_free, 1)
                pool.wait_ge(cN_ev, units(b, 2, 2))
                spread(b, 0)
                for u in range(U0):
                    if u + 1 < U0:
                        spread(b, u + 1)
                    window(b, u)

        @block.tensor
        def _(pe):
            def transpose_tiles(bank, src, done):
                for t in range(TT):
                    ins = pe.transpose(bank[:, P * t:P * t + P], src[:, t, :], ident[:])
                ins.then_inc(done, 1)

            pe.wait_ge(loads, NLOAD)
            for r in range(R):
                pe.wait_ge(setup_v, 5 + R + r + 1)
                if r >= 2:
                    pe.wait_ge(setup_t, r - 1)
                for half in range(HALF):
                    ins = pe.transpose(ps_t[:, r % 2, P * half:P * half + P],
                                       rotv_src[:, r % 2, HH * half:HH * half + HH, :].rearrange("p h r -> p (h r)"), ident[:])
                ins.then_inc(setup_t_mm, 1)
            pe.wait_ge(setup_t, R)
            pe.wait_ge(setup_v, 5 + 2 * R)

            def scores(b, u):
                g, t = u // TT, u % TT
                n = P * (t + 1)
                if u >= 1:
                    pe.wait_ge(exp_done, units(b, HG * U0, HG * u))
                for h in range(HG):
                    s = STRIP * h
                    pe.matmul(ps_s[:, h, 0:n], qg[s:s + D0, g, P * t:P * t + P], kg[s:s + D0, g, 0:n],
                              start=True, stop=False)
                for h in range(HG):
                    ins = pe.matmul(ps_s[:, h, n - P:n], ident_b[:], causal[:], start=False, stop=True)
                ins.then_inc(score_mm, 1)

            def turn_probs(b, u):
                t = u % TT
                pe.wait_ge(exp_done, units(b, HG * U0, HG * (u + 1)))
                for h in range(HG):
                    k = HG * u + h
                    if k >= 2:
                        uu, hh = (k - 2) // HG, (k - 2) % HG
                        if hh == 3:
                            pe.wait_ge(pT_ev_v, units(b, U0, uu + 1))
                        else:
                            pe.wait_ge(pT_ev_a, units(b, 3 * U0, 3 * uu + hh + 1))
                    for j in range(t + 1):
                        ins = pe.transpose(ps_t[:, k % 2, P * j:P * j + P], prob[:, u % 2, h, P * j:P * j + P], ident[:])
                    ins.then_inc(pT_mm, 1)

            def values(b, u):
                g, t = u // TT, u % TT
                pe.wait_ge(pT_ev_a, units(b, 3 * U0, 3 * (u + 1)))
                pe.wait_ge(pT_ev_v, units(b, U0, u + 1))
                if u >= 2:
                    pe.wait_ge(ctxn_ready, units(b, U0, u - 1))
                for j in range(t + 1):
                    for h in range(HG):
                        s = STRIP * h
                        ins = pe.matmul(ps_a[s:s + STRIP, u % 2, 0:P], vp[:, j, HG * g + h, :],
                                        probT[:, u % 2, h, j, :], start=(j == 0), stop=(j == t))
                ins.then_inc(ctx_mm, 1)

            def turn_ctx(b, u):
                pe.wait_ge(ctx_ev, units(b, U0, u + 1))
                pe.transpose(ps_a[:, u % 2, P:2 * P], ctxs[:, u % 2, :], ident[:]).then_inc(ctxt_mm, 1)

            with pe.Fori(0, NB) as b:
                pe.wait_ge(turn, TT * b + 1)
                pe.wait_ge(x_in, 16 * b + 16)
                transpose_tiles(ps_a[:, 0, :], x_sb, xT_mm)
                pe.wait_ge(xT_ev, units(b, 4, 1))
                for g in range(G0):
                    pe.matmul(ps_s[:, g, :], wqg[:, g].rearrange("p h c -> p (h c)"), xT[:], start=True, stop=True).then_inc(proj_mm, 1)
                pe.matmul(ps_a[:, 0, :], wq_sb[:], xT[:], start=True, stop=True).then_inc(proj_mm, 1)
                for t in range(TT):
                    ins = pe.matmul(ps_a[:, 1, P * t:P * t + P], xT[:, P * t:P * t + P], wv_sb[:], start=True, stop=True)
                ins.then_inc(proj_mm, 1)
                for g in range(G0):
                    bank = ps_t[:, g, :] if g < 2 else ps_s[:, g - 2, :]
                    if g >= 2:
                        pe.wait_ge(q_ev, units(b, G0 + 1, g - 1))
                    pe.matmul(bank, wkg[:, g].rearrange("p h c -> p (h c)"), xT[:], start=True, stop=True).then_inc(proj_mm, 1)
                pe.wait_ge(q_ev, units(b, G0 + 1, G0 + 1))
                pe.wait_ge(kv_ev, units(b, G0 + 1, 1))
                for half in range(HALF):
                    for r in range(R):
                        ins = pe.matmul(ps_a[:, half, STRIP * r:STRIP * r + STRIP],
                                        rotk[:, r, HH * half:HH * half + HH, :].rearrange("p h r -> p (h r)"),
                                        qT[:].rearrange("p (a r) -> p r a", r=R)[:, r, :], start=True, stop=True)
                    ins.then_inc(c_mm, 1)
                pe.wait_ge(cT_ev_a, b + 1)
                pe.wait_ge(cT_ev_v, b + 1)
                pe.wait_ge(kv_ev, units(b, G0 + 1, G0 + 1))
                for t in range(TT):
                    for half in range(HALF):
                        ins = pe.transpose(ps_t[:, t // 2, 256 * (t % 2) + P * half:256 * (t % 2) + P * half + P],
                                           cT[:, half, P * t:P * t + P], ident[:])
                    if t % 2:
                        ins.then_inc(c_mm, 1)
                scores(b, 0)
                pe.wait_ge(cN_ev, units(b, 2, 2))
                for u in range(U0):
                    if u + 1 < U0:
                        scores(b, u + 1)
                    if u >= 1:
                        values(b, u - 1)
                    turn_probs(b, u)
                    if u >= 1:
                        turn_ctx(b, u - 1)
                values(b, U0 - 1)
                turn_ctx(b, U0 - 1)
                pe.wait_ge(bandn_ready, b + 1)
                for half in range(HALF):
                    for t in range(TT):
                        ins = pe.transpose(ps_t[:, half, P * t:P * t + P],
                                           band[:, t, HH * half:HH * half + HH, :].rearrange("p h r -> p (h r)"), ident[:])
                    ins.then_inc(bandT_mm, 1)
                pe.wait_ge(ctxn_ready, units(b, U0, U0))
                for t in range(TT):
                    ins = pe.transpose(ps_a[:, 1, P * t:P * t + P], ctxn[:, t].rearrange("p h c -> p (h c)"), ident[:])
                ins.then_inc(ctxT_mm, 1)
                pe.wait_ge(bandT_ev_a, b + 1)
                pe.wait_ge(bandT_ev_v, b + 1)
                for r in range(R):
                    for half in range(HALF):
                        ins = pe.matmul(ps_a[:, 0, STRIP * r:STRIP * r + STRIP], rotv[:, r, half, :],
                                        bandT[:, half, :].rearrange("p (a r) -> p r a", r=R)[:, r, :],
                                        start=(half == 0), stop=(half == HALF - 1))
                ins.then_inc(crel_mm, 1)
                pe.wait_ge(ctxT_ready, b + 1)
                for t in range(TT):
                    ins = pe.matmul(ps_t[:, 0, P * t:P * t + P], ctxT[:, P * t:P * t + P], wo_sb[:], start=True, stop=True)
                ins.then_inc(wo_mm, 1)

                pe.wait_ge(xn_ready, units(b, 3 * TT, TT))
                transpose_tiles(ps_a[:, 0, :], xn, xT_mm)
                pe.wait_ge(mix_v, units(b, 4, 2))
                for t in range(TT):
                    ins = pe.matmul(ps_s[:, 0, P * t:P * t + P], mix[:, 0, P * t:P * t + P], wr_sb[:], start=True, stop=True)
                ins.then_inc(ffn_mm, 1)
                pe.wait_ge(mix_v, units(b, 4, 4))
                pe.matmul(ps_s[:, 1, :], wkf_sb[:], mix[:, 1, :], start=True, stop=True).then_inc(ffn_mm, 1)
                pe.wait_ge(ksq_ready, b + 1)
                for t in range(TT):
                    ins = pe.matmul(ps_s[:, 2, P * t:P * t + P], ksq[:, P * t:P * t + P], wvf_sb[:], start=True, stop=True)
                ins.then_inc(ffn_mm, 1)

                pe.wait_ge(xn_ready, units(b, 3 * TT, 2 * TT))
                transpose_tiles(ps_a[:, 0, :], xn, xT_mm)
                pe.wait_ge(xT_ev, units(b, 4, 3))
                pe.matmul(ps_s[:, 0, :], wk1_sb[:], xT[:], start=True, stop=True).then_inc(proj1_mm, 1)
                for t in range(TT):
                    ins = pe.matmul(ps_s[:, 1, P * t:P * t + P], xT[:, P * t:P * t + P], wv1_sb[:], start=True, stop=True)
                ins.then_inc(proj1_mm, 1)
                for h in range(H1):
                    if h >= 2:
                        pe.wait_ge(q1_ev, units(b, H1, h - 1))
                    pe.matmul(ps_t[:, h % 2, :], wq1_sb[:, h, :], xT[:], start=True, stop=True).then_inc(proj1_mm, 1)
                pe.wait_ge(kv1_ev, units(b, 2, 2))

                def scores1(w):
                    h, t = w // TT, w % TT
                    n = P * (t + 1)
                    if t == 0:
                        pe.wait_ge(q1_ev, units(b, H1, h + 1))
                    if w >= 4:
                        pe.wait_ge(e1_done, units(b, U1, w - 3))
                    pe.matmul(ps_s[:, w % 4, 0:n], q1[:, h, P * t:P * t + P], k1[:, 0:n], start=True, stop=False)
                    pe.matmul(ps_s[:, w % 4, n - P:n], ident_b[:], causal[:], start=False, stop=True).then_inc(s1_mm, 1)

                def turn1(w):
                    t = w % TT
                    if w == 0:
                        pe.wait_ge(q1_ev, units(b, H1, H1))
                    pe.wait_ge(n1_ready, units(b, U1, w + 1))
                    if w >= 2:
                        if w % 2:
                            pe.wait_ge(t1_ev_v, units(b, U1 // 2, (w - 1) // 2))
                        else:
                            pe.wait_ge(t1_ev_a, units(b, U1 // 2, w // 2))
                    for j in range(t + 1):
                        ins = pe.transpose(ps_t[:, w % 2, P * j:P * j + P], p1[:, w % 2, P * j:P * j + P], ident[:])
                    ins.then_inc(t1_mm, 1)

                def values1(w):
                    h, t = w // TT, w % TT
                    if w % 2:
                        pe.wait_ge(t1_ev_v, units(b, U1 // 2, (w + 1) // 2))
                    else:
                        pe.wait_ge(t1_ev_a, units(b, U1 // 2, w // 2 + 1))
                    if t == 0 and h >= 2:
                        pe.wait_ge(a1_ev, units(b, H1, h - 1))
                    for j in range(t + 1):
                        ins = pe.matmul(ps_a[:, h % 2, P * t:P * t + P], v1[:, j, :], p1T[:, w % 2, j, :],
                                        start=(j == 0), stop=(j == t))
                    ins.then_inc(a1_mm, 1)

                for w in range(3):
                    scores1(w)
                for w in range(U1):
                    if w + 3 < U1:
                        scores1(w + 3)
                    turn1(w)
                    if w >= 1:
                        values1(w - 1)
                values1(U1 - 1)
                pe.wait_ge(a1_ev, units(b, H1, H1))
                for t in range(TT):
                    for h in range(H1):
                        ins = pe.matmul(ps_t[:, 0, P * t:P * t + P], a1[:, h, P * t:P * t + P], wo1_sb[:, h, :],
                                        start=(h == 0), stop=(h == H1 - 1))
                ins.then_inc(o1_mm, 1)

                pe.wait_ge(xn_ready, units(b, 3 * TT, 3 * TT))
                transpose_tiles(ps_a[:, 0, :], xn, xT_mm)
                pe.wait_ge(xT_ev, units(b, 4, 4))
                for t in range(TT):
                    ins = pe.matmul(ps_a[:, 1, E * t:E * t + E], xT[:, P * t:P * t + P], wg_sb[:], start=True, stop=True)
                ins.then_inc(gate_mm, 1)

                def hidden(e):
                    for k, (k0, kn) in enumerate(KT):
                        m = len(KT) * e + k
                        if m >= 2:
                            pe.wait_ge(hT_ready, units(b, len(KT) * E, m - 1))
                        pe.matmul(ps_s[0:kn, 2 * (m % 2), :], w1_sb[:, e, k0:k0 + kn], xT[:], start=True, stop=True).then_inc(h_mm, 1)
                        pe.matmul(ps_s[0:kn, 2 * (m % 2) + 1, :], w3_sb[:, e, k0:k0 + kn], xT[:], start=True, stop=True).then_inc(h_mm, 1)

                def down(e):
                    pe.wait_ge(hT_ready, units(b, len(KT) * E, len(KT) * (e + 1)))
                    if e >= 2:
                        pe.wait_ge(y_added, units(b, TT * E, TT * (e - 1)))
                    for t in range(TT):
                        for k, (k0, kn) in enumerate(KT):
                            ins = pe.matmul(ps_t[:, e % 2, P * t:P * t + P], hT[0:kn, e % 2, k, P * t:P * t + P],
                                            w2_sb[0:kn, e, k, :], start=(k == 0), stop=(k == len(KT) - 1))
                    ins.then_inc(y_mm, 1)

                for e in range(E):
                    hidden(e)
                    if e >= 1:
                        down(e - 1)
                down(E - 1)

        @block.scalar
        def _(act):
            act.wait_ge(loads, NLOAD)
            act.wait_ge(setup_v, 5)
            act.wait_ge(y_free, 16)
            with act.Fori(0, NB) as b:
                act.wait_ge(turn, TT * b + 1)
                act.wait_ge(xT_mm, units(b, 4, 1))
                act.activation(xT[:], ps_a[:, 0, :], ACT.Copy).then_inc(xT_ev, 1)
                for g in range(G0):
                    act.wait_ge(proj_mm, units(b, 2 * G0 + 2, g + 1))
                    act.activation(qg[:, g, :], ps_s[:, g, :], ACT.Copy, scale=SC0).then_inc(q_ev, 1)
                act.wait_ge(proj_mm, units(b, 2 * G0 + 2, G0 + 1))
                act.activation(qT[:], ps_a[:, 0, :], ACT.Copy, scale=SC0).then_inc(q_ev, 1)
                act.wait_ge(c_mm, units(b, 4, 1))
                act.activation(cT[:, 0, :].rearrange("p (a r) -> p r a", r=R),
                               ps_a[:, 0, :].rearrange("p (r a) -> p r a", r=R), ACT.Copy).then_inc(cT_ev_a, 1)

                def ctx_copy(u):
                    act.wait_ge(ctx_mm, units(b, U0, u + 1))
                    if u >= 2:
                        act.wait_ge(ctxt_mm, units(b, U0, u - 1))
                    act.activation(ctxs[:, u % 2, :], ps_a[:, u % 2, 0:P], ACT.Copy).then_inc(ctx_ev, 1)

                def exp0(u, h):
                    g, t = u // TT, u % TT
                    n = P * (t + 1)
                    if h == 0:
                        act.wait_ge(max_ready, units(b, U0, u + 1))
                        if u >= 2:
                            act.wait_ge(pT_mm, units(b, HG * U0, HG * (u - 1)))
                            act.wait_ge(pwin_ready, units(b, U0, u - 1))
                    hd = HG * g + h
                    act.activation(prob[:, u % 2, h, 0:n], ps_s[:, h, 0:n], ACT.Exp, bias=negmax[:, u, h:h + 1],
                                   accum_out=rowsum[:, t, hd:hd + 1]).then_inc(exp_done, 1)

                def pT_copy(u, h):
                    t = u % TT
                    k = HG * u + h
                    act.wait_ge(pT_mm, units(b, HG * U0, k + 1))
                    if h == 0 and u >= 2:
                        act.wait_ge(ctx_mm, units(b, U0, u - 1))
                    act.activation(probT[:, u % 2, h, 0:t + 1, :].rearrange("p j i -> p (j i)"),
                                   ps_t[:, k % 2, 0:P * (t + 1)], ACT.Copy).then_inc(pT_ev_a, 1)

                for h in range(HG):
                    exp0(0, h)
                for u in range(U0):
                    if u >= 1:
                        ctx_copy(u - 1)
                    for h in range(HG):
                        if h < 3:
                            pT_copy(u, h)
                        if u + 1 < U0:
                            exp0(u + 1, h)
                ctx_copy(U0 - 1)
                act.wait_ge(bandT_mm, units(b, 2, 1))
                act.activation(bandT[:, 0, :], ps_t[:, 0, :], ACT.Copy).then_inc(bandT_ev_a, 1)
                act.wait_ge(crel_mm, b + 1)
                act.activation(crel[:].rearrange("p (a r) -> p r a", r=R), ps_a[:, 0, :].rearrange("p (r a) -> p r a", r=R),
                               ACT.Identity, bias=relv0[:, 0:1]).then_inc(crel_ev, 1)

                def rstd_ln(k):
                    act.wait_ge(ln_v, units(b, 4, k + 1))
                    act.activation(lnv[:], mv[:, :, 1], ACT.Ln, bias=eps_sb[:, 0:1]).then_inc(ln_a, 1)
                    act.wait_ge(ln_a, units(b, 8, 2 * k + 1))
                    act.activation(rstd[:], lnv[:], ACT.Exp, scale=-0.5).then_inc(ln_a, 1)

                rstd_ln(0)
                act.wait_ge(xT_mm, units(b, 4, 2))
                act.activation(xsh[:, 1:N + 1], ps_a[:, 0, :], ACT.Copy).then_inc(xT_ev, 1)
                act.wait_ge(ffn_mm, units(b, 3, 1))
                act.activation(er[:], ps_s[:, 0, :], ACT.Exp, scale=-1.0).then_inc(ffn_a, 1)
                act.wait_ge(ffn_mm, units(b, 3, 2))
                act.activation(kr[:], ps_s[:, 1, :], ACT.Relu).then_inc(ffn_a, 1)
                rstd_ln(1)
                act.wait_ge(xT_mm, units(b, 4, 3))
                act.activation(xT[:], ps_a[:, 0, :], ACT.Copy).then_inc(xT_ev, 1)
                act.wait_ge(proj1_mm, units(b, H1 + 2, 1))
                act.activation(k1[:], ps_s[:, 0, :], ACT.Identity, bias=pe0_sb[:, 0:1]).then_inc(kv1_ev, 1)
                act.wait_ge(proj1_mm, units(b, H1 + 2, 2))
                act.activation(v1[:].rearrange("p t c -> p (t c)"), ps_s[:, 1, :], ACT.Copy).then_inc(kv1_ev, 1)

                def exp1(w):
                    t = w % TT
                    n = P * (t + 1)
                    act.wait_ge(m1_ready, units(b, U1, w + 1))
                    if w >= 2:
                        act.wait_ge(t1_mm, units(b, U1, w - 1))
                    act.activation(p1[:, w % 2, 0:n], ps_s[:, w % 4, 0:n], ACT.Exp, bias=nm1[:, w:w + 1],
                                   accum_out=rs1[:, w:w + 1]).then_inc(e1_done, 1)

                def p1T_copy(w):
                    t = w % TT
                    act.wait_ge(t1_mm, units(b, U1, w + 1))
                    if w >= 2:
                        act.wait_ge(a1_mm, units(b, U1, w - 1))
                    act.activation(p1T[:, w % 2, 0:t + 1, :].rearrange("p j i -> p (j i)"),
                                   ps_t[:, w % 2, 0:P * (t + 1)], ACT.Copy).then_inc(t1_ev_a, 1)

                def a1_copy(h):
                    act.wait_ge(a1_mm, units(b, U1, TT * (h + 1)))
                    act.activation(a1[:, h, :], ps_a[:, h % 2, :], ACT.Copy).then_inc(a1_ev, 1)

                exp1(0)
                exp1(1)
                for w in range(U1):
                    if w % 2 == 0:
                        p1T_copy(w)
                    if w + 2 < U1:
                        exp1(w + 2)
                    if w % TT == 0 and w >= TT:
                        a1_copy(w // TT - 1)
                a1_copy(H1 - 1)
                rstd_ln(2)
                act.wait_ge(xT_mm, units(b, 4, 4))
                act.activation(xT[:], ps_a[:, 0, :], ACT.Copy).then_inc(xT_ev, 1)
                act.wait_ge(gate_v, units(b, 2, 2))
                act.activation(gsm[:, 1], gsm[:, 0], ACT.Exp).then_inc(gate_a, 1)
                for m in range(len(KT) * E):
                    kn = KT[m % len(KT)][1]
                    act.wait_ge(h_mm, units(b, 2 * len(KT) * E, 2 * m + 1))
                    if m >= 2:
                        act.wait_ge(hT_ready, units(b, len(KT) * E, m - 1))
                    act.activation(sg[0:kn, m % 2, :], ps_s[0:kn, 2 * (m % 2), :], ACT.Silu).then_inc(silu_done, 1)
                rstd_ln(3)

        @block.vector
        def _(dve):
            dve.memset(eps_sb[:], EPS).then_inc(setup_v, 1)
            dve.memset(y[:], 0.0).then_inc(turn, 1)
            dve.wait_ge(loads, NLOAD)
            dve.tensor_copy(causal[:], causal_f[:]).then_inc(setup_v, 1)
            dve.tensor_copy(ident_b[:], ident[:]).then_inc(setup_v, 1)
            dve.tensor_scalar(omu[:], mu[:], -1.0, 1.0, ALU.mult, ALU.add).then_inc(setup_v, 1)
            dve.tensor_copy(relv0[:], reltab[:, 1, 0:1]).then_inc(setup_v, 1)
            for k in range(2):
                for rep in range(2):
                    ins = dve.tensor_scalar(reld[:, k, rep, :], reltab[:, k, 1:R + 1], reltab[:, k, 0:1], None, ALU.subtract)
                    ins.then_inc(reld_ready, 1)
            dve.wait_ge(reld_ready, 4)
            for k in range(2):
                flat = reld[:, k].rearrange("p a r -> p (a r)")
                for r in range(R):
                    if k == 1 and r >= 2:
                        dve.wait_ge(setup_t_mm, r - 1)
                    dst = rotk[:, r] if k == 0 else rotv_src[:, r % 2]
                    dve.tensor_tensor(dst, flat[:, R - 1 - r:2 * R - 1 - r].unsqueeze(1).broadcast_to([P, H0, R]),
                                      headmask[:].unsqueeze(2).broadcast_to([P, H0, R]), ALU.mult).then_inc(setup_v, 1)
                    if k == 1 and r >= 1:
                        dve.wait_ge(setup_t_mm, r)
                        dve.tensor_copy(rotv[:, r - 1].rearrange("p h c -> p (h c)"), ps_t[:, (r - 1) % 2, 0:2 * P]).then_inc(setup_t, 1)
            dve.wait_ge(setup_t_mm, R)
            dve.tensor_copy(rotv[:, R - 1].rearrange("p h c -> p (h c)"), ps_t[:, (R - 1) % 2, 0:2 * P]).then_inc(setup_t, 1)
            dve.wait_ge(setup_zero, 5)

            with dve.Fori(0, NB) as b:
                dve.wait_ge(turn, TT * b + 1)
                dve.wait_ge(xT_mm, units(b, 4, 1))
                dve.wait_ge(proj_mm, units(b, 2 * G0 + 2, G0 + 2))
                dve.tensor_copy(vp[:, :, :, 0:D0], ps_a[:, 1, :].rearrange("p (t h c) -> p t h c", t=TT, c=D0)).then_inc(kv_ev, 1)
                for g in range(G0):
                    bank = ps_t[:, g, :] if g < 2 else ps_s[:, g - 2, :]
                    dve.wait_ge(proj_mm, units(b, 2 * G0 + 2, G0 + 3 + g))
                    dve.tensor_scalar(kg[:, g, :], bank, relk0[:, 0:1], None, ALU.add).then_inc(kv_ev, 1)
                dve.wait_ge(c_mm, units(b, 4, 2))
                dve.tensor_copy(cT[:, 1, :].rearrange("p (a r) -> p r a", r=R),
                                ps_a[:, 1, :].rearrange("p (r a) -> p r a", r=R)).then_inc(cT_ev_v, 1)
                for k in range(2):
                    dve.wait_ge(c_mm, units(b, 4, 3 + k))
                    dve.tensor_copy(cN[:, 2 * k:2 * k + 2].rearrange("p t h r -> p (t h r)"), ps_t[:, k, :]).then_inc(cN_ev, 1)

                def unit_max(u):
                    t = u % TT
                    n = P * (t + 1)
                    w0 = 0 if t else 1
                    nw = (WG - w0) * R
                    dve.wait_ge(score_mm, units(b, U0, u + 1))
                    dve.wait_ge(corr_ready, units(b, U0, u + 1))
                    dve.tensor_tensor(ps_s[:, :, n - nw:n], ps_s[:, :, n - nw:n],
                                      corr[:, u % 2, :, w0:WG, :].rearrange("p h w r -> p h (w r)"),
                                      ALU.add).then_inc(near_added, 1)
                    dve.wait_ge(near_added, units(b, U0, u + 1))
                    dve.tensor_reduce(negmax[:, u, :], ps_s[:, :, 0:n], AX.X, ALU.max, negate=True).then_inc(max_ready, 1)

                def unit_ctx(u):
                    g, t = u // TT, u % TT
                    dve.wait_ge(ctxt_mm, units(b, U0, u + 1))
                    dve.wait_ge(rinv_ready, units(b, U0, u + 1))
                    dve.tensor_tensor(ctxn[:, t, HG * g:HG * g + HG, :],
                                      ps_a[:, u % 2, P:2 * P].rearrange("p (h c) -> p h c", h=HG)[:, :, 0:D0],
                                      rinv[:, t, HG * g:HG * g + HG].unsqueeze(2).broadcast_to([P, HG, D0]),
                                      ALU.mult).then_inc(ctxn_ready, 1)

                unit_max(0)
                for u in range(U0):
                    g, t = u // TT, u % TT
                    k = HG * u + 3
                    w0 = 0 if t else 1
                    if u + 1 < U0:
                        unit_max(u + 1)
                    dve.wait_ge(exp_done, units(b, HG * U0, HG * (u + 1)))
                    dve.reciprocal(rinv[:, t, HG * g:HG * g + HG], rowsum[:, t, HG * g:HG * g + HG]).then_inc(rinv_ready, 1)
                    dve.wait_ge(pwin_ready, units(b, U0, u + 1))
                    dve.tensor_reduce(band[:, t, HG * g:HG * g + HG, :],
                                      pwin[:, u % 2, :, w0:WG, :].rearrange("p h w r -> p h r w"),
                                      AX.X, ALU.add).then_inc(band_ready, 1)
                    dve.wait_ge(pT_mm, units(b, HG * U0, k + 1))
                    if u >= 2:
                        dve.wait_ge(ctx_mm, units(b, U0, u - 1))
                    dve.tensor_copy(probT[:, u % 2, 3, 0:t + 1, :].rearrange("p j i -> p (j i)"),
                                    ps_t[:, k % 2, 0:P * (t + 1)]).then_inc(pT_ev_v, 1)
                    if u >= 1:
                        unit_ctx(u - 1)
                dve.wait_ge(band_ready, units(b, U0, U0))
                dve.wait_ge(rinv_ready, units(b, U0, U0))
                dve.tensor_tensor(band[:].rearrange("p t h r -> p (t h) r"), band[:].rearrange("p t h r -> p (t h) r"),
                                  rinv[:].rearrange("p t h -> p (t h)").unsqueeze(2).broadcast_to([P, TT * H0, R]),
                                  ALU.mult).then_inc(bandn_ready, 1)
                unit_ctx(U0 - 1)
                dve.wait_ge(bandT_mm, units(b, 2, 2))
                dve.tensor_copy(bandT[:, 1, :], ps_t[:, 1, :]).then_inc(bandT_ev_v, 1)
                dve.wait_ge(ctxT_mm, b + 1)
                dve.wait_ge(crel_ev, b + 1)
                dve.tensor_tensor(ctxT[:], ps_a[:, 1, :], crel[:], ALU.add).then_inc(ctxT_ready, 1)
                dve.wait_ge(wo_mm, b + 1)
                dve.wait_ge(x_free, b + 1)
                dve.tensor_tensor(res[:].rearrange("p t c -> p (t c)"), ps_t[:, 0, :], xb[:].rearrange("p t c -> p (t c)"),
                                  ALU.add).then_inc(step_v, 1)

                def layer_norm(k, src, dst, ready, src_sem, src_val):
                    dve.wait_ge(src_sem, src_val)
                    for t in range(TT):
                        dve.bn_stats(stats[:, t, :], src[:, t, :]).then_inc(ln_s, 1)
                    dve.wait_ge(ln_s, units(b, 8 * TT, 2 * TT * k + TT))
                    dve.tensor_copy(nwt[:, 0, :], stats[:, :, 0])
                    for t in range(TT):
                        ins = dve.bn_aggr(mv[:, t, :], stats[:, t, :])
                        ins.then_inc(ln_s, 1)
                    dve.wait_ge(ln_s, units(b, 8 * TT, 2 * TT * k + 2 * TT))
                    dve.tensor_scalar(nwt[:, 1, :], mv[:, :, 1], EPS, 0.5, ALU.add, ALU.mult).then_inc(ln_v, 1)
                    dve.wait_ge(ln_a, units(b, 8, 2 * k + 2))
                    dve.tensor_tensor(nwt[:, 0, :], rstd[:], rstd[:], ALU.mult).then_inc(ln_n, 1)
                    dve.wait_ge(ln_n, units(b, 16, 4 * k + 1))
                    dve.wait_ge(ln_v, units(b, 4, k + 1))
                    dve.tensor_tensor(nwt[:, 0, :], nwt[:, 0, :], nwt[:, 1, :], ALU.mult).then_inc(ln_n, 1)
                    dve.wait_ge(ln_n, units(b, 16, 4 * k + 2))
                    dve.tensor_scalar(nwt[:, 0, :], nwt[:, 0, :], -1.0, 1.5, ALU.mult, ALU.add).then_inc(ln_n, 1)
                    dve.wait_ge(ln_n, units(b, 16, 4 * k + 3))
                    dve.tensor_tensor(rstd[:], rstd[:], nwt[:, 0, :], ALU.mult).then_inc(ln_n, 1)
                    dve.wait_ge(ln_n, units(b, 16, 4 * k + 4))
                    for t in range(TT):
                        dve.tensor_scalar(dst[:, t, :], src[:, t, :], mv[:, t, 0:1], rstd[:, t:t + 1],
                                          ALU.subtract, ALU.mult).then_inc(ready, 1)

                layer_norm(0, res, xn, xn_ready, step_v, units(b, NSTEP, 1))

                dve.wait_ge(xT_ev, units(b, 4, 2))
                for m in range(2):
                    dve.tensor_scalar(mixp[:, m, :], xsh[:, 0:N], omu[:, m:m + 1], None, ALU.mult).then_inc(mix_v, 1)
                    dve.wait_ge(mix_v, units(b, 4, 2 * m + 1))
                    dve.scalar_tensor_tensor(mix[:, m, :], xsh[:, 1:N + 1], mu[:, m:m + 1], mixp[:, m, :],
                                             ALU.mult, ALU.add).then_inc(mix_v, 1)
                dve.wait_ge(ffn_a, units(b, 2, 1))
                dve.tensor_scalar(er[:], er[:], 1.0, None, ALU.add).then_inc(step_v, 1)
                dve.wait_ge(ffn_a, units(b, 2, 2))
                dve.tensor_tensor(ksq[:], kr[:], kr[:], ALU.mult).then_inc(ksq_ready, 1)
                dve.wait_ge(step_v, units(b, NSTEP, 2))
                dve.reciprocal(er[:], er[:]).then_inc(step_v, 1)
                dve.wait_ge(step_v, units(b, NSTEP, 3))
                dve.wait_ge(ffn_mm, units(b, 3, 3))
                dve.tensor_tensor(rv[:], ps_s[:, 2, :], er[:], ALU.mult).then_inc(step_v, 1)
                dve.wait_ge(step_v, units(b, NSTEP, 4))
                dve.wait_ge(xn_ready, units(b, 3 * TT, TT))
                dve.tensor_tensor(res[:].rearrange("p t c -> p (t c)"), rv[:], xn[:].rearrange("p t c -> p (t c)"),
                                  ALU.add).then_inc(step_v, 1)
                layer_norm(1, res, xn, xn_ready, step_v, units(b, NSTEP, 5))

                for h in range(H1):
                    dve.wait_ge(proj1_mm, units(b, H1 + 2, h + 3))
                    dve.scalar_tensor_tensor(q1[:, h, :], ps_t[:, h % 2, :], SC1, pe_sb[:], ALU.mult, ALU.add).then_inc(q1_ev, 1)

                def max1(w):
                    n = P * (w % TT + 1)
                    dve.wait_ge(s1_mm, units(b, U1, w + 1))
                    dve.tensor_reduce(nm1[:, w:w + 1], ps_s[:, w % 4, 0:n], AX.X, ALU.max, negate=True).then_inc(m1_ready, 1)

                max1(0)
                max1(1)
                for w in range(U1):
                    t = w % TT
                    n = P * (t + 1)
                    if w + 2 < U1:
                        max1(w + 2)
                    dve.wait_ge(e1_done, units(b, U1, w + 1))
                    dve.reciprocal(ri1[:, w:w + 1], rs1[:, w:w + 1]).then_inc(r1_ready, 1)
                    if w >= 1 and (w - 1) % 2 == 1:
                        dve.wait_ge(t1_mm, units(b, U1, w))
                        if w >= 3:
                            dve.wait_ge(a1_mm, units(b, U1, w - 2))
                        dve.tensor_copy(p1T[:, 1, 0:(w - 1) % TT + 1, :].rearrange("p j i -> p (j i)"),
                                        ps_t[:, 1, 0:P * ((w - 1) % TT + 1)]).then_inc(t1_ev_v, 1)
                    dve.wait_ge(r1_ready, units(b, U1, w + 1))
                    dve.tensor_scalar(p1[:, w % 2, 0:n], p1[:, w % 2, 0:n], ri1[:, w:w + 1], None, ALU.mult).then_inc(n1_ready, 1)
                dve.wait_ge(t1_mm, units(b, U1, U1))
                dve.wait_ge(a1_mm, units(b, U1, U1 - 2))
                dve.tensor_copy(p1T[:, 1].rearrange("p j i -> p (j i)"), ps_t[:, 1, :]).then_inc(t1_ev_v, 1)
                dve.wait_ge(o1_mm, b + 1)
                dve.wait_ge(xn_ready, units(b, 3 * TT, 2 * TT))
                dve.tensor_tensor(res[:].rearrange("p t c -> p (t c)"), ps_t[:, 0, :], xn[:].rearrange("p t c -> p (t c)"),
                                  ALU.add).then_inc(step_v, 1)
                layer_norm(2, res, xn, xn_ready, step_v, units(b, NSTEP, 6))

                lg = ps_a[:, 1, 0:TT * E].rearrange("p (t e) -> p t e", e=E)

                def wide(a):
                    return a.unsqueeze(2).broadcast_to([P, TT, E])

                steps = [0]

                def then(ins):
                    steps[0] += 1
                    ins.then_inc(gate_s, 1)
                    dve.wait_ge(gate_s, units(b, NGATE, steps[0]))

                dve.wait_ge(gate_mm, b + 1)
                dve.tensor_reduce(g1[:, 0, :], lg, AX.X, ALU.max).then_inc(gate_v, 1)
                dve.wait_ge(gate_v, units(b, 2, 1))
                dve.tensor_tensor(gsm[:, 0], lg, wide(g1[:, 0, :]), ALU.subtract).then_inc(gate_v, 1)
                dve.wait_ge(gate_a, b + 1)
                then(dve.tensor_reduce(g1[:, 1, :], gsm[:, 1], AX.X, ALU.add))
                then(dve.reciprocal(g1[:, 2, :], g1[:, 1, :]))
                then(dve.tensor_tensor(gsm[:, 2], gsm[:, 1], wide(g1[:, 2, :]), ALU.mult))
                dve.tensor_copy(g1[:, 5, :], g1[:, 2, :])
                for t in range(TT):
                    ins = dve.max(top[:, t, :], gsm[:, 2, t, :])
                then(ins)
                then(dve.tensor_tensor(gsm[:, 3], gsm[:, 2], wide(top[:, :, 1]), ALU.is_gt))
                then(dve.tensor_tensor(gsm[:, 4], gsm[:, 2], wide(top[:, :, 1]), ALU.is_equal))
                then(dve.tensor_reduce(g1[:, 3, :], gsm[:, 3], AX.X, ALU.add))
                then(dve.tensor_scalar(g1[:, 4, :], g1[:, 3, :], -1.0, 2.0, ALU.mult, ALU.add))
                src = 4
                for i, s in enumerate((1, 2, 4)):
                    then(dve.tensor_copy(gsm[:, 5 + i, :, 0:s], gsm[:, src, :, 0:s]))
                    then(dve.tensor_tensor(gsm[:, 5 + i, :, s:E], gsm[:, src, :, s:E], gsm[:, src, :, 0:E - s], ALU.add))
                    src = 5 + i
                then(dve.tensor_tensor(gsm[:, 8], gsm[:, 7], wide(g1[:, 4, :]), ALU.is_le))
                then(dve.tensor_tensor(gsm[:, 9], gsm[:, 8], gsm[:, 4], ALU.mult))
                then(dve.tensor_tensor(gsm[:, 10], gsm[:, 9], gsm[:, 3], ALU.add))
                then(dve.tensor_tensor(gsm[:, 11], gsm[:, 10], gsm[:, 2], ALU.mult))
                then(dve.tensor_tensor(g1[:, 5, :], top[:, :, 0], top[:, :, 1], ALU.add))
                then(dve.tensor_scalar(g1[:, 6, :], g1[:, 5, :], 1e-20, None, ALU.add))
                then(dve.reciprocal(g1[:, 7, :], g1[:, 6, :]))
                then(dve.tensor_tensor(cw[:], gsm[:, 11], wide(g1[:, 7, :]), ALU.mult))

                def combine(e):
                    dve.wait_ge(y_mm, units(b, E, e + 1))
                    if e >= 1:
                        dve.wait_ge(y_added, units(b, TT * E, TT * e))
                    for t in range(TT):
                        src = xn if e == 0 else res
                        dve.scalar_tensor_tensor(res[:, t, :], ps_t[:, e % 2, P * t:P * t + P], cw[:, t, e:e + 1],
                                                 src[:, t, :], ALU.mult, ALU.add).then_inc(y_added, 1)

                for m in range(len(KT) * E):
                    e, k = m // len(KT), m % len(KT)
                    kn = KT[k][1]
                    dve.wait_ge(silu_done, units(b, len(KT) * E, m + 1))
                    dve.wait_ge(h_mm, units(b, 2 * len(KT) * E, 2 * m + 2))
                    if k == 0 and e >= 2:
                        dve.wait_ge(y_mm, units(b, E, e - 1))
                    dve.tensor_tensor(hT[0:kn, e % 2, k, :], sg[0:kn, m % 2, :], ps_s[0:kn, 2 * (m % 2) + 1, :],
                                      ALU.mult).then_inc(hT_ready, 1)
                    if k == 1 and e >= 1:
                        combine(e - 1)
                combine(E - 1)
                dve.wait_ge(y_free, 16 * b + 16)
                layer_norm(3, res, y, turn, y_added, units(b, TT * E, TT * E))


def kernel(L0_attn_x, L0_attn_W_q, L0_attn_W_k, L0_attn_W_v, L0_attn_W_o, L0_attn_b_o, L0_attn_rel_k, L0_attn_rel_v,
           L0_ffn_W_r, L0_ffn_W_k, L0_ffn_W_v, L0_ffn_mu_r, L0_ffn_mu_k, L1_attn_Wq, L1_attn_Wk, L1_attn_Wv, L1_attn_Wo,
           L1_ffn_Wg, L1_ffn_W1, L1_ffn_W2, L1_ffn_W3):
    import concourse.bacc as bacc
    from concourse.bass_utils import run_bass_kernel_spmd

    i = np.arange(P)[:, None]
    back = i + R - np.arange(WIN)[None, :]
    near = ((back >= 0) & (back < CLIP)).astype(np.float32).reshape(P, WG, R)
    causal = np.where(np.arange(P)[None, :] > i, np.float32(NEG), np.float32(0)).astype(np.float32)
    head = (i // D0 == np.arange(H0)[None, :]).astype(np.float32)
    inv = np.exp(-np.log(np.float32(10000.0)) * (np.arange(0, C, 2, dtype=np.float32) / np.float32(C))).astype(np.float32)
    ang = (np.arange(N, dtype=np.float32)[:, None] * inv[None, :]).astype(np.float32)
    pe = np.zeros((N, C), np.float32)
    pe[:, 0::2], pe[:, 1::2] = np.sin(ang), np.cos(ang)
    given = {
        "x": L0_attn_x, "wq0": L0_attn_W_q, "wk0": L0_attn_W_k, "wv0": L0_attn_W_v, "wo0": L0_attn_W_o,
        "bo": L0_attn_b_o, "relk": L0_attn_rel_k, "relv": L0_attn_rel_v,
        "wr": L0_ffn_W_r.T, "wkf": L0_ffn_W_k.T, "wvf": L0_ffn_W_v.T,
        "mur": L0_ffn_mu_r[:, None], "muk": L0_ffn_mu_k[:, None],
        "wq1": L1_attn_Wq.T.reshape(C, H1, C), "wk1": L1_attn_Wk.T, "wv1": L1_attn_Wv.T,
        "wo1": L1_attn_Wo.reshape(C, H1, C).transpose(2, 1, 0), "wg": L1_ffn_Wg.T,
        "w1": L1_ffn_W1.transpose(2, 0, 1), "w2": L1_ffn_W2.transpose(2, 0, 1), "w3": L1_ffn_W3.transpose(2, 0, 1),
        "c_ident": np.eye(P, dtype=np.float32), "c_near": near, "c_causal": causal, "c_head": head,
        "c_pe": pe.T * np.float32(SC1), "c_pe0": pe[0][:, None],
    }
    nc = bacc.Bacc("TRN2", target_bir_lowering=False, num_devices=1)
    arrays, args = {}, []
    for name, a in given.items():
        a = np.ascontiguousarray(a)
        arrays[f"in_{name}"] = a
        args.append(nc.dram_tensor(f"in_{name}", a.shape, mybir.dt.from_np(a.dtype), kind="ExternalInput").ap())
    out = nc.dram_tensor("out", (NB, N, C), F32, kind="ExternalOutput").ap()
    build(nc, *args, out)
    r = run_bass_kernel_spmd(nc, [arrays], core_ids=[0])
    return r.results[0]["out"]
```

```python
from contextlib import ExitStack

import concourse.bass as bass
import concourse.mybir as mybir
import numpy as np

ALU = mybir.AluOpType
ACT = mybir.ActivationFunctionType
AX = mybir.AxisListType
F32 = mybir.dt.float32
BF16 = mybir.dt.bfloat16
I32 = mybir.dt.int32

P = 128
NB, N, C = 8, 512, 128
TT = N // P
H0, D0, CLIP = 16, 8, 16
HG = 4
G0 = H0 // HG
STRIP = P // HG
R = CLIP
WIN = P + R
WG = WIN // R
HALF = 2
HH = H0 // HALF
HW = HH * D0
QPART = (0, 0, 1, 1, 0, 2)
KPART = (0, 1, 0, 1, 2, 0)
KS = len(QPART) * D0
HP = H0 // 2
PAIRS = G0 * TT * 2
H1 = 8
E, HF = 8, 352
KT = [(0, 128), (128, 128), (256, 96)]
EPS = 1e-5
SC0 = float(1.0 / np.sqrt(np.float32(D0)))
SC1 = float(1.0 / np.sqrt(np.float32(C)))
NEG = -1.0e30
U0 = G0 * TT
NGATE = 22
NLN = 2 * TT + 13
NH = len(KT) * E
MAGIC = 0x5f3759df
NEWTON = 3
U1 = H1 * TT


def build(nc, x, wq0, wk0, wv0, wo0, bo, relk, relv, wr, wkf, wvf, mur, muk,
          wq1, wk1, wv1, wo1, wg, w1, w2, w3, c_ident, c_near, c_causal, c_head, c_pe, c_pe0, out):
    ctx = ExitStack()
    with ctx:
        ctx.enter_context(nc.allow_non_contiguous_dma(reason="small tables laid out once"))

        def sb(name, shape, dt=F32):
            return ctx.enter_context(nc.sbuf_tensor(name, shape, dt))

        def sem(name):
            return ctx.enter_context(nc.semaphore(name))

        ident = sb("ident", [P, P])
        near = sb("near", [P, WG, R])
        causal = sb("causal", [P, P], BF16)
        ident_b = sb("ident_b", [P, P], BF16)
        headmask = sb("headmask", [P, HH])
        wq_sb = sb("wq_sb", [P, C])
        wk_sb = sb("wk_sb", [P, C])
        wv_sb = sb("wv_sb", [P, C])
        wo_sb = sb("wo_sb", [P, C])
        bo_sb = sb("bo_sb", [P, C])
        relv0 = sb("relv0", [P, 1])
        relk0 = sb("relk0", [P, 1])
        reltab = sb("reltab", [P, 2, R + 1])
        reld = sb("reld", [P, 2, 2, R])
        rotk = sb("rotk", [P, R, HH, R])
        rotv = sb("rotv", [P, R, HALF, HW])
        wr_sb = sb("wr_sb", [P, C])
        wkf_sb = sb("wkf_sb", [P, C])
        wvf_sb = sb("wvf_sb", [P, C])
        mu = sb("mu", [P, 2])
        omu = sb("omu", [P, 2])
        wq1_sb = sb("wq1_sb", [P, H1, C])
        wk1_sb = sb("wk1_sb", [P, C])
        wv1_sb = sb("wv1_sb", [P, C])
        wo1_sb = sb("wo1_sb", [P, H1, C])
        wg_sb = sb("wg_sb", [P, E])
        w1_sb = sb("w1_sb", [P, E, HF])
        w3_sb = sb("w3_sb", [P, E, HF])
        w2_sb = sb("w2_sb", [P, E, len(KT), C])
        pe_sb = sb("pe_sb", [P, N])
        pe0_sb = sb("pe0_sb", [P, 1])

        x_sb = sb("x_sb", [P, TT, C])
        xb = sb("xb", [P, TT, C])
        xT = sb("xT", [P, N])
        qkT = sb("qkT", [P, 2, N])
        parts = sb("parts", [P, 2, 3, N], BF16)
        qs = sb("qs", [P, HP, N], BF16)
        ks = sb("ks", [P, HP, N], BF16)
        vp = sb("vp", [P, TT, H0, STRIP])
        cT = sb("cT", [P, HALF, N])
        cN = sb("cN", [P, TT, H0, R])
        corr = sb("corr", [P, 2, 2, WG, R])
        prob = sb("prob", [P, 2, 2, N])
        pwin = sb("pwin", [P, 2, 2, WG, R])
        band = sb("band", [P, TT, H0, R])
        probT = sb("probT", [P, 2, 2, TT, P])
        negmax = sb("negmax", [P, PAIRS, 2])
        rowsum = sb("rowsum", [P, TT, H0])
        rinv = sb("rinv", [P, TT, H0])
        ctxs = sb("ctxs", [P, 2, P])
        ctxn = sb("ctxn", [P, TT, H0, D0])
        bandT = sb("bandT", [P, HALF, N])
        crel = sb("crel", [P, N])
        ctxT = sb("ctxT", [P, N])
        res_a = sb("res_a", [P, TT, C])
        x1 = sb("x1", [P, TT, C])
        x2 = sb("x2", [P, TT, C])
        xsh = sb("xsh", [P, N + 1])
        mixp, mix = cT, cN[:].rearrange("p t h r -> p (t h r)").rearrange("p (a n) -> p a n", a=2)
        er, kr = qkT[:, 0, :], qkT[:, 1, :]
        ksq, rv = bandT[:, 0, :], bandT[:, 1, :]
        rotv_src = prob[:].rearrange("p a h n -> p (a h n)")[:, 0:2 * P].rearrange("p (a h r) -> p a h r", a=2, h=HH)
        causal_f = crel[:, 0:P]

        yT = sb("yT", [P, N])
        q1 = sb("q1", [P, H1, N])
        k1 = sb("k1", [P, N])
        v1 = sb("v1", [P, TT, C])
        p1 = sb("p1", [P, 3, N])
        p1T = sb("p1T", [P, 2, TT, P])
        nm1 = sb("nm1", [P, U1])
        rs1 = sb("rs1", [P, U1])
        ri1 = sb("ri1", [P, U1])
        res_b = sb("res_b", [P, TT, C])
        x3 = sb("x3", [P, TT, C])
        gsm = sb("gsm", [P, 12, TT, E])
        g1 = sb("g1", [P, 8, TT])
        top = sb("top", [P, TT, 8])
        cw = sb("cw", [P, TT, E])
        y = sb("y", [P, TT, C])
        a1 = q1
        hT = q1[:, 0:2 * len(KT), :].rearrange("p (a k) n -> p a k n", a=2)
        th = p1
        hs = p1T[:].rearrange("p a j i -> p a (j i)")

        class Norm:
            def __init__(self, name):
                self.stats = sb(name + "_stats", [P, TT, 6])
                self.mv = sb(name + "_mv", [P, TT, 2])
                self.hv = sb(name + "_hv", [P, TT])
                self.var = sb(name + "_var", [P, TT])
                self.t = sb(name + "_t", [P, TT])
                self.yr = sb(name + "_yr", [P, TT])
                self.steps = sem(name + "_steps")

        norm_a, norm_b = Norm("norm_a"), Norm("norm_b")
        scratch = nc.dram_tensor("qk_parts", (2, P, 3, N), BF16, kind="Internal").ap()

        psa = ctx.enter_context(nc.psum_tensor("psa", [P, 4, N], F32))
        psb = ctx.enter_context(nc.psum_tensor("psb", [P, 4, N], F32))
        TB, XB = 2, 3

        loads, setup_zero, setup_v = sem("loads"), sem("setup_zero"), sem("setup_v")
        setup_t_mm, setup_t, reld_ready = sem("setup_t_mm"), sem("setup_t"), sem("reld_ready")
        x_in, x_free, turn_a = sem("x_in"), sem("x_free"), sem("turn_a")
        xT_mm, xT_ev = sem("xT_mm"), sem("xT_ev")
        proj_mm, q_ev, k_ev, v_ev = sem("proj_mm"), sem("q_ev"), sem("k_ev"), sem("v_ev")
        q_part, k_part = sem("q_part"), sem("k_part")
        q_split, k_split, parts_out, stack_in = sem("q_split"), sem("k_split"), sem("parts_out"), sem("stack_in")
        c_mm, cT_ev_a, cT_ev_v, ct_mm, cN_ev = sem("c_mm"), sem("cT_ev_a"), sem("cT_ev_v"), sem("ct_mm"), sem("cN_ev")
        corr_ready, score_mm, near_added = sem("corr_ready"), sem("score_mm"), sem("near_added")
        max_ready, exp_done, rinv_ready = sem("max_ready"), sem("exp_done"), sem("rinv_ready")
        pT_mm, pT_ev_a, pT_ev_v = sem("pT_mm"), sem("pT_ev_a"), sem("pT_ev_v")
        pwin_ready, band_ready, bandn_ready = sem("pwin_ready"), sem("band_ready"), sem("bandn_ready")
        ctx_mm, ctx_ev, ctxt_mm, ctxn_ready = sem("ctx_mm"), sem("ctx_ev"), sem("ctxt_mm"), sem("ctxn_ready")
        bandT_mm, bandT_ev_a, bandT_ev_v = sem("bandT_mm"), sem("bandT_ev_a"), sem("bandT_ev_v")
        crel_mm, crel_ev, ctxT_mm, ctxT_ready, wo_mm, res_ready = (sem("crel_mm"), sem("crel_ev"), sem("ctxT_mm"),
                                                                    sem("ctxT_ready"), sem("wo_mm"), sem("res_ready"))
        x1_ready, mix_v, ffn_mm, ffn_a = sem("x1_ready"), sem("mix_v"), sem("ffn_mm"), sem("ffn_a")
        er_v, ksq_ready = sem("er_v"), sem("ksq_ready")
        turn_b, y_free = sem("turn_b"), sem("y_free")
        yT_mm, yT_ev = sem("yT_mm"), sem("yT_ev")
        proj1_mm, kv1_ev, q1_ev = sem("proj1_mm"), sem("kv1_ev"), sem("q1_ev")
        s1_mm, m1_ready, e1_done, r1_ready, n1_ready = sem("s1_mm"), sem("m1_ready"), sem("e1_done"), sem("r1_ready"), sem("n1_ready")
        t1_mm, t1_ev_a, t1_ev_v, a1_mm, a1_ev, o1_mm = sem("t1_mm"), sem("t1_ev_a"), sem("t1_ev_v"), sem("a1_mm"), sem("a1_ev"), sem("o1_mm")
        res1_ready, x3_ready = sem("res1_ready"), sem("x3_ready")
        gate_mm, gate_v, gate_s, gate_a = sem("gate_mm"), sem("gate_v"), sem("gate_s"), sem("gate_a")
        h_mm, tanh_done, hs_ready, hT_ready, y_mm, y_added = (sem("h_mm"), sem("tanh_done"), sem("hs_ready"),
                                                              sem("hT_ready"), sem("y_mm"), sem("y_added"))

        steps_a = [("pre", i, 3.0) for i in range(5)]
        for p in range(PAIRS):
            steps_a += [("p0", p, 1.2), ("p1", p, 0.9), ("p2", p, 0.9)]
        steps_a += [("post", i, 3.0) for i in range(9)]
        steps_b = [("in", 0, 0.5), ("kv", 0, 1.7)] + [("q", h, 0.9) for h in range(H1)] + [("first", 0, 1.0)]
        steps_b += [("w", w, 0.3 + 0.5 * (w % TT + 1)) for w in range(U1)] + [("last", 0, 1.0)]
        steps_b += [("wo", t, 1.7) for t in range(TT)] + [("norm", 0, 0.5), ("in", 1, 0.5), ("gate", 0, 0.3)]
        for e in range(E):
            for k in range(len(KT)):
                steps_b += [("hid", len(KT) * e + k, 1.7)]
                if e and k:
                    steps_b += [("down", 2 * (e - 1) + k - 1, 1.3)]
        steps_b += [("hid", NH, 0.1), ("down", 2 * E - 2, 1.3), ("down", 2 * E - 1, 1.3), ("down", 2 * E, 0.1)]

        def merged():
            total = [sum(s[2] for s in steps) for steps in (steps_a, steps_b)]
            order, at, used = [], [0, 0], [0.0, 0.0]
            while at[0] < len(steps_a) or at[1] < len(steps_b):
                k = 0 if used[0] <= used[1] else 1
                k = k if at[k] < len((steps_a, steps_b)[k]) else 1 - k
                kind, i, weight = (steps_a, steps_b)[k][at[k]]
                order.append((k, kind, i))
                used[k] += weight / total[k]
                at[k] += 1
            return order

        def run_turns(eng, step_a, step_b):
            for kind, i, _ in steps_a:
                step_a(0, kind, i)
            with eng.Fori(1, NB) as b:
                for k, kind, i in merged():
                    (step_b if k else step_a)(b - 1 if k else b, kind, i)
            for kind, i, _ in steps_b:
                step_b(NB - 1, kind, i)

        def units(b, per, k):
            return b * per + k

        def pair(p):
            g, t, q = p // (2 * TT), (p // 2) % TT, p % 2
            return g, t, q, HG * g + 2 * q, P * (t + 1), 0 if t else 1

        SETUP = [
            (ident[:], c_ident), (near[:], c_near), (causal_f, c_causal), (headmask[:], c_head),
            (wq_sb[:], wq0), (wk_sb[:], wk0), (wv_sb[:], wv0), (wo_sb[:], wo0), (bo_sb[:], bo.partition_broadcast(P)),
            (wr_sb[:], wr), (wkf_sb[:], wkf), (wvf_sb[:], wvf), (mu[:, 0:1], mur), (mu[:, 1:2], muk),
        ]
        SETUP += [(reltab[D0 * h:D0 * h + D0, k, :], t[0:R + 1, :].rearrange("t c -> c t"))
                  for h in range(H0) for k, t in enumerate((relk, relv))]
        LATER = [
            (wq1_sb[:], wq1), (wk1_sb[:], wk1), (wv1_sb[:], wv1), (wo1_sb[:], wo1), (wg_sb[:], wg), (pe_sb[:], c_pe),
            (w1_sb[:], w1), (w3_sb[:], w3),
            (w2_sb[:, :, 0, :], w2[0:128]), (w2_sb[:, :, 1, :], w2[128:256]), (w2_sb[0:96, :, 2, :], w2[256:352]),
        ]
        NLOAD, NALL = 16 * len(SETUP), 16 * (len(SETUP) + len(LATER))
        NSETUP_V = 4 + R + R
        STACK = [(t, par, w) for w in range(2) for t in range(len(QPART)) for par in range(2)]

        block = ctx.enter_context(nc.Block())

        @block.sync
        def _(sp):
            def stack(b):
                for w, split in enumerate((q_split, k_split)):
                    sp.wait_ge(split, units(b, 3, 3))
                    sp.dma_start(scratch[w], parts[:, w]).then_inc(parts_out, 16)
                sp.wait_ge(parts_out, units(b, 32, 32))
                for t, par, w in STACK:
                    dst = (qs, ks)[w][64 * par + D0 * t:64 * par + D0 * t + D0]
                    src = scratch[w, :, (QPART, KPART)[w][t], :].rearrange("(hp par c) n -> par c hp n", par=2, c=D0)[par]
                    sp.dma_start(dst, src).then_inc(stack_in, 16)

            sp.dma_start(x_sb[:], x[0:1].rearrange("b (t p) c -> p (b t) c", p=P)).then_inc(x_in, 16)
            sp.dma_start(pe0_sb[:], c_pe0).then_inc(y_free, 16)
            for dst, src in SETUP:
                sp.dma_start(dst, src).then_inc(loads, 16)
            sp.wait_ge(loads, NLOAD)
            for dst, src in LATER:
                sp.dma_start(dst, src).then_inc(loads, 16)
            stack(0)
            sp.wait_ge(x_free, 1)
            sp.wait_ge(xT_mm, 1)
            sp.dma_start(x_sb[:], x[1:2].rearrange("b (t p) c -> p (b t) c", p=P)).then_inc(x_in, 16)
            with sp.Fori(1, NB - 1) as b:
                stack(b)
                sp.wait_ge(x_free, b + 1)
                sp.wait_ge(xT_mm, 2 * b + 1)
                sp.dma_start(x_sb[:], x[bass.ds(b + 1, 1)].rearrange("b (t p) c -> p (b t) c", p=P)).then_inc(x_in, 16)
                sp.wait_ge(turn_b, TT * b + 1)
                sp.dma_start(out[bass.ds(b - 1, 1)].rearrange("b (t p) c -> p (b t) c", p=P), y[:]).then_inc(y_free, 16)
            stack(NB - 1)
            for b in (NB - 2, NB - 1):
                sp.wait_ge(turn_b, TT * (b + 1) + 1)
                sp.dma_start(out[b:b + 1].rearrange("b (t p) c -> p (b t) c", p=P), y[:]).then_inc(y_free, 16)
            sp.wait_ge(y_free, 16 * NB + 16)

        @block.gpsimd
        def _(pool):
            pool.memset(vp[:], 0.0).then_inc(setup_zero, 1)
            pool.memset(xsh[:], 0.0).then_inc(setup_zero, 1)
            pool.wait_ge(loads, NLOAD)

            def spread(b, p):
                g, t, q, h, n, w0 = pair(p)
                if p == 0:
                    pool.wait_ge(cN_ev, units(b, 2, 2))
                if p >= 2:
                    pool.wait_ge(near_added, units(b, PAIRS, p - 1))
                pool.tensor_tensor(corr[:, p % 2, :, w0:WG, :],
                                   cN[:, t, h:h + 2, :].unsqueeze(2).broadcast_to([P, 2, WG - w0, R]),
                                   near[:, w0:WG, :].unsqueeze(1).broadcast_to([P, 2, WG - w0, R]),
                                   ALU.mult).then_inc(corr_ready, 1)

            def window(b, p):
                g, t, q, h, n, w0 = pair(p)
                pool.wait_ge(exp_done, units(b, 2 * PAIRS, 2 * (p + 1)))
                if p >= 2:
                    pool.wait_ge(band_ready, units(b, PAIRS, p - 1))
                pool.tensor_tensor(pwin[:, p % 2, :, w0:WG, :],
                                   prob[:, p % 2, :, n - (WG - w0) * R:n].rearrange("p h (w r) -> p h w r", r=R),
                                   near[:, w0:WG, :].unsqueeze(1).broadcast_to([P, 2, WG - w0, R]),
                                   ALU.mult).then_inc(pwin_ready, 1)

            def step_a(b, kind, i):
                if kind == "pre" and i == 0:
                    pool.wait_ge(turn_a, TT * b + 1)
                    pool.wait_ge(x_in, 16 * b + 16)
                    pool.tensor_tensor(xb[:], x_sb[:], bo_sb[:].unsqueeze(1).broadcast_to([P, TT, C]),
                                       ALU.add).then_inc(x_free, 1)
                if kind == "pre" and i == 1:
                    pool.wait_ge(k_ev, b + 1)
                    pool.wait_ge(k_part, b + 1)
                    pool.tensor_tensor(parts[:, 1, 1, :], qkT[:, 1, :], parts[:, 1, 0, :], ALU.subtract).then_inc(k_split, 1)
                    pool.tensor_tensor(qkT[:, 1, :], qkT[:, 1, :], parts[:, 1, 0, :], ALU.subtract).then_inc(k_split, 1)
                    pool.wait_ge(k_split, units(b, 3, 2))
                    pool.tensor_tensor(parts[:, 1, 2, :], qkT[:, 1, :], parts[:, 1, 1, :], ALU.subtract).then_inc(k_split, 1)
                if kind == "pre" and i == 4:
                    spread(b, 0)
                    spread(b, 1)
                if kind == "p0":
                    window(b, i)
                    if i + 2 < PAIRS:
                        spread(b, i + 2)

            run_turns(pool, step_a, lambda b, kind, i: None)

        @block.tensor
        def _(pe):
            def transpose_tiles(bank, src, done):
                for t in range(TT):
                    ins = pe.transpose(bank[:, P * t:P * t + P], src[:, t, :], ident[:])
                ins.then_inc(done, 1)

            pe.wait_ge(loads, NLOAD)
            for r in range(R):
                pe.wait_ge(setup_v, 4 + R + r + 1)
                if r >= 2:
                    pe.wait_ge(setup_t, r - 1)
                pe.transpose(psa[:, r % 2, 0:P], rotv_src[:, r % 2].rearrange("p h r -> p (h r)"),
                             ident[:]).then_inc(setup_t_mm, 1)
            pe.wait_ge(setup_t, R)

            def scores(b, p):
                g, t, q, h, n, w0 = pair(p)
                if p == 0:
                    pe.wait_ge(stack_in, 16 * len(STACK) * (b + 1))
                    pe.wait_ge(cN_ev, units(b, 2, 2))
                else:
                    pe.wait_ge(exp_done, units(b, 2 * PAIRS, 2 * p))
                for par in range(2):
                    s = 64 * par
                    pe.matmul(psa[:, par, 0:n], qs[s:s + KS, h // 2, P * t:P * t + P], ks[s:s + KS, h // 2, 0:n],
                              start=True, stop=False)
                for par in range(2):
                    ins = pe.matmul(psa[:, par, n - P:n], ident_b[:], causal[:], start=False, stop=True)
                ins.then_inc(score_mm, 1)

            def turn_prob(b, p, par):
                g, t, q, h, n, w0 = pair(p)
                if par == 0:
                    pe.wait_ge(exp_done, units(b, 2 * PAIRS, 2 * (p + 1)))
                    if p:
                        pe.wait_ge(pT_ev_v, units(b, PAIRS, p))
                else:
                    pe.wait_ge(pT_ev_a, units(b, PAIRS, p + 1))
                for j in range(t + 1):
                    ins = pe.transpose(psa[:, TB, P * j:P * j + P], prob[:, p % 2, par, P * j:P * j + P], ident[:])
                ins.then_inc(pT_mm, 1)

            def values(b, p):
                g, t, q, h, n, w0 = pair(p)
                pe.wait_ge(pT_ev_a, units(b, PAIRS, p + 1))
                pe.wait_ge(pT_ev_v, units(b, PAIRS, p + 1))
                if q == 0 and p:
                    pe.wait_ge(ctxn_ready, units(b, U0, p // 2))
                for j in range(t + 1):
                    for par in range(2):
                        s = STRIP * (2 * q + par)
                        ins = pe.matmul(psa[s:s + STRIP, XB, 0:P], vp[:, j, h + par, :], probT[:, p % 2, par, j, :],
                                        start=(j == 0), stop=(j == t))
                ins.then_inc(ctx_mm, 1)

            def turn_ctx(b, u):
                pe.wait_ge(ctx_ev, units(b, U0, u + 1))
                pe.transpose(psa[:, XB, P:2 * P], ctxs[:, u % 2, :], ident[:]).then_inc(ctxt_mm, 1)

            def step_a(b, kind, i):
                if kind == "pre" and i == 0:
                    pe.wait_ge(turn_a, TT * b + 1)
                    pe.wait_ge(x_in, 16 * b + 16)
                    transpose_tiles(psa[:, XB, :], x_sb, xT_mm)
                if kind == "pre" and i == 1:
                    pe.wait_ge(xT_ev, units(b, 2, 1))
                    pe.matmul(psa[:, 1, :], wk_sb[:], xT[:], start=True, stop=True).then_inc(proj_mm, 1)
                    pe.matmul(psa[:, 0, :], wq_sb[:], xT[:], start=True, stop=True).then_inc(proj_mm, 1)
                    for t in range(TT):
                        ins = pe.matmul(psa[:, TB, P * t:P * t + P], xT[:, P * t:P * t + P], wv_sb[:], start=True, stop=True)
                    ins.then_inc(proj_mm, 1)
                if kind == "pre" and i == 2:
                    pe.wait_ge(q_ev, b + 1)
                    pe.wait_ge(v_ev, b + 1)
                    for r in range(R):
                        for half in range(HALF):
                            s = HW * half
                            ins = pe.matmul(psa[:, TB + half, STRIP * r:STRIP * r + STRIP],
                                            rotk[s:s + HW, r].rearrange("p h r -> p (h r)"),
                                            qkT[s:s + HW, 0, :].rearrange("p (a r) -> p r a", r=R)[:, r, :],
                                            start=True, stop=True)
                    ins.then_inc(c_mm, 1)
                if kind == "pre" and i == 3:
                    pe.wait_ge(cT_ev_a, b + 1)
                    pe.wait_ge(cT_ev_v, b + 1)
                    pe.wait_ge(k_part, b + 1)
                    pe.wait_ge(q_part, b + 1)
                    for t in range(TT):
                        for half in range(HALF):
                            at = 2 * P * (t % 2) + P * half
                            ins = pe.transpose(psa[:, t // 2, at:at + P], cT[:, half, P * t:P * t + P], ident[:])
                        if t % 2:
                            ins.then_inc(ct_mm, 1)
                if kind == "pre" and i == 4:
                    scores(b, 0)
                if kind == "p0":
                    turn_prob(b, i, 0)
                    if i + 1 < PAIRS:
                        scores(b, i + 1)
                if kind == "p1":
                    turn_prob(b, i, 1)
                    if i % 2 == 0 and i:
                        turn_ctx(b, i // 2 - 1)
                if kind == "p2":
                    values(b, i)
                if kind == "post" and i == 0:
                    turn_ctx(b, U0 - 1)
                    pe.wait_ge(bandn_ready, b + 1)
                    for half in range(HALF):
                        for t in range(TT):
                            ins = pe.transpose(psa[:, half, P * t:P * t + P],
                                               band[:, t, HH * half:HH * half + HH, :].rearrange("p h r -> p (h r)"), ident[:])
                        ins.then_inc(bandT_mm, 1)
                if kind == "post" and i == 1:
                    pe.wait_ge(ctxn_ready, units(b, U0, U0))
                    for t in range(TT):
                        ins = pe.transpose(psa[:, TB, P * t:P * t + P], ctxn[:, t].rearrange("p h c -> p (h c)"), ident[:])
                    ins.then_inc(ctxT_mm, 1)
                    pe.wait_ge(bandT_ev_a, b + 1)
                    pe.wait_ge(bandT_ev_v, b + 1)
                    for r in range(R):
                        for half in range(HALF):
                            s = HW * half
                            ins = pe.matmul(psa[s:s + HW, XB, STRIP * r:STRIP * r + STRIP], rotv[:, r, half, :],
                                            bandT[:, half, :].rearrange("p (a r) -> p r a", r=R)[:, r, :],
                                            start=True, stop=True)
                    ins.then_inc(crel_mm, 1)
                if kind == "post" and i == 2:
                    pe.wait_ge(ctxT_ready, b + 1)
                    for t in range(TT):
                        ins = pe.matmul(psa[:, 0, P * t:P * t + P], ctxT[:, P * t:P * t + P], wo_sb[:], start=True, stop=True)
                    ins.then_inc(wo_mm, 1)
                if kind == "post" and i == 4:
                    pe.wait_ge(x1_ready, units(b, TT, TT))
                    transpose_tiles(psa[:, XB, :], x1, xT_mm)
                if kind == "post" and i == 5:
                    pe.wait_ge(mix_v, units(b, 4, 4))
                    pe.matmul(psa[:, 1, :], wkf_sb[:], mix[:, 1, :], start=True, stop=True).then_inc(ffn_mm, 1)
                    for t in range(TT):
                        ins = pe.matmul(psa[:, 0, P * t:P * t + P], mix[:, 0, P * t:P * t + P], wr_sb[:], start=True, stop=True)
                    ins.then_inc(ffn_mm, 1)
                if kind == "post" and i == 6:
                    pe.wait_ge(ksq_ready, b + 1)
                    for t in range(TT):
                        ins = pe.matmul(psa[:, TB, P * t:P * t + P], ksq[:, P * t:P * t + P], wvf_sb[:], start=True, stop=True)
                    ins.then_inc(ffn_mm, 1)

            def scores1(b, w):
                h, t = w // TT, w % TT
                n = P * (t + 1)
                if w >= 2:
                    pe.wait_ge(e1_done, units(b, U1, w - 1))
                pe.matmul(psb[:, w % 2, 0:n], q1[:, h, P * t:P * t + P], k1[:, 0:n], start=True, stop=False)
                pe.matmul(psb[:, w % 2, n - P:n], ident_b[:], causal[:], start=False, stop=True).then_inc(s1_mm, 1)

            def wait_p1T(b, w):
                pe.wait_ge(t1_ev_v if w % 2 else t1_ev_a, units(b, U1 // 2, w // 2 + 1))

            def turn1(b, w):
                t = w % TT
                pe.wait_ge(n1_ready, units(b, U1, w + 1))
                if w >= 1:
                    wait_p1T(b, w - 1)
                for j in range(t + 1):
                    ins = pe.transpose(psb[:, TB, P * j:P * j + P], p1[:, w % 3, P * j:P * j + P], ident[:])
                ins.then_inc(t1_mm, 1)

            def values1(b, w):
                h, t = w // TT, w % TT
                wait_p1T(b, w)
                if t == 0 and h:
                    pe.wait_ge(a1_ev, units(b, H1, h))
                for j in range(t + 1):
                    ins = pe.matmul(psb[:, XB, P * t:P * t + P], v1[:, j, :], p1T[:, w % 2, j, :],
                                    start=(j == 0), stop=(j == t))
                ins.then_inc(a1_mm, 1)

            def step_b(b, kind, i):
                if kind == "in" and i == 0:
                    pe.wait_ge(turn_a, TT * (b + 1) + 1)
                    pe.wait_ge(turn_b, TT * b + 1)
                    pe.wait_ge(loads, NALL)
                    transpose_tiles(psb[:, XB, :], x2, yT_mm)
                if kind == "kv":
                    pe.wait_ge(yT_ev, units(b, 2, 1))
                    pe.matmul(psb[:, 0, :], wk1_sb[:], yT[:], start=True, stop=True).then_inc(proj1_mm, 1)
                    for t in range(TT):
                        ins = pe.matmul(psb[:, 1, P * t:P * t + P], yT[:, P * t:P * t + P], wv1_sb[:], start=True, stop=True)
                    ins.then_inc(proj1_mm, 1)
                if kind == "q":
                    if i >= 2:
                        pe.wait_ge(q1_ev, units(b, H1, i - 1))
                    pe.matmul(psb[:, TB + i % 2, :], wq1_sb[:, i, :], yT[:], start=True, stop=True).then_inc(proj1_mm, 1)
                if kind == "first":
                    pe.wait_ge(kv1_ev, units(b, 2, 2))
                    pe.wait_ge(q1_ev, units(b, H1, H1))
                    scores1(b, 0)
                    scores1(b, 1)
                if kind == "w":
                    turn1(b, i)
                    if i + 2 < U1:
                        scores1(b, i + 2)
                    if i:
                        values1(b, i - 1)
                if kind == "last":
                    values1(b, U1 - 1)
                if kind == "wo":
                    if i == 0:
                        pe.wait_ge(a1_ev, units(b, H1, H1))
                    for h in range(H1):
                        ins = pe.matmul(psb[:, 0, P * i:P * i + P], a1[:, h, P * i:P * i + P], wo1_sb[:, h, :],
                                        start=(h == 0), stop=(h == H1 - 1))
                    if i == TT - 1:
                        ins.then_inc(o1_mm, 1)
                if kind == "in" and i == 1:
                    pe.wait_ge(x3_ready, units(b, TT, TT))
                    transpose_tiles(psb[:, XB, :], x3, yT_mm)
                if kind == "gate":
                    pe.wait_ge(yT_ev, units(b, 2, 2))
                    for t in range(TT):
                        ins = pe.matmul(psb[:, XB, E * t:E * t + E], yT[:, P * t:P * t + P], wg_sb[:], start=True, stop=True)
                    ins.then_inc(gate_mm, 1)
                if kind == "hid" and i < NH:
                    e, k = i // len(KT), i % len(KT)
                    k0, kn = KT[k]
                    if i >= 2:
                        pe.wait_ge(hT_ready, units(b, NH, i - 1))
                    pe.matmul(psb[0:kn, (2 * i) % 3, :], w1_sb[:, e, k0:k0 + kn], yT[:], start=True, stop=True).then_inc(h_mm, 1)
                    if i >= 1:
                        pe.wait_ge(hs_ready, units(b, NH, i))
                    pe.matmul(psb[0:kn, (2 * i + 1) % 3, :], w3_sb[:, e, k0:k0 + kn], yT[:], start=True, stop=True).then_inc(h_mm, 1)
                if kind == "down" and i < 2 * E:
                    e, part = i // 2, i % 2
                    if part == 0:
                        pe.wait_ge(hT_ready, units(b, NH, len(KT) * (e + 1)))
                        if e:
                            pe.wait_ge(y_added, units(b, TT * E, TT * e))
                        else:
                            pe.wait_ge(gate_s, units(b, NGATE, NGATE))
                    for t in range(2 * part, 2 * part + 2):
                        for k, (k0, kn) in enumerate(KT):
                            ins = pe.matmul(psb[:, XB, P * t:P * t + P], hT[0:kn, e % 2, k, P * t:P * t + P],
                                            w2_sb[0:kn, e, k, :], start=(k == 0), stop=(k == len(KT) - 1))
                    if part:
                        ins.then_inc(y_mm, 1)

            run_turns(pe, step_a, step_b)

        @block.scalar
        def _(act):
            act.wait_ge(loads, NLOAD)
            act.wait_ge(setup_v, 4)
            act.wait_ge(y_free, 16)

            def exp0(b, p, par):
                g, t, q, h, n, w0 = pair(p)
                if par == 0:
                    act.wait_ge(max_ready, units(b, PAIRS, p + 1))
                    if p >= 2:
                        act.wait_ge(pT_mm, units(b, 2 * PAIRS, 2 * (p - 1)))
                        act.wait_ge(pwin_ready, units(b, PAIRS, p - 1))
                act.activation(prob[:, p % 2, par, 0:n], psa[:, par, 0:n], ACT.Exp, bias=negmax[:, p, par:par + 1],
                               accum_out=rowsum[:, t, h + par:h + par + 1]).then_inc(exp_done, 1)

            def ctx_copy(b, u):
                act.wait_ge(ctx_mm, units(b, PAIRS, 2 * (u + 1)))
                if u >= 2:
                    act.wait_ge(ctxt_mm, units(b, U0, u - 1))
                act.activation(ctxs[:, u % 2, :], psa[:, XB, 0:P], ACT.Copy).then_inc(ctx_ev, 1)

            def step_a(b, kind, i):
                if kind == "pre" and i == 0:
                    act.wait_ge(turn_a, TT * b + 1)
                    act.wait_ge(xT_mm, units(b, 2, 1))
                    act.activation(xT[:], psa[:, XB, :], ACT.Copy).then_inc(xT_ev, 1)
                if kind == "pre" and i == 1:
                    act.wait_ge(k_ev, b + 1)
                    act.activation(parts[:, 1, 0, :], psa[:, 1, :], ACT.Identity, bias=relk0[:, 0:1]).then_inc(k_part, 1)
                    act.wait_ge(proj_mm, units(b, 3, 2))
                    act.activation(qkT[:, 0, :], psa[:, 0, :], ACT.Copy, scale=SC0).then_inc(q_ev, 1)
                    act.activation(parts[:, 0, 0, :], psa[:, 0, :], ACT.Copy, scale=SC0).then_inc(q_part, 1)
                if kind == "pre" and i == 2:
                    act.wait_ge(c_mm, b + 1)
                    act.activation(cT[:, 0, :].rearrange("p (a r) -> p r a", r=R),
                                   psa[:, TB, :].rearrange("p (r a) -> p r a", r=R), ACT.Copy).then_inc(cT_ev_a, 1)
                if kind == "pre" and i == 4:
                    exp0(b, 0, 0)
                    exp0(b, 0, 1)
                if kind == "p0":
                    g, t, q, h, n, w0 = pair(i)
                    act.wait_ge(pT_mm, units(b, 2 * PAIRS, 2 * i + 1))
                    if i >= 2:
                        act.wait_ge(ctx_mm, units(b, PAIRS, i - 1))
                    act.activation(probT[:, i % 2, 0, 0:t + 1, :].rearrange("p j i -> p (j i)"),
                                   psa[:, TB, 0:n], ACT.Copy).then_inc(pT_ev_a, 1)
                if kind == "p1" and i + 1 < PAIRS:
                    exp0(b, i + 1, 0)
                    exp0(b, i + 1, 1)
                if kind == "p2" and i % 2:
                    ctx_copy(b, i // 2)
                if kind == "post" and i == 0:
                    act.wait_ge(bandT_mm, units(b, 2, 1))
                    act.activation(bandT[:, 0, :], psa[:, 0, :], ACT.Copy).then_inc(bandT_ev_a, 1)
                if kind == "post" and i == 1:
                    act.wait_ge(crel_mm, b + 1)
                    act.activation(crel[:].rearrange("p (a r) -> p r a", r=R), psa[:, XB, :].rearrange("p (r a) -> p r a", r=R),
                                   ACT.Identity, bias=relv0[:, 0:1]).then_inc(crel_ev, 1)
                if kind == "post" and i == 4:
                    act.wait_ge(xT_mm, units(b, 2, 2))
                    act.activation(xsh[:, 1:N + 1], psa[:, XB, :], ACT.Copy).then_inc(xT_ev, 1)
                if kind == "post" and i == 5:
                    act.wait_ge(ffn_mm, units(b, 3, 1))
                    act.activation(kr, psa[:, 1, :], ACT.Relu).then_inc(ffn_a, 1)
                    act.wait_ge(ffn_mm, units(b, 3, 2))
                    act.activation(er, psa[:, 0, :], ACT.Exp, scale=-1.0).then_inc(ffn_a, 1)

            def exp1(b, w):
                n = P * (w % TT + 1)
                act.wait_ge(m1_ready, units(b, U1, w + 1))
                if w >= 3:
                    act.wait_ge(t1_mm, units(b, U1, w - 2))
                act.activation(p1[:, w % 3, 0:n], psb[:, w % 2, 0:n], ACT.Exp, bias=nm1[:, w:w + 1],
                               accum_out=rs1[:, w:w + 1]).then_inc(e1_done, 1)

            def step_b(b, kind, i):
                if kind == "in":
                    act.wait_ge(yT_mm, units(b, 2, i + 1))
                    act.activation(yT[:], psb[:, XB, :], ACT.Copy).then_inc(yT_ev, 1)
                if kind == "kv":
                    act.wait_ge(proj1_mm, units(b, H1 + 2, 1))
                    act.activation(k1[:], psb[:, 0, :], ACT.Identity, bias=pe0_sb[:, 0:1]).then_inc(kv1_ev, 1)
                    act.wait_ge(proj1_mm, units(b, H1 + 2, 2))
                    act.activation(v1[:].rearrange("p t c -> p (t c)"), psb[:, 1, :], ACT.Copy).then_inc(kv1_ev, 1)
                if kind == "first":
                    exp1(b, 0)
                    exp1(b, 1)
                if kind == "w":
                    t = i % TT
                    if i % 2 == 0:
                        act.wait_ge(t1_mm, units(b, U1, i + 1))
                        if i >= 2:
                            act.wait_ge(a1_mm, units(b, U1, i - 1))
                        act.activation(p1T[:, 0, 0:t + 1, :].rearrange("p j i -> p (j i)"),
                                       psb[:, TB, 0:P * (t + 1)], ACT.Copy).then_inc(t1_ev_a, 1)
                    if i + 2 < U1:
                        exp1(b, i + 2)
                if (kind == "w" and i % TT == 0 and i) or kind == "last":
                    h = i // TT - 1 if kind == "w" else H1 - 1
                    act.wait_ge(a1_mm, units(b, U1, TT * (h + 1)))
                    act.activation(a1[:, h, :], psb[:, XB, :], ACT.Copy).then_inc(a1_ev, 1)
                if kind == "gate":
                    act.wait_ge(gate_v, units(b, 2, 2))
                    act.activation(gsm[:, 1], gsm[:, 0], ACT.Exp).then_inc(gate_a, 1)
                if kind == "hid" and i < NH:
                    kn = KT[i % len(KT)][1]
                    act.wait_ge(h_mm, units(b, 2 * NH, 2 * i + 1))
                    if i >= 3:
                        act.wait_ge(hs_ready, units(b, NH, i - 2))
                    act.activation(th[0:kn, i % 3, :], psb[0:kn, (2 * i) % 3, :], ACT.Tanh, scale=0.5).then_inc(tanh_done, 1)

            run_turns(act, step_a, step_b)

        @block.vector
        def _(dve):
            dve.memset(y[:], 0.0).then_inc(turn_a, 1)
            dve.memset(xT[:], 0.0).then_inc(turn_b, 1)
            dve.wait_ge(loads, NLOAD)
            dve.tensor_copy(causal[:], causal_f).then_inc(setup_v, 1)
            dve.tensor_copy(ident_b[:], ident[:]).then_inc(setup_v, 1)
            dve.tensor_scalar(omu[:], mu[:], -1.0, 1.0, ALU.mult, ALU.add).then_inc(setup_v, 1)
            dve.tensor_copy(relk0[:], reltab[:, 0, 0:1])
            dve.tensor_copy(relv0[:], reltab[:, 1, 0:1]).then_inc(setup_v, 1)
            for k in range(2):
                for rep in range(2):
                    dve.tensor_scalar(reld[:, k, rep, :], reltab[:, k, 1:R + 1], reltab[:, k, 0:1], None,
                                      ALU.subtract).then_inc(reld_ready, 1)
            dve.wait_ge(reld_ready, 4)
            for k in range(2):
                flat = reld[:, k].rearrange("p a r -> p (a r)")
                for r in range(R):
                    if k == 1 and r >= 2:
                        dve.wait_ge(setup_t_mm, r - 1)
                    dst = rotk[:, r] if k == 0 else rotv_src[:, r % 2]
                    dve.tensor_tensor(dst, flat[:, R - 1 - r:2 * R - 1 - r].unsqueeze(1).broadcast_to([P, HH, R]),
                                      headmask[:].unsqueeze(2).broadcast_to([P, HH, R]), ALU.mult).then_inc(setup_v, 1)
                    if k == 1 and r >= 1:
                        dve.wait_ge(setup_t_mm, r)
                        dve.tensor_copy(rotv[:, r - 1].rearrange("p h c -> p (h c)"), psa[:, (r - 1) % 2, 0:P]).then_inc(setup_t, 1)
            dve.wait_ge(setup_t_mm, R)
            dve.tensor_copy(rotv[:, R - 1].rearrange("p h c -> p (h c)"), psa[:, (R - 1) % 2, 0:P]).then_inc(setup_t, 1)
            dve.wait_ge(setup_zero, 2)

            def layer_norm(b, k, nm, src, dst, ready):
                count = [0]

                def done(ins, wait=True):
                    count[0] += 1
                    ins.then_inc(nm.steps, 1)
                    if wait:
                        dve.wait_ge(nm.steps, units(b, 2 * NLN, NLN * k + count[0]))

                for t in range(TT):
                    done(dve.bn_stats(nm.stats[:, t, :], src[:, t, :]), t == TT - 1)
                done(dve.tensor_copy(nm.t[:], nm.stats[:, :, 0]), False)
                for t in range(TT):
                    done(dve.bn_aggr(nm.mv[:, t, :], nm.stats[:, t, :]), t == TT - 1)
                done(dve.tensor_scalar(nm.var[:], nm.mv[:, :, 1], EPS, None, ALU.add))
                done(dve.tensor_scalar(nm.t[:].bitcast(I32), nm.var[:].bitcast(I32), 1, None, ALU.logical_shift_right))
                done(dve.tensor_scalar(nm.yr[:].bitcast(I32), nm.t[:].bitcast(I32), -1.0, float(MAGIC), ALU.mult, ALU.add))
                for _ in range(NEWTON):
                    done(dve.tensor_tensor(nm.t[:], nm.yr[:], nm.yr[:], ALU.mult))
                    done(dve.scalar_tensor_tensor(nm.hv[:], nm.t[:], -0.5, nm.var[:], ALU.mult, ALU.mult))
                    done(dve.scalar_tensor_tensor(nm.yr[:], nm.hv[:], 1.5, nm.yr[:], ALU.add, ALU.mult))
                assert count[0] == NLN
                for t in range(TT):
                    dve.tensor_scalar(dst[:, t, :], src[:, t, :], nm.mv[:, t, 0:1], nm.yr[:, t:t + 1],
                                      ALU.subtract, ALU.mult).then_inc(ready, 1)

            def flat(a):
                return a[:].rearrange("p t c -> p (t c)")

            def unit_max(b, p):
                g, t, q, h, n, w0 = pair(p)
                nw = (WG - w0) * R
                dve.wait_ge(score_mm, units(b, PAIRS, p + 1))
                dve.wait_ge(corr_ready, units(b, PAIRS, p + 1))
                dve.tensor_tensor(psa[:, 0:2, n - nw:n], psa[:, 0:2, n - nw:n],
                                  corr[:, p % 2, :, w0:WG, :].rearrange("p h w r -> p h (w r)"),
                                  ALU.add).then_inc(near_added, 1)
                dve.wait_ge(near_added, units(b, PAIRS, p + 1))
                dve.tensor_reduce(negmax[:, p, :], psa[:, 0:2, 0:n], AX.X, ALU.max, negate=True).then_inc(max_ready, 1)

            def unit_ctx(b, u):
                g, t = u // TT, u % TT
                dve.wait_ge(ctxt_mm, units(b, U0, u + 1))
                dve.wait_ge(rinv_ready, units(b, PAIRS, 2 * (u + 1)))
                dve.tensor_tensor(ctxn[:, t, HG * g:HG * g + HG, :],
                                  psa[:, XB, P:2 * P].rearrange("p (h c) -> p h c", h=HG)[:, :, 0:D0],
                                  rinv[:, t, HG * g:HG * g + HG].unsqueeze(2).broadcast_to([P, HG, D0]),
                                  ALU.mult).then_inc(ctxn_ready, 1)

            def step_a(b, kind, i):
                if kind == "pre" and i == 0:
                    dve.wait_ge(turn_a, TT * b + 1)
                if kind == "pre" and i == 1:
                    dve.wait_ge(proj_mm, units(b, 3, 1))
                    dve.tensor_scalar(qkT[:, 1, :], psa[:, 1, :], relk0[:, 0:1], None, ALU.add).then_inc(k_ev, 1)
                    dve.wait_ge(proj_mm, units(b, 3, 3))
                    dve.tensor_copy(vp[:, :, :, 0:D0], psa[:, TB, :].rearrange("p (t h c) -> p t h c", t=TT, c=D0)).then_inc(v_ev, 1)
                    dve.wait_ge(q_ev, b + 1)
                    dve.wait_ge(q_part, b + 1)
                    dve.tensor_tensor(parts[:, 0, 1, :], qkT[:, 0, :], parts[:, 0, 0, :], ALU.subtract).then_inc(q_split, 1)
                    dve.tensor_tensor(crel[:], qkT[:, 0, :], parts[:, 0, 0, :], ALU.subtract).then_inc(q_split, 1)
                    dve.wait_ge(q_split, units(b, 3, 2))
                    dve.tensor_tensor(parts[:, 0, 2, :], crel[:], parts[:, 0, 1, :], ALU.subtract).then_inc(q_split, 1)
                if kind == "pre" and i == 2:
                    dve.wait_ge(c_mm, b + 1)
                    dve.tensor_copy(cT[:, 1, :].rearrange("p (a r) -> p r a", r=R),
                                    psa[:, XB, :].rearrange("p (r a) -> p r a", r=R)).then_inc(cT_ev_v, 1)
                if kind == "pre" and i == 3:
                    for k in range(2):
                        dve.wait_ge(ct_mm, units(b, 2, k + 1))
                        dve.tensor_copy(cN[:, 2 * k:2 * k + 2].rearrange("p t h r -> p (t h r)"), psa[:, k, :]).then_inc(cN_ev, 1)
                if kind == "pre" and i == 4:
                    unit_max(b, 0)
                if kind == "p0" and i + 1 < PAIRS:
                    unit_max(b, i + 1)
                if kind == "p1":
                    g, t, q, h, n, w0 = pair(i)
                    dve.wait_ge(pT_mm, units(b, 2 * PAIRS, 2 * i + 2))
                    if i >= 2:
                        dve.wait_ge(ctx_mm, units(b, PAIRS, i - 1))
                    dve.tensor_copy(probT[:, i % 2, 1, 0:t + 1, :].rearrange("p j i -> p (j i)"),
                                    psa[:, TB, 0:n]).then_inc(pT_ev_v, 1)
                    dve.wait_ge(exp_done, units(b, 2 * PAIRS, 2 * (i + 1)))
                    dve.reciprocal(rinv[:, t, h:h + 2], rowsum[:, t, h:h + 2]).then_inc(rinv_ready, 1)
                    if i % 2 == 0 and i:
                        unit_ctx(b, i // 2 - 1)
                if kind == "p2":
                    g, t, q, h, n, w0 = pair(i)
                    dve.wait_ge(pwin_ready, units(b, PAIRS, i + 1))
                    dve.tensor_reduce(band[:, t, h:h + 2, :], pwin[:, i % 2, :, w0:WG, :].rearrange("p h w r -> p h r w"),
                                      AX.X, ALU.add).then_inc(band_ready, 1)
                if kind == "post" and i == 0:
                    dve.wait_ge(band_ready, units(b, PAIRS, PAIRS))
                    dve.wait_ge(rinv_ready, units(b, PAIRS, PAIRS))
                    dve.tensor_tensor(band[:].rearrange("p t h r -> p (t h) r"), band[:].rearrange("p t h r -> p (t h) r"),
                                      rinv[:].rearrange("p t h -> p (t h)").unsqueeze(2).broadcast_to([P, TT * H0, R]),
                                      ALU.mult).then_inc(bandn_ready, 1)
                    unit_ctx(b, U0 - 1)
                    dve.wait_ge(bandT_mm, units(b, 2, 2))
                    dve.tensor_copy(bandT[:, 1, :], psa[:, 1, :]).then_inc(bandT_ev_v, 1)
                if kind == "post" and i == 1:
                    dve.wait_ge(ctxT_mm, b + 1)
                    dve.wait_ge(crel_ev, b + 1)
                    dve.tensor_tensor(ctxT[:], psa[:, TB, :], crel[:], ALU.add).then_inc(ctxT_ready, 1)
                if kind == "post" and i == 2:
                    dve.wait_ge(wo_mm, b + 1)
                    dve.wait_ge(x_free, b + 1)
                    dve.tensor_tensor(flat(res_a), psa[:, 0, :], flat(xb), ALU.add).then_inc(res_ready, 1)
                if kind == "post" and i == 3:
                    dve.wait_ge(res_ready, units(b, 2, 1))
                    layer_norm(b, 0, norm_a, res_a, x1, x1_ready)
                if kind == "post" and i == 4:
                    dve.wait_ge(xT_ev, units(b, 2, 2))
                    for m in range(2):
                        dve.tensor_scalar(mixp[:, m, :], xsh[:, 0:N], omu[:, m:m + 1], None, ALU.mult).then_inc(mix_v, 1)
                        dve.wait_ge(mix_v, units(b, 4, 2 * m + 1))
                        dve.scalar_tensor_tensor(mix[:, m, :], xsh[:, 1:N + 1], mu[:, m:m + 1], mixp[:, m, :],
                                                 ALU.mult, ALU.add).then_inc(mix_v, 1)
                if kind == "post" and i == 5:
                    dve.wait_ge(ffn_a, units(b, 2, 1))
                    dve.tensor_tensor(ksq, kr, kr, ALU.mult).then_inc(ksq_ready, 1)
                    dve.wait_ge(ffn_a, units(b, 2, 2))
                    dve.tensor_scalar(er, er, 1.0, None, ALU.add).then_inc(er_v, 1)
                    dve.wait_ge(er_v, units(b, 3, 1))
                    dve.reciprocal(er, er).then_inc(er_v, 1)
                if kind == "post" and i == 6:
                    dve.wait_ge(er_v, units(b, 3, 2))
                    dve.wait_ge(ffn_mm, units(b, 3, 3))
                    dve.tensor_tensor(rv, psa[:, TB, :], er, ALU.mult).then_inc(er_v, 1)
                if kind == "post" and i == 7:
                    dve.wait_ge(er_v, units(b, 3, 3))
                    dve.wait_ge(x1_ready, units(b, TT, TT))
                    dve.tensor_tensor(flat(res_a), rv, flat(x1), ALU.add).then_inc(res_ready, 1)
                if kind == "post" and i == 8:
                    dve.wait_ge(res_ready, units(b, 2, 2))
                    if not isinstance(b, int):
                        dve.wait_ge(res1_ready, b)
                    layer_norm(b, 1, norm_a, res_a, x2, turn_a)

            def max1(b, w):
                n = P * (w % TT + 1)
                dve.wait_ge(s1_mm, units(b, U1, w + 1))
                dve.tensor_reduce(nm1[:, w:w + 1], psb[:, w % 2, 0:n], AX.X, ALU.max, negate=True).then_inc(m1_ready, 1)

            def norm1(b, w):
                n = P * (w % TT + 1)
                dve.wait_ge(e1_done, units(b, U1, w + 1))
                dve.reciprocal(ri1[:, w:w + 1], rs1[:, w:w + 1]).then_inc(r1_ready, 1)
                dve.wait_ge(r1_ready, units(b, U1, w + 1))
                dve.tensor_scalar(p1[:, w % 3, 0:n], p1[:, w % 3, 0:n], ri1[:, w:w + 1], None, ALU.mult).then_inc(n1_ready, 1)

            def wide(a):
                return a.unsqueeze(2).broadcast_to([P, TT, E])

            def router(b):
                lg = psb[:, XB, 0:TT * E].rearrange("p (t e) -> p t e", e=E)
                steps = [0]

                def then(ins):
                    steps[0] += 1
                    ins.then_inc(gate_s, 1)
                    dve.wait_ge(gate_s, units(b, NGATE, steps[0]))

                dve.wait_ge(gate_mm, b + 1)
                dve.tensor_reduce(g1[:, 0, :], lg, AX.X, ALU.max).then_inc(gate_v, 1)
                dve.wait_ge(gate_v, units(b, 2, 1))
                dve.tensor_tensor(gsm[:, 0], lg, wide(g1[:, 0, :]), ALU.subtract).then_inc(gate_v, 1)
                dve.wait_ge(gate_a, b + 1)
                then(dve.tensor_reduce(g1[:, 1, :], gsm[:, 1], AX.X, ALU.add))
                then(dve.reciprocal(g1[:, 2, :], g1[:, 1, :]))
                then(dve.tensor_tensor(gsm[:, 2], gsm[:, 1], wide(g1[:, 2, :]), ALU.mult))
                dve.tensor_copy(g1[:, 5, :], g1[:, 2, :])
                for t in range(TT):
                    ins = dve.max(top[:, t, :], gsm[:, 2, t, :])
                then(ins)
                then(dve.tensor_tensor(gsm[:, 3], gsm[:, 2], wide(top[:, :, 1]), ALU.is_gt))
                then(dve.tensor_tensor(gsm[:, 4], gsm[:, 2], wide(top[:, :, 1]), ALU.is_equal))
                then(dve.tensor_reduce(g1[:, 3, :], gsm[:, 3], AX.X, ALU.add))
                then(dve.tensor_scalar(g1[:, 4, :], g1[:, 3, :], -1.0, 2.0, ALU.mult, ALU.add))
                src = 4
                for k, s in enumerate((1, 2, 4)):
                    then(dve.tensor_copy(gsm[:, 5 + k, :, 0:s], gsm[:, src, :, 0:s]))
                    then(dve.tensor_tensor(gsm[:, 5 + k, :, s:E], gsm[:, src, :, s:E], gsm[:, src, :, 0:E - s], ALU.add))
                    src = 5 + k
                then(dve.tensor_tensor(gsm[:, 8], gsm[:, 7], wide(g1[:, 4, :]), ALU.is_le))
                then(dve.tensor_tensor(gsm[:, 9], gsm[:, 8], gsm[:, 4], ALU.mult))
                then(dve.tensor_tensor(gsm[:, 10], gsm[:, 9], gsm[:, 3], ALU.add))
                then(dve.tensor_tensor(gsm[:, 11], gsm[:, 10], gsm[:, 2], ALU.mult))
                then(dve.tensor_tensor(g1[:, 5, :], top[:, :, 0], top[:, :, 1], ALU.add))
                then(dve.tensor_scalar(g1[:, 6, :], g1[:, 5, :], 1e-20, None, ALU.add))
                then(dve.reciprocal(g1[:, 7, :], g1[:, 6, :]))
                then(dve.tensor_tensor(cw[:], gsm[:, 11], wide(g1[:, 7, :]), ALU.mult))

            def step_b(b, kind, i):
                if kind == "in" and i == 0:
                    dve.wait_ge(turn_b, TT * b + 1)
                if kind == "q":
                    dve.wait_ge(proj1_mm, units(b, H1 + 2, i + 3))
                    dve.scalar_tensor_tensor(q1[:, i, :], psb[:, TB + i % 2, :], SC1, pe_sb[:], ALU.mult, ALU.add).then_inc(q1_ev, 1)
                if kind == "first":
                    max1(b, 0)
                    max1(b, 1)
                    norm1(b, 0)
                if kind == "w":
                    if i + 2 < U1:
                        max1(b, i + 2)
                    if i % 2:
                        dve.wait_ge(t1_mm, units(b, U1, i + 1))
                        if i >= 2:
                            dve.wait_ge(a1_mm, units(b, U1, i - 1))
                        dve.tensor_copy(p1T[:, 1, 0:i % TT + 1, :].rearrange("p j i -> p (j i)"),
                                        psb[:, TB, 0:P * (i % TT + 1)]).then_inc(t1_ev_v, 1)
                    if i + 1 < U1:
                        norm1(b, i + 1)
                if kind == "norm":
                    dve.wait_ge(o1_mm, b + 1)
                    dve.tensor_tensor(flat(res_b), psb[:, 0, :], flat(x2), ALU.add).then_inc(res1_ready, 1)
                    dve.wait_ge(res1_ready, b + 1)
                    layer_norm(b, 0, norm_b, res_b, x3, x3_ready)
                if kind == "gate":
                    router(b)
                if kind == "hid":
                    if i < NH:
                        kn = KT[i % len(KT)][1]
                        dve.wait_ge(tanh_done, units(b, NH, i + 1))
                        if i >= 2:
                            dve.wait_ge(hT_ready, units(b, NH, i - 1))
                        dve.scalar_tensor_tensor(hs[0:kn, i % 2, :], th[0:kn, i % 3, :], 1.0, psb[0:kn, (2 * i) % 3, :],
                                                 ALU.add, ALU.mult).then_inc(hs_ready, 1)
                    if i >= 1:
                        m = i - 1
                        e, k = m // len(KT), m % len(KT)
                        kn = KT[k][1]
                        dve.wait_ge(hs_ready, units(b, NH, m + 1))
                        dve.wait_ge(h_mm, units(b, 2 * NH, 2 * m + 2))
                        if k == 0 and e >= 2:
                            dve.wait_ge(y_mm, units(b, E, e - 1))
                        dve.scalar_tensor_tensor(hT[0:kn, e % 2, k, :], hs[0:kn, m % 2, :], 0.5, psb[0:kn, (2 * m + 1) % 3, :],
                                                 ALU.mult, ALU.mult).then_inc(hT_ready, 1)
                if kind == "hid" and i % len(KT) == 0 and i >= 2 * len(KT) or kind == "down" and i == 2 * E:
                    e = i // len(KT) - 2 if kind == "hid" else E - 1
                    dve.wait_ge(y_mm, units(b, E, e + 1))
                    if e:
                        dve.wait_ge(y_added, units(b, TT * E, TT * e))
                    for t in range(TT):
                        dve.scalar_tensor_tensor(res_b[:, t, :], psb[:, XB, P * t:P * t + P], cw[:, t, e:e + 1],
                                                 (res_b if e else x3)[:, t, :], ALU.mult, ALU.add).then_inc(y_added, 1)
                if kind == "down" and i == 2 * E:
                    dve.wait_ge(y_free, 16 * b + 16)
                    dve.wait_ge(y_added, units(b, TT * E, TT * E))
                    layer_norm(b, 1, norm_b, res_b, y, turn_b)

            run_turns(dve, step_a, step_b)


def kernel(L0_attn_x, L0_attn_W_q, L0_attn_W_k, L0_attn_W_v, L0_attn_W_o, L0_attn_b_o, L0_attn_rel_k, L0_attn_rel_v,
           L0_ffn_W_r, L0_ffn_W_k, L0_ffn_W_v, L0_ffn_mu_r, L0_ffn_mu_k, L1_attn_Wq, L1_attn_Wk, L1_attn_Wv, L1_attn_Wo,
           L1_ffn_Wg, L1_ffn_W1, L1_ffn_W2, L1_ffn_W3):
    import concourse.bacc as bacc
    from concourse.bass_utils import run_bass_kernel_spmd

    i = np.arange(P)[:, None]
    back = i + R - np.arange(WIN)[None, :]
    near = ((back >= 0) & (back < CLIP)).astype(np.float32).reshape(P, WG, R)
    causal = np.where(np.arange(P)[None, :] > i, np.float32(NEG), np.float32(0)).astype(np.float32)
    head = (i // D0 % HH == np.arange(HH)[None, :]).astype(np.float32)
    inv = np.exp(-np.log(np.float32(10000.0)) * (np.arange(0, C, 2, dtype=np.float32) / np.float32(C))).astype(np.float32)
    ang = (np.arange(N, dtype=np.float32)[:, None] * inv[None, :]).astype(np.float32)
    pe = np.zeros((N, C), np.float32)
    pe[:, 0::2], pe[:, 1::2] = np.sin(ang), np.cos(ang)
    given = {
        "x": L0_attn_x, "wq0": L0_attn_W_q, "wk0": L0_attn_W_k, "wv0": L0_attn_W_v, "wo0": L0_attn_W_o,
        "bo": L0_attn_b_o, "relk": L0_attn_rel_k, "relv": L0_attn_rel_v,
        "wr": L0_ffn_W_r.T, "wkf": L0_ffn_W_k.T, "wvf": L0_ffn_W_v.T,
        "mur": L0_ffn_mu_r[:, None], "muk": L0_ffn_mu_k[:, None],
        "wq1": L1_attn_Wq.T.reshape(C, H1, C), "wk1": L1_attn_Wk.T, "wv1": L1_attn_Wv.T,
        "wo1": L1_attn_Wo.reshape(C, H1, C).transpose(2, 1, 0), "wg": L1_ffn_Wg.T,
        "w1": L1_ffn_W1.transpose(2, 0, 1), "w2": L1_ffn_W2.transpose(2, 0, 1), "w3": L1_ffn_W3.transpose(2, 0, 1),
        "c_ident": np.eye(P, dtype=np.float32), "c_near": near, "c_causal": causal, "c_head": head,
        "c_pe": pe.T * np.float32(SC1), "c_pe0": pe[0][:, None],
    }
    nc = bacc.Bacc("TRN2", target_bir_lowering=False, num_devices=1)
    arrays, args = {}, []
    for name, a in given.items():
        a = np.ascontiguousarray(a)
        arrays[f"in_{name}"] = a
        args.append(nc.dram_tensor(f"in_{name}", a.shape, mybir.dt.from_np(a.dtype), kind="ExternalInput").ap())
    out = nc.dram_tensor("out", (NB, N, C), F32, kind="ExternalOutput").ap()
    build(nc, *args, out)
    r = run_bass_kernel_spmd(nc, [arrays], core_ids=[0])
    return r.results[0]["out"]
```

```python
from contextlib import ExitStack

import concourse.bass as bass
import concourse.mybir as mybir
import numpy as np

ALU = mybir.AluOpType
ACT = mybir.ActivationFunctionType
AX = mybir.AxisListType
F32 = mybir.dt.float32
BF16 = mybir.dt.bfloat16
I32 = mybir.dt.int32

P = 128
NB, N, C = 8, 512, 128
TT = N // P
H0, D0, CLIP = 16, 8, 16
HG = 4
G0 = H0 // HG
STRIP = P // HG
R = CLIP
WIN = P + R
WG = WIN // R
HALF = 2
HH = H0 // HALF
HW = HH * D0
RB = N // P
QPART = (0, 0, 1, 1, 0, 2)
KPART = (0, 1, 0, 1, 2, 0)
KS = len(QPART) * D0
HP = H0 // 2
PAIRS = G0 * TT * 2
H1 = 8
E, HF = 8, 352
KT = [(0, 128), (128, 128), (256, 96)]
EPS = 1e-5
SC0 = float(1.0 / np.sqrt(np.float32(D0)))
SC1 = float(1.0 / np.sqrt(np.float32(C)))
NEG = -1.0e30
U0 = G0 * TT
NGATE = 23
NLN = 2 * TT + 13
NH = len(KT) * E
MAGIC = 0x5f3759df
NEWTON = 3
LN_PARTS = NEWTON + 3
U1 = H1 * TT
TENSOR_ORDER = """
    b4 a1 b2 a2 b1 a1 b1 a4 b2 a1 b1 a3 b1 a1 b3 a2 b2 a2 b1 a1 b3 a1 b1 a2 b1 a2 b2 a1 b1 a1 b1 a1 b2 a1 b1 a1 b2
    a1 b3 a2 b1 a2 b2 a2 b3 a2 b1 a1 b2 a1 b3 a2 b1 a1 b1 a1 b2 a1 b2 a1 b1 a3 b2 a1 b3 a2 b1 a2 b2 a2 b1 a4 b4 a2
    b1 a2 b2 a1 b1 a1 b1 a3 b2 a1 b3 a3 b1 a1 b2 a2 b7 a1 b1 a2 b3 a1 b2 a4 b1 a1 b1 a1 b1 a3 b2 a1 b2 a3 b1 a1 b2
    a2 b4 a2 b1 a2 b1 a2 b1 a2 b1 a2 b1 a9 b8 a1 b1 a1 b5 a1 b1 a2 b2 a2 b1 a2 b1 a2 b2 a3 b1 a1 b1 a2 b1 a2 b1 a2
    b2 a3 b1 a1 b5 a2 b1 a2 b1 a1 b1 a1 b1 a2 b1 a1 b3 a1 b3 a4 b1 a1 b1 a1 b1 a2 b2 a2 b2 a2 b1 a1 b2 a1 b5 a1 b8
    a7 b4 a1 b1 a2 b1 a1 b3 a1 b1 a1 b7"""
SCALAR_ORDER = """
    b1 a1 b1 a9 b9 a2 b3 a3 b2 a2 b4 a3 b2 a2 b2 a2 b2 a1 b2 a2 b4 a3 b2 a2 b4 a3 b2 a2 b4 a3 b2 a2 b5 a3 b1 a2 b4
    a2 b1 a1 b1 a2 b3 a3 b2 a2 b1 a3 b4 a5 b4 a2 b2 a3 b2 a2 b4 a2 b2 a1 b6 a2 b2 a3 b2 a2 b2 a3 b2 a2 b2 a3 b2 a2
    b4 a5 b4 a15 b12 a2 b1 a3 b6 a2 b1 a1 b1 a1 b1 a1 b1 a3 b1 a2 b1 a3 b1 a4 b1 a1 b2 a2 b4 a3 b2 a1 b1 a1 b3 a3 b2
    a2 b3 a3 b1 a1 b3 a4 b3 a2 b3 a4 b3 a1 b2 a1 b12 a8 b3 a1 b1 a2 b2 a1 b1 a1 b6"""
POOL_ORDER = """
    a118 b129 a10 b2 a5 b4 a5 b3 a5 b3 a4 b3 a1 b3 a4 b6 a5 b21 a17 b9 a1 b9"""
VECTOR_ORDER = """
    b4 a1 b2 a2 b1 a3 b1 a2 b2 a1 b1 a2 b2 a4 b4 a1 b2 a2 b2 a1 b2 a2 b1 a2 b1 a2 b2 a1 b4 a3 b3 a2 b3 a5 b6 a3 b2
    a2 b4 a2 b3 a2 b1 a1 b2 a2 b2 a2 b2 a1 b2 a3 b2 a1 b1 a3 b1 a1 b1 a1 b1 a4 b3 a1 b3 a3 b2 a1 b1 a1 b1 a1 b2 a3
    b6 a1 b3 a1 b2 a2 b1 a2 b3 a5 b3 a5 b2 a1 b3 a5 b5 a10 b7 a2 b1 a1 b2 a1 b2 a6 b7 a3 b2 a4 b2 a3 b2 a4 b2 a5 b3
    a3 b5 a3 b1 a3 b3 a1 b3 a1 b2 a2 b1 a5 b3 a2 b5 a6 b1 a1 b6 a1 b3 a5 b3 a2 b6 a2 b3 a1 b3 a2 b2 a1 b1 a3 b3 a1
    b3 a4 b9"""


FIRST = [("ident", P), ("wk", C), ("wq", C), ("wv", C), ("bo", C), ("rel", 2 * (R + 1)), ("head", HH)]
SECOND = [("near", WIN), ("causal", P), ("wo", C), ("wr", C), ("wkf", C), ("wvf", C), ("mu", 2)]


def build(nc, x, first, second, wq1, wk1, wv1, wo1, wg, w1, w2, w3, c_pe, c_pe0, out):
    ctx = ExitStack()
    with ctx:
        ctx.enter_context(nc.allow_non_contiguous_dma(reason="small tables laid out once"))

        def sb(name, shape, dt=F32):
            return ctx.enter_context(nc.sbuf_tensor(name, shape, dt))

        def sem(name):
            return ctx.enter_context(nc.semaphore(name))

        def columns(name, fields):
            t = sb(name, [P, sum(n for _, n in fields)])
            part, at = {}, 0
            for field, n in fields:
                part[field] = t[:, at:at + n]
                at += n
            return t, part

        first_sb, part = columns("first_sb", FIRST)
        ident, wk_sb, wq_sb, wv_sb, bo_sb = (part[n] for n in ("ident", "wk", "wq", "wv", "bo"))
        reltab = part["rel"].rearrange("p (k r) -> p k r", k=2)
        relk0, relv0 = reltab[:, 0, 0:1], reltab[:, 1, 0:1]
        headmask = part["head"]
        second_sb, part = columns("second_sb", SECOND)
        near = part["near"].rearrange("p (w r) -> p w r", r=R)
        causal_f, wo_sb, wr_sb, wkf_sb, wvf_sb, mu = (part[n] for n in ("causal", "wo", "wr", "wkf", "wvf", "mu"))
        causal = sb("causal", [P, P], BF16)
        ident_b = sb("ident_b", [P, P], BF16)
        reld = sb("reld", [P, 2, 2, R])
        rotk = sb("rotk", [P, R, HH, R])
        rotv = sb("rotv", [P, R, HALF, HW])
        omu = sb("omu", [P, 2])
        wq1_sb = sb("wq1_sb", [P, H1, C])
        wk1_sb = sb("wk1_sb", [P, C])
        wv1_sb = sb("wv1_sb", [P, C])
        wo1_sb = sb("wo1_sb", [P, H1, C])
        wg_sb = sb("wg_sb", [P, E])
        w1_sb = sb("w1_sb", [P, E, HF])
        w3_sb = sb("w3_sb", [P, E, HF])
        w2_sb = sb("w2_sb", [P, E, len(KT), C])
        pe_sb = sb("pe_sb", [P, N])
        pe0_sb = sb("pe0_sb", [P, 1])

        x_sb = sb("x_sb", [P, TT, C])
        xb = sb("xb", [P, TT, C])
        xT = sb("xT", [P, N])
        qkT = sb("qkT", [P, 2, N])
        parts = sb("parts", [P, 2, 3, N], BF16)
        qs = sb("qs", [P, HP, N], BF16)
        ks = sb("ks", [P, HP, N], BF16)
        vp = sb("vp", [P, TT, H0, STRIP])
        cT = sb("cT", [P, HALF, N])
        cN = sb("cN", [P, TT, H0, R])
        corr = sb("corr", [P, 2, 2, WG, R])
        prob = sb("prob", [P, 2, 2, N])
        pwin = sb("pwin", [P, 2, 2, WG, R])
        band = sb("band", [P, TT, H0, R])
        probT = sb("probT", [P, 2, 2, TT, P])
        negmax = sb("negmax", [P, PAIRS, 2])
        rowsum = sb("rowsum", [P, TT, H0])
        rinv = sb("rinv", [P, TT, H0])
        ctxs = sb("ctxs", [P, 2, P])
        ctxn = sb("ctxn", [P, TT, H0, D0])
        bandT = sb("bandT", [P, HALF, N])
        crel = sb("crel", [P, N])
        ctxT = sb("ctxT", [P, N])
        res_a = sb("res_a", [P, TT, C])
        x1 = sb("x1", [P, TT, C])
        x2 = sb("x2", [P, TT, C])
        xsh = sb("xsh", [P, N + 1])
        rotv_flat = rotv[:].rearrange("p r a c -> p (r a c)").rearrange("p (k n) -> p k n", n=N)
        mixp, mix = cT, cN[:].rearrange("p t h r -> p (t h r)").rearrange("p (a n) -> p a n", a=2)
        rt, kr = qkT[:, 0, :], qkT[:, 1, :]
        ksq, rv = bandT[:, 0, :], bandT[:, 1, :]
        rotv_src = prob[:].rearrange("p a h n -> p (a h n)").rearrange("p (a h r) -> p a h r", a=R, h=HH)

        yT = sb("yT", [P, N])
        q1 = sb("q1", [P, H1, N])
        k1 = sb("k1", [P, N])
        v1 = sb("v1", [P, TT, C])
        p1 = sb("p1", [P, 3, N])
        p1T = sb("p1T", [P, 2, TT, P])
        nm1 = sb("nm1", [P, U1])
        rs1 = sb("rs1", [P, U1])
        ri1 = sb("ri1", [P, U1])
        res_b = sb("res_b", [P, TT, C])
        x3 = sb("x3", [P, TT, C])
        gsm = sb("gsm", [P, 12, TT, E])
        g1 = sb("g1", [P, 8, TT])
        top = sb("top", [P, TT, 8])
        cw = sb("cw", [P, TT, E])
        y = sb("y", [P, TT, C])
        a1 = q1
        hT = q1[:, 0:2 * len(KT), :].rearrange("p (a k) n -> p a k n", a=2)
        th = p1
        ups = sb("ups", [P, 2, N])
        hs = p1T[:].rearrange("p a j i -> p a (j i)")

        class Norm:
            def __init__(self, name):
                self.stats = sb(name + "_stats", [P, TT, 6])
                self.mv = sb(name + "_mv", [P, TT, 2])
                self.hv = sb(name + "_hv", [P, TT])
                self.var = sb(name + "_var", [P, TT])
                self.t = sb(name + "_t", [P, TT])
                self.yr = sb(name + "_yr", [P, TT])
                self.steps = sem(name + "_steps")

        norm_a, norm_b = Norm("norm_a"), Norm("norm_b")
        scratch = nc.dram_tensor("qk_parts", (2, P, 3, N), BF16, kind="Internal").ap()

        psa = ctx.enter_context(nc.psum_tensor("psa", [P, 4, N], F32))
        psb = ctx.enter_context(nc.psum_tensor("psb", [P, 4, N], F32))
        TB, XB = 2, 3

        first_in, second_in, loads, setup_zero = sem("first_in"), sem("second_in"), sem("loads"), sem("setup_zero")
        rotk_ready, setup_v, rotv_part = sem("rotk_ready"), sem("setup_v"), sem("rotv_part")
        rotv_mm, rotv_ev_v, rotv_ev_a, reld_ready = sem("rotv_mm"), sem("rotv_ev_v"), sem("rotv_ev_a"), sem("reld_ready")
        x_in, x_free, x2_ready = sem("x_in"), sem("x_free"), sem("x2_ready")
        xT_mm, xT_ev = sem("xT_mm"), sem("xT_ev")
        proj_mm, q_ev, k_ev, v_ev = sem("proj_mm"), sem("q_ev"), sem("k_ev"), sem("v_ev")
        q_part, k_part = sem("q_part"), sem("k_part")
        q_split, k_split, parts_out, stack_in = sem("q_split"), sem("k_split"), sem("parts_out"), sem("stack_in")
        c_mm, cT_ev_a, cT_ev_v, ct_mm, cN_ev = sem("c_mm"), sem("cT_ev_a"), sem("cT_ev_v"), sem("ct_mm"), sem("cN_ev")
        corr_ready, score_mm, near_added = sem("corr_ready"), sem("score_mm"), sem("near_added")
        max_ready, exp_done, rinv_ready = sem("max_ready"), sem("exp_done"), sem("rinv_ready")
        pT_mm, pT_ev_a, pT_ev_v = sem("pT_mm"), sem("pT_ev_a"), sem("pT_ev_v")
        pwin_ready, band_ready, bandn_ready = sem("pwin_ready"), sem("band_ready"), sem("bandn_ready")
        ctx_mm, ctx_ev, ctxt_mm, ctxn_ready = sem("ctx_mm"), sem("ctx_ev"), sem("ctxt_mm"), sem("ctxn_ready")
        bandT_mm, bandT_ev_a, bandT_ev_v = sem("bandT_mm"), sem("bandT_ev_a"), sem("bandT_ev_v")
        crel_mm, crel_ev, ctxT_mm, ctxT_ready, wo_mm, res_ready = (sem("crel_mm"), sem("crel_ev"), sem("ctxT_mm"),
                                                                    sem("ctxT_ready"), sem("wo_mm"), sem("res_ready"))
        x1_ready, mix_v, ffn_mm, ffn_a = sem("x1_ready"), sem("mix_v"), sem("ffn_mm"), sem("ffn_a")
        rv_ready, ksq_ready = sem("rv_ready"), sem("ksq_ready")
        y_ready, y_free = sem("y_ready"), sem("y_free")
        yT_mm, yT_ev = sem("yT_mm"), sem("yT_ev")
        proj1_mm, kv1_ev, q1_ev = sem("proj1_mm"), sem("kv1_ev"), sem("q1_ev")
        s1_mm, m1_ready, e1_done, r1_ready, n1_ready = sem("s1_mm"), sem("m1_ready"), sem("e1_done"), sem("r1_ready"), sem("n1_ready")
        t1_mm, t1_ev_a, t1_ev_v, a1_mm, a1_ev, o1_mm = sem("t1_mm"), sem("t1_ev_a"), sem("t1_ev_v"), sem("a1_mm"), sem("a1_ev"), sem("o1_mm")
        res1_ready, x3_ready = sem("res1_ready"), sem("x3_ready")
        gate_mm, gate_v, gate_s, gate_a = sem("gate_mm"), sem("gate_v"), sem("gate_s"), sem("gate_a")
        h_mm, tanh_done, up_ev, hs_ready, hT_ready, y_mm, y_added = (sem("h_mm"), sem("tanh_done"), sem("up_ev"), sem("hs_ready"),
                                                              sem("hT_ready"), sem("y_mm"), sem("y_added"))

        PRE = [("pre", i) for i in range(4)]
        MAIN = [("open", 0)]
        for p in range(PAIRS):
            MAIN += [(kind, p) for kind in ("turn0", "score", "turn1", "ctx", "value")]
        LN = range(LN_PARTS)
        MAIN += [("post", i) for i in range(3)] + [("ln0", i) for i in LN]
        MAIN += [("post", i) for i in range(3, 6)]
        END = [("post", 6)] + [("ln1", i) for i in LN]
        steps_b = [("in", 0), ("kv", 0)] + [("q", h) for h in range(H1)] + [("first", 0)]
        for w in range(U1):
            steps_b += [("score", w), ("turn", w), ("use", w)]
        steps_b += [("last", 0)] + [("wo", t) for t in range(TT)] + [("res", 0)] + [("ln0", i) for i in LN]
        steps_b += [("in", 1)] + [("gate", i) for i in range(5)]
        for e in range(E):
            for k in range(len(KT)):
                m = len(KT) * e + k
                steps_b += [("hid", m), ("up", m)]
                if e >= 2 and k == 0:
                    steps_b += [("add", e - 2)]
                if e and k:
                    steps_b += [("down", 2 * (e - 1) + k - 1)]
        steps_b += [("add", E - 2), ("down", 2 * E - 2), ("down", 2 * E - 1), ("add", E - 1)]
        steps_b += [("ln1", i) for i in LN]

        def run_turns(eng, step_a, step_b, order):
            def turn(b, ahead):
                first = [(b, s) for s in MAIN] + [(b + 1, s) for s in PRE] + [(b, s) for s in END]
                second = [(b - 1, s) for s in steps_b]
                for run in order.split() + ["a999", "b999"]:
                    layer, step = (first, step_a) if run[0] == "a" else (second, step_b)
                    for _ in range(int(run[1:])):
                        if layer:
                            c, (kind, i) = layer.pop(0)
                            if kind != "pre" or ahead:
                                step(c, kind, i)

            for kind, i in PRE[0:2] + [("tables", 0)] + PRE[2:] + [("tables", 1)] + MAIN:
                step_a(0, kind, i)
            for kind, i in PRE:
                step_a(1, kind, i)
            for kind, i in END:
                step_a(0, kind, i)
            with eng.Fori(1, NB - 1) as b:
                turn(b, True)
            turn(NB - 1, False)
            for kind, i in steps_b:
                step_b(NB - 1, kind, i)

        def alone(b, k):
            return isinstance(b, int) and b == (0, NB - 1)[k]

        def scores_at(b, p):
            return psb[:, 0:2] if alone(b, 0) and p % 2 else psa[:, 0:2]

        def turned_at(b, par):
            return psb[:, TB] if alone(b, 0) and par else psa[:, TB]

        def scores1_at(b, w):
            return (psa if alone(b, 1) and w % 4 >= 2 else psb)[:, w % 2]

        def turned1_at(b, w):
            return (psa if alone(b, 1) and w % 2 else psb)[:, TB]

        def lead(b):
            return 2 if alone(b, 0) else 1

        def turned_ctx_at(b):
            return (psb if alone(b, 0) else psa)[:, XB, P:2 * P]

        def value_pairs(b, i):
            if not alone(b, 0):
                return [i]
            return [p for p in ((i - 1, i) if i == PAIRS - 1 else (i - 1,)) if p >= 0]

        def turned_unit(b, i):
            i -= 1 if alone(b, 0) else 0
            return i // 2 - 1 if i % 2 == 0 and i >= 2 else None

        def lead1(b):
            return 3 if alone(b, 1) else 2

        def is_first(b):
            return isinstance(b, int) and b == 0

        def units(b, per, k):
            return b * per + k

        def pair(p):
            g, t, q = p // (2 * TT), (p // 2) % TT, p % 2
            return g, t, q, HG * g + 2 * q, P * (t + 1), 0 if t else 1

        LATER = [
            (wq1_sb[:], wq1), (wk1_sb[:], wk1), (wv1_sb[:], wv1), (wo1_sb[:], wo1), (wg_sb[:], wg), (pe_sb[:], c_pe),
            (w1_sb[:], w1), (w3_sb[:], w3),
            (w2_sb[:, :, 0, :], w2[0:128]), (w2_sb[:, :, 1, :], w2[128:256]), (w2_sb[0:96, :, 2, :], w2[256:352]),
        ]
        STACK = [(t, par, w) for w in range(2) for t in range(len(QPART)) for par in range(2)]

        block = ctx.enter_context(nc.Block())

        @block.sync
        def _(sp):
            def stack(b):
                for w, split in enumerate((q_split, k_split)):
                    sp.wait_ge(split, units(b, 3, 3))
                    sp.dma_start(scratch[w], parts[:, w]).then_inc(parts_out, 16)
                sp.wait_ge(parts_out, units(b, 32, 32))
                for t, par, w in STACK:
                    dst = (qs, ks)[w][64 * par + D0 * t:64 * par + D0 * t + D0]
                    src = scratch[w, :, (QPART, KPART)[w][t], :].rearrange("(hp par c) n -> par c hp n", par=2, c=D0)[par]
                    sp.dma_start(dst, src).then_inc(stack_in, 16)

            sp.dma_start(x_sb[:], x[0:1].rearrange("b (t p) c -> p (b t) c", p=P)).then_inc(x_in, 16)
            sp.dma_start(first_sb[:], first).then_inc(first_in, 16)
            sp.dma_start(pe0_sb[:], c_pe0).then_inc(y_free, 16)
            sp.dma_start(second_sb[:], second).then_inc(second_in, 16)
            stack(0)
            for dst, src in LATER:
                sp.dma_start(dst, src).then_inc(loads, 16)
            sp.wait_ge(x_free, 1)
            sp.wait_ge(xT_mm, 1)
            sp.dma_start(x_sb[:], x[1:2].rearrange("b (t p) c -> p (b t) c", p=P)).then_inc(x_in, 16)
            stack(1)
            with sp.Fori(1, NB - 1) as b:
                sp.wait_ge(x_free, b + 1)
                sp.wait_ge(xT_mm, 2 * b + 1)
                sp.dma_start(x_sb[:], x[bass.ds(b + 1, 1)].rearrange("b (t p) c -> p (b t) c", p=P)).then_inc(x_in, 16)
                stack(b + 1)
                sp.wait_ge(y_ready, TT * b)
                sp.dma_start(out[bass.ds(b - 1, 1)].rearrange("b (t p) c -> p (b t) c", p=P), y[:]).then_inc(y_free, 16)
            for b in (NB - 2, NB - 1):
                sp.wait_ge(y_ready, TT * (b + 1))
                sp.dma_start(out[b:b + 1].rearrange("b (t p) c -> p (b t) c", p=P), y[:]).then_inc(y_free, 16)
            sp.wait_ge(y_free, 16 * NB + 16)

        @block.gpsimd
        def _(pool):
            pool.memset(vp[:], 0.0).then_inc(setup_zero, 1)
            pool.memset(xsh[:], 0.0).then_inc(setup_zero, 1)
            pool.wait_ge(first_in, 16)

            def spread(b, p):
                g, t, q, h, n, w0 = pair(p)
                if p == 0:
                    pool.wait_ge(cN_ev, units(b, 2, 2))
                if p >= 2:
                    pool.wait_ge(near_added, units(b, PAIRS, p - 1))
                pool.tensor_tensor(corr[:, p % 2, :, w0:WG, :],
                                   cN[:, t, h:h + 2, :].unsqueeze(2).broadcast_to([P, 2, WG - w0, R]),
                                   near[:, w0:WG, :].unsqueeze(1).broadcast_to([P, 2, WG - w0, R]),
                                   ALU.mult).then_inc(corr_ready, 1)

            def window(b, p):
                g, t, q, h, n, w0 = pair(p)
                pool.wait_ge(exp_done, units(b, 2 * PAIRS, 2 * (p + 1)))
                if p >= 2:
                    pool.wait_ge(band_ready, units(b, PAIRS, p - 1))
                pool.tensor_tensor(pwin[:, p % 2, :, w0:WG, :],
                                   prob[:, p % 2, :, n - (WG - w0) * R:n].rearrange("p h (w r) -> p h w r", r=R),
                                   near[:, w0:WG, :].unsqueeze(1).broadcast_to([P, 2, WG - w0, R]),
                                   ALU.mult).then_inc(pwin_ready, 1)

            def step_a(b, kind, i):
                if kind == "pre" and i == 0:
                    pool.wait_ge(x_in, 16 * b + 16)
                    if not is_first(b):
                        pool.wait_ge(res_ready, 2 * b - 1)
                    pool.tensor_tensor(xb[:], x_sb[:], bo_sb[:].unsqueeze(1).broadcast_to([P, TT, C]),
                                       ALU.add).then_inc(x_free, 1)
                if kind == "pre" and i == 1:
                    pool.wait_ge(k_ev, b + 1)
                    pool.wait_ge(k_part, b + 1)
                    pool.tensor_tensor(parts[:, 1, 1, :], qkT[:, 1, :], parts[:, 1, 0, :], ALU.subtract).then_inc(k_split, 1)
                    pool.tensor_tensor(qkT[:, 1, :], qkT[:, 1, :], parts[:, 1, 0, :], ALU.subtract).then_inc(k_split, 1)
                    pool.wait_ge(k_split, units(b, 3, 2))
                    pool.tensor_tensor(parts[:, 1, 2, :], qkT[:, 1, :], parts[:, 1, 1, :], ALU.subtract).then_inc(k_split, 1)
                if kind == "tables" and i == 1:
                    pool.wait_ge(second_in, 16)
                if kind == "open":
                    spread(b, 0)
                    spread(b, 1)
                if kind == "turn0":
                    window(b, i)
                if kind == "score" and i + 2 < PAIRS:
                    spread(b, i + 2)

            def step_b(b, kind, i):
                if kind == "up":
                    e, k = i // len(KT), i % len(KT)
                    kn = KT[k][1]
                    pool.wait_ge(up_ev, units(b, NH, i + 1))
                    pool.wait_ge(hs_ready, units(b, NH, i + 1))
                    if k == 0 and e >= 2:
                        pool.wait_ge(y_mm, units(b, E, e - 1))
                    pool.tensor_tensor(hT[0:kn, e % 2, k, :], hs[0:kn, i % 2, :], ups[0:kn, i % 2, :],
                                       ALU.mult).then_inc(hT_ready, 1)

            run_turns(pool, step_a, step_b, POOL_ORDER)

        @block.tensor
        def _(pe):
            def transpose_tiles(bank, src, done):
                for t in range(TT):
                    ins = pe.transpose(bank[:, P * t:P * t + P], src[:, t, :], ident[:])
                ins.then_inc(done, 1)

            pe.wait_ge(first_in, 16)

            def scores(b, p):
                g, t, q, h, n, w0 = pair(p)
                if p == 0:
                    pe.wait_ge(stack_in, 16 * len(STACK) * (b + 1))
                    pe.wait_ge(cN_ev, units(b, 2, 2))
                elif p >= lead(b):
                    pe.wait_ge(exp_done, units(b, 2 * PAIRS, 2 * (p + 1 - lead(b))))
                for par in range(2):
                    s = 64 * par
                    pe.matmul(scores_at(b, p)[:, par, 0:n], qs[s:s + KS, h // 2, P * t:P * t + P], ks[s:s + KS, h // 2, 0:n],
                              start=True, stop=False)
                for par in range(2):
                    ins = pe.matmul(scores_at(b, p)[:, par, n - P:n], ident_b[:], causal[:], start=False, stop=True)
                ins.then_inc(score_mm, 1)

            def turn_prob(b, p, par):
                g, t, q, h, n, w0 = pair(p)
                if par == 0:
                    pe.wait_ge(exp_done, units(b, 2 * PAIRS, 2 * (p + 1)))
                    if p and alone(b, 0):
                        pe.wait_ge(pT_ev_a, units(b, PAIRS, p))
                    elif p:
                        pe.wait_ge(pT_ev_v, units(b, PAIRS, p))
                elif not alone(b, 0):
                    pe.wait_ge(pT_ev_a, units(b, PAIRS, p + 1))
                elif p:
                    pe.wait_ge(pT_ev_v, units(b, PAIRS, p))
                for j in range(t + 1):
                    ins = pe.transpose(turned_at(b, par)[:, P * j:P * j + P], prob[:, p % 2, par, P * j:P * j + P], ident[:])
                ins.then_inc(pT_mm, 1)

            def values(b, p):
                g, t, q, h, n, w0 = pair(p)
                pe.wait_ge(pT_ev_a, units(b, PAIRS, p + 1))
                pe.wait_ge(pT_ev_v, units(b, PAIRS, p + 1))
                if q == 0 and p and not alone(b, 0):
                    pe.wait_ge(ctxn_ready, units(b, U0, p // 2))
                for j in range(t + 1):
                    for par in range(2):
                        s = STRIP * (2 * q + par)
                        ins = pe.matmul(psa[s:s + STRIP, XB, 0:P], vp[:, j, h + par, :], probT[:, p % 2, par, j, :],
                                        start=(j == 0), stop=(j == t))
                ins.then_inc(ctx_mm, 1)

            def turn_ctx(b, u):
                pe.wait_ge(ctx_ev, units(b, U0, u + 1))
                if alone(b, 0) and u:
                    pe.wait_ge(ctxn_ready, u)
                pe.transpose(turned_ctx_at(b), ctxs[:, u % 2, :], ident[:]).then_inc(ctxt_mm, 1)

            def step_a(b, kind, i):
                if kind == "tables" and i == 1:
                    pe.wait_ge(rotv_part, R)
                    for r in range(R):
                        at = P * (r % RB)
                        pe.transpose(psb[:, r // RB, at:at + P], rotv_src[:, r].rearrange("p h r -> p (h r)"),
                                     ident[:]).then_inc(rotv_mm, 1)
                    pe.wait_ge(rotv_ev_v, 2)
                    pe.wait_ge(rotv_ev_a, 2)
                    pe.wait_ge(second_in, 16)
                    pe.wait_ge(setup_v, 3)
                if kind == "pre" and i == 0:
                    pe.wait_ge(x_in, 16 * b + 16)
                    if not is_first(b):
                        pe.wait_ge(xT_ev, 2 * b)
                    transpose_tiles(psa[:, XB, :], x_sb, xT_mm)
                if kind == "pre" and i == 1:
                    pe.wait_ge(xT_ev, units(b, 2, 1))
                    if not is_first(b):
                        pe.wait_ge(ffn_a, 2 * b)
                        pe.wait_ge(rv_ready, b)
                    pe.matmul(psa[:, 1, :], wk_sb[:], xT[:], start=True, stop=True).then_inc(proj_mm, 1)
                    pe.matmul(psa[:, 0, :], wq_sb[:], xT[:], start=True, stop=True).then_inc(proj_mm, 1)
                    for t in range(TT):
                        ins = pe.matmul(psa[:, TB, P * t:P * t + P], xT[:, P * t:P * t + P], wv_sb[:], start=True, stop=True)
                    ins.then_inc(proj_mm, 1)
                if kind == "pre" and i == 2:
                    pe.wait_ge(q_ev, b + 1)
                    pe.wait_ge(v_ev, b + 1)
                    for r in range(R):
                        if is_first(b):
                            pe.wait_ge(rotk_ready, r + 1)
                        for half in range(HALF):
                            s = HW * half
                            ins = pe.matmul(psa[:, TB + half, STRIP * r:STRIP * r + STRIP],
                                            rotk[s:s + HW, r].rearrange("p h r -> p (h r)"),
                                            qkT[s:s + HW, 0, :].rearrange("p (a r) -> p r a", r=R)[:, r, :],
                                            start=True, stop=True)
                    ins.then_inc(c_mm, 1)
                if kind == "pre" and i == 3:
                    pe.wait_ge(cT_ev_a, b + 1)
                    pe.wait_ge(cT_ev_v, b + 1)
                    pe.wait_ge(k_part, b + 1)
                    pe.wait_ge(q_part, b + 1)
                    for t in range(TT):
                        for half in range(HALF):
                            at = 2 * P * (t % 2) + P * half
                            ins = pe.transpose(psa[:, t // 2, at:at + P], cT[:, half, P * t:P * t + P], ident[:])
                        if t % 2:
                            ins.then_inc(ct_mm, 1)
                if kind == "open":
                    for p in range(lead(b)):
                        scores(b, p)
                if kind == "turn0":
                    turn_prob(b, i, 0)
                if kind == "score" and i + lead(b) < PAIRS:
                    scores(b, i + lead(b))
                if kind == "turn1":
                    turn_prob(b, i, 1)
                if kind == "ctx" and turned_unit(b, i) is not None:
                    turn_ctx(b, turned_unit(b, i))
                if kind == "value":
                    for p in value_pairs(b, i):
                        values(b, p)
                if kind == "post" and i == 0:
                    turn_ctx(b, U0 - 1)
                    pe.wait_ge(bandn_ready, b + 1)
                    for half in range(HALF):
                        for t in range(TT):
                            ins = pe.transpose(psa[:, half, P * t:P * t + P],
                                               band[:, t, HH * half:HH * half + HH, :].rearrange("p h r -> p (h r)"), ident[:])
                        ins.then_inc(bandT_mm, 1)
                if kind == "post" and i == 1:
                    pe.wait_ge(ctxn_ready, units(b, U0, U0))
                    for t in range(TT):
                        ins = pe.transpose(psa[:, TB, P * t:P * t + P], ctxn[:, t].rearrange("p h c -> p (h c)"), ident[:])
                    ins.then_inc(ctxT_mm, 1)
                    pe.wait_ge(bandT_ev_a, b + 1)
                    pe.wait_ge(bandT_ev_v, b + 1)
                    for r in range(R):
                        for half in range(HALF):
                            s = HW * half
                            ins = pe.matmul(psa[s:s + HW, XB, STRIP * r:STRIP * r + STRIP], rotv[:, r, half, :],
                                            bandT[:, half, :].rearrange("p (a r) -> p r a", r=R)[:, r, :],
                                            start=True, stop=True)
                    ins.then_inc(crel_mm, 1)
                if kind == "post" and i == 2:
                    pe.wait_ge(ctxT_ready, b + 1)
                    for t in range(TT):
                        ins = pe.matmul(psa[:, 0, P * t:P * t + P], ctxT[:, P * t:P * t + P], wo_sb[:], start=True, stop=True)
                    ins.then_inc(wo_mm, 1)
                if kind == "post" and i == 3:
                    pe.wait_ge(x1_ready, units(b, TT, TT))
                    transpose_tiles(psa[:, XB, :], x1, xT_mm)
                if kind == "post" and i == 4:
                    pe.wait_ge(mix_v, units(b, 4, 4))
                    pe.matmul(psa[:, 1, :], wkf_sb[:], mix[:, 1, :], start=True, stop=True).then_inc(ffn_mm, 1)
                    for t in range(TT):
                        ins = pe.matmul(psa[:, 0, P * t:P * t + P], mix[:, 0, P * t:P * t + P], wr_sb[:], start=True, stop=True)
                    ins.then_inc(ffn_mm, 1)
                if kind == "post" and i == 5:
                    pe.wait_ge(ksq_ready, b + 1)
                    for t in range(TT):
                        ins = pe.matmul(psa[:, TB, P * t:P * t + P], ksq[:, P * t:P * t + P], wvf_sb[:], start=True, stop=True)
                    ins.then_inc(ffn_mm, 1)

            def scores1(b, w):
                h, t = w // TT, w % TT
                n = P * (t + 1)
                banks = 4 if alone(b, 1) else 2
                if w >= banks:
                    pe.wait_ge(e1_done, units(b, U1, w + 1 - banks))
                pe.matmul(scores1_at(b, w)[:, 0:n], q1[:, h, P * t:P * t + P], k1[:, 0:n], start=True, stop=False)
                pe.matmul(scores1_at(b, w)[:, n - P:n], ident_b[:], causal[:], start=False, stop=True).then_inc(s1_mm, 1)

            def wait_p1T(b, w):
                pe.wait_ge(t1_ev_v if w % 2 else t1_ev_a, units(b, U1 // 2, w // 2 + 1))

            def turn1(b, w):
                t = w % TT
                pe.wait_ge(n1_ready, units(b, U1, w + 1))
                if w >= 1 and not alone(b, 1):
                    wait_p1T(b, w - 1)
                elif w >= 2:
                    wait_p1T(b, w - 2)
                for j in range(t + 1):
                    ins = pe.transpose(turned1_at(b, w)[:, P * j:P * j + P], p1[:, w % 3, P * j:P * j + P], ident[:])
                ins.then_inc(t1_mm, 1)

            def values1(b, w):
                h, t = w // TT, w % TT
                wait_p1T(b, w)
                if t == 0 and h:
                    pe.wait_ge(a1_ev, units(b, H1, h))
                for j in range(t + 1):
                    ins = pe.matmul(psb[:, XB, P * t:P * t + P], v1[:, j, :], p1T[:, w % 2, j, :],
                                    start=(j == 0), stop=(j == t))
                ins.then_inc(a1_mm, 1)

            def step_b(b, kind, i):
                if kind == "in" and i == 0:
                    pe.wait_ge(x2_ready, TT * (b + 1))
                    pe.wait_ge(y_added, TT * E * b + 1)
                    pe.wait_ge(loads, 16 * len(LATER))
                    transpose_tiles(psb[:, XB, :], x2, yT_mm)
                if kind == "kv":
                    pe.wait_ge(yT_ev, units(b, 2, 1))
                    pe.matmul(psb[:, 0, :], wk1_sb[:], yT[:], start=True, stop=True).then_inc(proj1_mm, 1)
                    for t in range(TT):
                        ins = pe.matmul(psb[:, 1, P * t:P * t + P], yT[:, P * t:P * t + P], wv1_sb[:], start=True, stop=True)
                    ins.then_inc(proj1_mm, 1)
                if kind == "q":
                    if i >= 2:
                        pe.wait_ge(q1_ev, units(b, H1, i - 1))
                    pe.matmul(psb[:, TB + i % 2, :], wq1_sb[:, i, :], yT[:], start=True, stop=True).then_inc(proj1_mm, 1)
                if kind == "first":
                    pe.wait_ge(kv1_ev, units(b, 2, 2))
                    pe.wait_ge(q1_ev, units(b, H1, H1))
                    for w in range(lead1(b)):
                        scores1(b, w)
                if kind == "score" and i + lead1(b) < U1:
                    scores1(b, i + lead1(b))
                if kind == "turn":
                    turn1(b, i)
                if kind == "use" and i:
                    values1(b, i - 1)
                if kind == "last":
                    values1(b, U1 - 1)
                if kind == "wo":
                    if i == 0:
                        pe.wait_ge(a1_ev, units(b, H1, H1))
                    for h in range(H1):
                        ins = pe.matmul(psb[:, 0, P * i:P * i + P], a1[:, h, P * i:P * i + P], wo1_sb[:, h, :],
                                        start=(h == 0), stop=(h == H1 - 1))
                    if i == TT - 1:
                        ins.then_inc(o1_mm, 1)
                if kind == "in" and i == 1:
                    pe.wait_ge(x3_ready, units(b, TT, TT))
                    transpose_tiles(psb[:, XB, :], x3, yT_mm)
                if kind == "gate" and i == 0:
                    pe.wait_ge(yT_ev, units(b, 2, 2))
                    for t in range(TT):
                        ins = pe.matmul(psb[:, XB, E * t:E * t + E], yT[:, P * t:P * t + P], wg_sb[:], start=True, stop=True)
                    ins.then_inc(gate_mm, 1)
                if kind in ("hid", "up"):
                    e, k = i // len(KT), i % len(KT)
                    k0, kn = KT[k]
                if kind == "hid":
                    if i >= 2:
                        pe.wait_ge(up_ev, units(b, NH, i - 1))
                    pe.matmul(psb[0:kn, (2 * i) % 3, :], w1_sb[:, e, k0:k0 + kn], yT[:], start=True, stop=True).then_inc(h_mm, 1)
                if kind == "up":
                    if i >= 1:
                        pe.wait_ge(hs_ready, units(b, NH, i))
                    pe.matmul(psb[0:kn, (2 * i + 1) % 3, :], w3_sb[:, e, k0:k0 + kn], yT[:], start=True, stop=True).then_inc(h_mm, 1)
                if kind == "down" and i < 2 * E:
                    e, part = i // 2, i % 2
                    if part == 0:
                        pe.wait_ge(hT_ready, units(b, NH, len(KT) * (e + 1)))
                        if e:
                            pe.wait_ge(y_added, units(b, TT * E, TT * e) + 1)
                        else:
                            pe.wait_ge(gate_s, units(b, NGATE, NGATE))
                    for t in range(2 * part, 2 * part + 2):
                        for k, (k0, kn) in enumerate(KT):
                            ins = pe.matmul(psb[:, XB, P * t:P * t + P], hT[0:kn, e % 2, k, P * t:P * t + P],
                                            w2_sb[0:kn, e, k, :], start=(k == 0), stop=(k == len(KT) - 1))
                    if part:
                        ins.then_inc(y_mm, 1)

            run_turns(pe, step_a, step_b, TENSOR_ORDER)

        @block.scalar
        def _(act):
            act.wait_ge(first_in, 16)

            def exp0(b, p, par):
                g, t, q, h, n, w0 = pair(p)
                if par == 0:
                    act.wait_ge(max_ready, units(b, PAIRS, p + 1))
                    if p >= 2:
                        act.wait_ge(pT_mm, units(b, 2 * PAIRS, 2 * (p - 1)))
                        act.wait_ge(pwin_ready, units(b, PAIRS, p - 1))
                act.activation(prob[:, p % 2, par, 0:n], scores_at(b, p)[:, par, 0:n], ACT.Exp, bias=negmax[:, p, par:par + 1],
                               accum_out=rowsum[:, t, h + par:h + par + 1]).then_inc(exp_done, 1)

            def ctx_copy(b, u):
                act.wait_ge(ctx_mm, units(b, PAIRS, 2 * (u + 1)))
                if u >= 2:
                    act.wait_ge(ctxt_mm, units(b, U0, u - 1))
                act.activation(ctxs[:, u % 2, :], psa[:, XB, 0:P], ACT.Copy).then_inc(ctx_ev, 1)

            def step_a(b, kind, i):
                if kind == "tables" and i == 1:
                    act.wait_ge(y_free, 16)
                    for k in (2, 3):
                        act.wait_ge(rotv_mm, RB * (k + 1))
                        act.activation(rotv_flat[:, k], psb[:, k, :], ACT.Copy).then_inc(rotv_ev_a, 1)
                if kind == "pre" and i == 0:
                    act.wait_ge(xT_mm, units(b, 2, 1))
                    act.activation(xT[:], psa[:, XB, :], ACT.Copy).then_inc(xT_ev, 1)
                if kind == "pre" and i == 1:
                    act.wait_ge(k_ev, b + 1)
                    act.activation(parts[:, 1, 0, :], psa[:, 1, :], ACT.Identity, bias=relk0[:, 0:1]).then_inc(k_part, 1)
                    act.wait_ge(proj_mm, units(b, 3, 2))
                    act.activation(qkT[:, 0, :], psa[:, 0, :], ACT.Copy, scale=SC0).then_inc(q_ev, 1)
                    act.activation(parts[:, 0, 0, :], psa[:, 0, :], ACT.Copy, scale=SC0).then_inc(q_part, 1)
                if kind == "pre" and i == 2:
                    act.wait_ge(c_mm, b + 1)
                    act.activation(cT[:, 0, :].rearrange("p (a r) -> p r a", r=R),
                                   psa[:, TB, :].rearrange("p (r a) -> p r a", r=R), ACT.Copy).then_inc(cT_ev_a, 1)
                if kind == "open":
                    exp0(b, 0, 0)
                    exp0(b, 0, 1)
                if kind == "turn0":
                    g, t, q, h, n, w0 = pair(i)
                    act.wait_ge(pT_mm, units(b, 2 * PAIRS, 2 * i + 1))
                    if i >= 2:
                        act.wait_ge(ctx_mm, units(b, PAIRS, i - 1))
                    act.activation(probT[:, i % 2, 0, 0:t + 1, :].rearrange("p j i -> p (j i)"),
                                   turned_at(b, 0)[:, 0:n], ACT.Copy).then_inc(pT_ev_a, 1)
                if kind in ("turn1", "ctx") and i + 1 < PAIRS:
                    exp0(b, i + 1, 0 if kind == "turn1" else 1)
                if kind == "value":
                    for p in value_pairs(b, i):
                        if p % 2:
                            ctx_copy(b, p // 2)
                if kind == "post" and i == 0:
                    act.wait_ge(bandT_mm, units(b, 2, 1))
                    act.activation(bandT[:, 0, :], psa[:, 0, :], ACT.Copy).then_inc(bandT_ev_a, 1)
                if kind == "post" and i == 1:
                    act.wait_ge(crel_mm, b + 1)
                    act.activation(crel[:].rearrange("p (a r) -> p r a", r=R), psa[:, XB, :].rearrange("p (r a) -> p r a", r=R),
                                   ACT.Identity, bias=relv0[:, 0:1]).then_inc(crel_ev, 1)
                if kind == "post" and i == 3:
                    act.wait_ge(xT_mm, units(b, 2, 2))
                    act.activation(xsh[:, 1:N + 1], psa[:, XB, :], ACT.Copy).then_inc(xT_ev, 1)
                if kind == "post" and i == 4:
                    act.wait_ge(ffn_mm, units(b, 3, 1))
                    act.activation(kr, psa[:, 1, :], ACT.Relu).then_inc(ffn_a, 1)
                    act.wait_ge(ffn_mm, units(b, 3, 2))
                    act.activation(rt, psa[:, 0, :], ACT.Tanh, scale=0.5).then_inc(ffn_a, 1)

            def exp1(b, w):
                n = P * (w % TT + 1)
                act.wait_ge(m1_ready, units(b, U1, w + 1))
                if w >= 3:
                    act.wait_ge(t1_mm, units(b, U1, w - 2))
                act.activation(p1[:, w % 3, 0:n], scores1_at(b, w)[:, 0:n], ACT.Exp, bias=nm1[:, w:w + 1],
                               accum_out=rs1[:, w:w + 1]).then_inc(e1_done, 1)

            def norm1(b, w):
                n = P * (w % TT + 1)
                act.wait_ge(r1_ready, units(b, U1, w + 1))
                act.activation(p1[:, w % 3, 0:n], p1[:, w % 3, 0:n], ACT.Copy, scale=ri1[:, w:w + 1]).then_inc(n1_ready, 1)

            def step_b(b, kind, i):
                if kind == "in":
                    act.wait_ge(yT_mm, units(b, 2, i + 1))
                    act.activation(yT[:], psb[:, XB, :], ACT.Copy).then_inc(yT_ev, 1)
                if kind == "kv":
                    act.wait_ge(proj1_mm, units(b, H1 + 2, 1))
                    act.activation(k1[:], psb[:, 0, :], ACT.Identity, bias=pe0_sb[:, 0:1]).then_inc(kv1_ev, 1)
                    act.wait_ge(proj1_mm, units(b, H1 + 2, 2))
                    act.activation(v1[:].rearrange("p t c -> p (t c)"), psb[:, 1, :], ACT.Copy).then_inc(kv1_ev, 1)
                if kind == "first":
                    exp1(b, 0)
                    exp1(b, 1)
                    norm1(b, 0)
                if kind == "score" and i + 1 < U1:
                    norm1(b, i + 1)
                if kind == "turn" and i + 2 < U1:
                    exp1(b, i + 2)
                if kind == "use" and i % 2 == 0:
                    t = i % TT
                    act.wait_ge(t1_mm, units(b, U1, i + 1))
                    if i >= 2:
                        act.wait_ge(a1_mm, units(b, U1, i - 1))
                    act.activation(p1T[:, 0, 0:t + 1, :].rearrange("p j i -> p (j i)"),
                                   turned1_at(b, i)[:, 0:P * (t + 1)], ACT.Copy).then_inc(t1_ev_a, 1)
                if (kind == "use" and i % TT == 0 and i) or kind == "last":
                    h = i // TT - 1 if kind == "use" else H1 - 1
                    act.wait_ge(a1_mm, units(b, U1, TT * (h + 1)))
                    act.activation(a1[:, h, :], psb[:, XB, :], ACT.Copy).then_inc(a1_ev, 1)
                if kind == "gate" and i == 0:
                    act.wait_ge(gate_v, units(b, 2, 2))
                    act.activation(gsm[:, 1], gsm[:, 0], ACT.Exp).then_inc(gate_a, 1)
                if kind == "hid":
                    kn = KT[i % len(KT)][1]
                    act.wait_ge(h_mm, units(b, 2 * NH, 2 * i + 1))
                    if i >= 3:
                        act.wait_ge(hs_ready, units(b, NH, i - 2))
                    act.activation(th[0:kn, i % 3, :], psb[0:kn, (2 * i) % 3, :], ACT.Tanh, scale=0.5).then_inc(tanh_done, 1)
                if kind == "up":
                    kn = KT[i % len(KT)][1]
                    act.wait_ge(h_mm, units(b, 2 * NH, 2 * i + 2))
                    if i >= 2:
                        act.wait_ge(hT_ready, units(b, NH, i - 1))
                    act.activation(ups[0:kn, i % 2, :], psb[0:kn, (2 * i + 1) % 3, :], ACT.Copy, scale=0.5).then_inc(up_ev, 1)

            run_turns(act, step_a, step_b, SCALAR_ORDER)

        @block.vector
        def _(dve):
            dve.memset(y[:], 0.0).then_inc(y_added, 1)
            dve.wait_ge(first_in, 16)
            for k in range(2):
                for rep in range(2):
                    dve.tensor_scalar(reld[:, k, rep, :], reltab[:, k, 1:R + 1], reltab[:, k, 0:1], None,
                                      ALU.subtract).then_inc(reld_ready, 1)
            dve.wait_ge(setup_zero, 2)

            def layer_norm(b, k, nm, src, dst, ready, part):
                guessed = 2 * TT + 4
                count = [[0, TT + 1, guessed, guessed + 3, guessed + 6, NLN][part]]

                def counted(ins):
                    count[0] += 1
                    ins.then_inc(nm.steps, 1)

                def wait():
                    dve.wait_ge(nm.steps, units(b, 2 * NLN, NLN * k + count[0]))

                if part == 0:
                    for t in range(TT):
                        counted(dve.bn_stats(nm.stats[:, t, :], src[:, t, :]))
                    wait()
                    counted(dve.tensor_copy(nm.t[:], nm.stats[:, :, 0]))
                if part == 1:
                    for t in range(TT):
                        counted(dve.bn_aggr(nm.mv[:, t, :], nm.stats[:, t, :]))
                    wait()
                    counted(dve.tensor_scalar(nm.var[:], nm.mv[:, :, 1], EPS, None, ALU.add))
                    wait()
                    counted(dve.tensor_scalar(nm.t[:].bitcast(I32), nm.var[:].bitcast(I32), 1, None, ALU.logical_shift_right))
                    wait()
                    counted(dve.tensor_scalar(nm.yr[:].bitcast(I32), nm.t[:].bitcast(I32), -1.0, float(MAGIC), ALU.mult, ALU.add))
                if 2 <= part < LN_PARTS - 1:
                    wait()
                    counted(dve.tensor_tensor(nm.t[:], nm.yr[:], nm.yr[:], ALU.mult))
                    wait()
                    counted(dve.scalar_tensor_tensor(nm.hv[:], nm.t[:], -0.5, nm.var[:], ALU.mult, ALU.mult))
                    wait()
                    counted(dve.scalar_tensor_tensor(nm.yr[:], nm.hv[:], 1.5, nm.yr[:], ALU.add, ALU.mult))
                if part == LN_PARTS - 1:
                    wait()
                    for t in range(TT):
                        dve.tensor_scalar(dst[:, t, :], src[:, t, :], nm.mv[:, t, 0:1], nm.yr[:, t:t + 1],
                                          ALU.subtract, ALU.mult).then_inc(ready, 1)

            def flat(a):
                return a[:].rearrange("p t c -> p (t c)")

            def unit_max(b, p):
                g, t, q, h, n, w0 = pair(p)
                nw = (WG - w0) * R
                dve.wait_ge(score_mm, units(b, PAIRS, p + 1))
                dve.wait_ge(corr_ready, units(b, PAIRS, p + 1))
                dve.tensor_tensor(scores_at(b, p)[:, :, n - nw:n], scores_at(b, p)[:, :, n - nw:n],
                                  corr[:, p % 2, :, w0:WG, :].rearrange("p h w r -> p h (w r)"),
                                  ALU.add).then_inc(near_added, 1)
                dve.wait_ge(near_added, units(b, PAIRS, p + 1))
                dve.tensor_reduce(negmax[:, p, :], scores_at(b, p)[:, :, 0:n], AX.X, ALU.max, negate=True).then_inc(max_ready, 1)

            def unit_ctx(b, u):
                g, t = u // TT, u % TT
                dve.wait_ge(ctxt_mm, units(b, U0, u + 1))
                dve.wait_ge(rinv_ready, units(b, PAIRS, 2 * (u + 1)))
                dve.tensor_tensor(ctxn[:, t, HG * g:HG * g + HG, :],
                                  turned_ctx_at(b).rearrange("p (h c) -> p h c", h=HG)[:, :, 0:D0],
                                  rinv[:, t, HG * g:HG * g + HG].unsqueeze(2).broadcast_to([P, HG, D0]),
                                  ALU.mult).then_inc(ctxn_ready, 1)

            def rotation(k, r, dst):
                table = reld[:, k].rearrange("p a r -> p (a r)")
                return dve.tensor_tensor(dst, table[:, R - 1 - r:2 * R - 1 - r].unsqueeze(1).broadcast_to([P, HH, R]),
                                         headmask[:].unsqueeze(2).broadcast_to([P, HH, R]), ALU.mult)

            def step_a(b, kind, i):
                if kind == "tables" and i == 0:
                    dve.wait_ge(reld_ready, 4)
                    for r in range(R):
                        rotation(0, r, rotk[:, r]).then_inc(rotk_ready, 1)
                    for r in range(R):
                        rotation(1, r, rotv_src[:, r]).then_inc(rotv_part, 1)
                if kind == "tables" and i == 1:
                    dve.wait_ge(second_in, 16)
                    dve.tensor_copy(causal[:], causal_f).then_inc(setup_v, 1)
                    dve.tensor_copy(ident_b[:], ident[:]).then_inc(setup_v, 1)
                    dve.tensor_scalar(omu[:], mu[:], -1.0, 1.0, ALU.mult, ALU.add).then_inc(setup_v, 1)
                    for k in range(2):
                        dve.wait_ge(rotv_mm, RB * (k + 1))
                        dve.tensor_copy(rotv_flat[:, k], psb[:, k, :]).then_inc(rotv_ev_v, 1)
                if kind == "pre" and i == 1:
                    dve.wait_ge(proj_mm, units(b, 3, 1))
                    dve.tensor_scalar(qkT[:, 1, :], psa[:, 1, :], relk0[:, 0:1], None, ALU.add).then_inc(k_ev, 1)
                    dve.wait_ge(proj_mm, units(b, 3, 3))
                    dve.tensor_copy(vp[:, :, :, 0:D0], psa[:, TB, :].rearrange("p (t h c) -> p t h c", t=TT, c=D0)).then_inc(v_ev, 1)
                    dve.wait_ge(q_ev, b + 1)
                    dve.wait_ge(q_part, b + 1)
                    dve.tensor_tensor(parts[:, 0, 1, :], qkT[:, 0, :], parts[:, 0, 0, :], ALU.subtract).then_inc(q_split, 1)
                    dve.tensor_tensor(crel[:], qkT[:, 0, :], parts[:, 0, 0, :], ALU.subtract).then_inc(q_split, 1)
                    dve.wait_ge(q_split, units(b, 3, 2))
                    dve.tensor_tensor(parts[:, 0, 2, :], crel[:], parts[:, 0, 1, :], ALU.subtract).then_inc(q_split, 1)
                if kind == "pre" and i == 2:
                    dve.wait_ge(c_mm, b + 1)
                    dve.tensor_copy(cT[:, 1, :].rearrange("p (a r) -> p r a", r=R),
                                    psa[:, XB, :].rearrange("p (r a) -> p r a", r=R)).then_inc(cT_ev_v, 1)
                if kind == "pre" and i == 3:
                    for k in range(2):
                        dve.wait_ge(ct_mm, units(b, 2, k + 1))
                        dve.tensor_copy(cN[:, 2 * k:2 * k + 2].rearrange("p t h r -> p (t h r)"), psa[:, k, :]).then_inc(cN_ev, 1)
                if kind == "open":
                    for p in range(lead(b)):
                        unit_max(b, p)
                if kind == "score" and i + lead(b) < PAIRS:
                    unit_max(b, i + lead(b))
                if kind == "turn1":
                    g, t, q, h, n, w0 = pair(i)
                    dve.wait_ge(pT_mm, units(b, 2 * PAIRS, 2 * i + 2))
                    if i >= 2:
                        dve.wait_ge(ctx_mm, units(b, PAIRS, i - 1))
                    dve.tensor_copy(probT[:, i % 2, 1, 0:t + 1, :].rearrange("p j i -> p (j i)"),
                                    turned_at(b, 1)[:, 0:n]).then_inc(pT_ev_v, 1)
                if kind == "ctx":
                    g, t, q, h, n, w0 = pair(i)
                    dve.wait_ge(exp_done, units(b, 2 * PAIRS, 2 * (i + 1)))
                    dve.reciprocal(rinv[:, t, h:h + 2], rowsum[:, t, h:h + 2]).then_inc(rinv_ready, 1)
                    if turned_unit(b, i) is not None:
                        unit_ctx(b, turned_unit(b, i))
                if kind == "value":
                    g, t, q, h, n, w0 = pair(i)
                    dve.wait_ge(pwin_ready, units(b, PAIRS, i + 1))
                    dve.tensor_reduce(band[:, t, h:h + 2, :], pwin[:, i % 2, :, w0:WG, :].rearrange("p h w r -> p h r w"),
                                      AX.X, ALU.add).then_inc(band_ready, 1)
                if kind == "post" and i == 0:
                    dve.wait_ge(band_ready, units(b, PAIRS, PAIRS))
                    dve.wait_ge(rinv_ready, units(b, PAIRS, PAIRS))
                    dve.tensor_tensor(band[:].rearrange("p t h r -> p (t h) r"), band[:].rearrange("p t h r -> p (t h) r"),
                                      rinv[:].rearrange("p t h -> p (t h)").unsqueeze(2).broadcast_to([P, TT * H0, R]),
                                      ALU.mult).then_inc(bandn_ready, 1)
                    unit_ctx(b, U0 - 1)
                    dve.wait_ge(bandT_mm, units(b, 2, 2))
                    dve.tensor_copy(bandT[:, 1, :], psa[:, 1, :]).then_inc(bandT_ev_v, 1)
                if kind == "post" and i == 1:
                    dve.wait_ge(ctxT_mm, b + 1)
                    dve.wait_ge(crel_ev, b + 1)
                    dve.tensor_tensor(ctxT[:], psa[:, TB, :], crel[:], ALU.add).then_inc(ctxT_ready, 1)
                if kind == "post" and i == 2:
                    dve.wait_ge(wo_mm, b + 1)
                    dve.wait_ge(x_free, b + 1)
                    dve.tensor_tensor(flat(res_a), psa[:, 0, :], flat(xb), ALU.add).then_inc(res_ready, 1)
                if kind == "ln0":
                    if i == 0:
                        dve.wait_ge(res_ready, units(b, 2, 1))
                    layer_norm(b, 0, norm_a, res_a, x1, x1_ready, i)
                if kind == "post" and i == 3:
                    dve.wait_ge(xT_ev, units(b, 2, 2))
                    for m in range(2):
                        dve.tensor_scalar(mixp[:, m, :], xsh[:, 0:N], omu[:, m:m + 1], None, ALU.mult).then_inc(mix_v, 1)
                        dve.wait_ge(mix_v, units(b, 4, 2 * m + 1))
                        dve.scalar_tensor_tensor(mix[:, m, :], xsh[:, 1:N + 1], mu[:, m:m + 1], mixp[:, m, :],
                                                 ALU.mult, ALU.add).then_inc(mix_v, 1)
                if kind == "post" and i == 4:
                    dve.wait_ge(ffn_a, units(b, 2, 1))
                    dve.tensor_tensor(ksq, kr, kr, ALU.mult).then_inc(ksq_ready, 1)
                if kind == "post" and i == 5:
                    dve.wait_ge(ffn_a, units(b, 2, 2))
                    dve.wait_ge(ffn_mm, units(b, 3, 3))
                    dve.scalar_tensor_tensor(rv, rt, 1.0, psa[:, TB, :], ALU.add, ALU.mult).then_inc(rv_ready, 1)
                if kind == "post" and i == 6:
                    dve.wait_ge(rv_ready, b + 1)
                    dve.wait_ge(x1_ready, units(b, TT, TT))
                    dve.scalar_tensor_tensor(flat(res_a), rv, 0.5, flat(x1), ALU.mult, ALU.add).then_inc(res_ready, 1)
                if kind == "ln1":
                    if i == 0:
                        dve.wait_ge(res_ready, units(b, 2, 2))
                    if i == LN_PARTS - 1 and not is_first(b):
                        dve.wait_ge(res1_ready, b)
                    layer_norm(b, 1, norm_a, res_a, x2, x2_ready, i)

            def max1(b, w):
                n = P * (w % TT + 1)
                dve.wait_ge(s1_mm, units(b, U1, w + 1))
                dve.tensor_reduce(nm1[:, w:w + 1], scores1_at(b, w)[:, 0:n], AX.X, ALU.max, negate=True).then_inc(m1_ready, 1)

            def rowsum1(b, w):
                dve.wait_ge(e1_done, units(b, U1, w + 1))
                dve.reciprocal(ri1[:, w:w + 1], rs1[:, w:w + 1]).then_inc(r1_ready, 1)

            def wide(a):
                return a.unsqueeze(2).broadcast_to([P, TT, E])

            def router(b, part):
                lg = psb[:, XB, 0:TT * E].rearrange("p (t e) -> p t e", e=E)
                steps = [[0, 0, 5, 9, 15][part]]

                def counted(ins):
                    steps[0] += 1
                    ins.then_inc(gate_s, 1)

                def wait():
                    dve.wait_ge(gate_s, units(b, NGATE, steps[0]))

                def then(ins):
                    counted(ins)
                    wait()

                if part == 0:
                    dve.wait_ge(gate_mm, b + 1)
                    dve.tensor_reduce(g1[:, 0, :], lg, AX.X, ALU.max).then_inc(gate_v, 1)
                    dve.wait_ge(gate_v, units(b, 2, 1))
                    dve.tensor_tensor(gsm[:, 0], lg, wide(g1[:, 0, :]), ALU.subtract).then_inc(gate_v, 1)
                if part == 1:
                    dve.wait_ge(gate_a, b + 1)
                    then(dve.tensor_reduce(g1[:, 1, :], gsm[:, 1], AX.X, ALU.add))
                    then(dve.reciprocal(g1[:, 2, :], g1[:, 1, :]))
                    then(dve.tensor_tensor(gsm[:, 2], gsm[:, 1], wide(g1[:, 2, :]), ALU.mult))
                    counted(dve.tensor_copy(g1[:, 5, :], g1[:, 2, :]))
                    for t in range(TT):
                        ins = dve.max(top[:, t, :], gsm[:, 2, t, :])
                    counted(ins)
                if part == 2:
                    wait()
                    then(dve.tensor_tensor(gsm[:, 3], gsm[:, 2], wide(top[:, :, 1]), ALU.is_gt))
                    then(dve.tensor_tensor(gsm[:, 4], gsm[:, 2], wide(top[:, :, 1]), ALU.is_equal))
                    then(dve.tensor_reduce(g1[:, 3, :], gsm[:, 3], AX.X, ALU.add))
                    counted(dve.tensor_scalar(g1[:, 4, :], g1[:, 3, :], -1.0, 2.0, ALU.mult, ALU.add))
                if part == 3:
                    src = 4
                    for k, s in enumerate((1, 2, 4)):
                        wait()
                        then(dve.tensor_copy(gsm[:, 5 + k, :, 0:s], gsm[:, src, :, 0:s]))
                        counted(dve.tensor_tensor(gsm[:, 5 + k, :, s:E], gsm[:, src, :, s:E], gsm[:, src, :, 0:E - s], ALU.add))
                        src = 5 + k
                if part == 4:
                    wait()
                    then(dve.tensor_tensor(gsm[:, 8], gsm[:, 7], wide(g1[:, 4, :]), ALU.is_le))
                    then(dve.tensor_tensor(gsm[:, 9], gsm[:, 8], gsm[:, 4], ALU.mult))
                    then(dve.tensor_tensor(gsm[:, 10], gsm[:, 9], gsm[:, 3], ALU.add))
                    then(dve.tensor_tensor(gsm[:, 11], gsm[:, 10], gsm[:, 2], ALU.mult))
                    then(dve.tensor_tensor(g1[:, 5, :], top[:, :, 0], top[:, :, 1], ALU.add))
                    then(dve.tensor_scalar(g1[:, 6, :], g1[:, 5, :], 1e-20, None, ALU.add))
                    then(dve.reciprocal(g1[:, 7, :], g1[:, 6, :]))
                    counted(dve.tensor_tensor(cw[:], gsm[:, 11], wide(g1[:, 7, :]), ALU.mult))

            def step_b(b, kind, i):
                if kind == "q":
                    dve.wait_ge(proj1_mm, units(b, H1 + 2, i + 3))
                    dve.scalar_tensor_tensor(q1[:, i, :], psb[:, TB + i % 2, :], SC1, pe_sb[:], ALU.mult, ALU.add).then_inc(q1_ev, 1)
                if kind == "first":
                    for w in range(lead1(b)):
                        max1(b, w)
                    rowsum1(b, 0)
                if kind == "score" and i + 1 < U1:
                    rowsum1(b, i + 1)
                if kind == "turn" and i + lead1(b) < U1:
                    max1(b, i + lead1(b))
                if kind == "use" and i % 2:
                    dve.wait_ge(t1_mm, units(b, U1, i + 1))
                    if i >= 2:
                        dve.wait_ge(a1_mm, units(b, U1, i - 1))
                    dve.tensor_copy(p1T[:, 1, 0:i % TT + 1, :].rearrange("p j i -> p (j i)"),
                                    turned1_at(b, i)[:, 0:P * (i % TT + 1)]).then_inc(t1_ev_v, 1)
                if kind == "res":
                    dve.wait_ge(o1_mm, b + 1)
                    dve.tensor_tensor(flat(res_b), psb[:, 0, :], flat(x2), ALU.add).then_inc(res1_ready, 1)
                if kind == "ln0":
                    if i == 0:
                        dve.wait_ge(res1_ready, b + 1)
                    layer_norm(b, 0, norm_b, res_b, x3, x3_ready, i)
                if kind == "gate":
                    router(b, i)
                if kind == "hid":
                    kn = KT[i % len(KT)][1]
                    dve.wait_ge(tanh_done, units(b, NH, i + 1))
                    if i >= 2:
                        dve.wait_ge(hT_ready, units(b, NH, i - 1))
                    dve.scalar_tensor_tensor(hs[0:kn, i % 2, :], th[0:kn, i % 3, :], 1.0, psb[0:kn, (2 * i) % 3, :],
                                             ALU.add, ALU.mult).then_inc(hs_ready, 1)
                if kind == "add":
                    e = i
                    dve.wait_ge(y_mm, units(b, E, e + 1))
                    if e == 0:
                        dve.wait_ge(gate_s, units(b, NGATE, NGATE))
                    if e:
                        dve.wait_ge(y_added, units(b, TT * E, TT * e) + 1)
                    for t in range(TT):
                        dve.scalar_tensor_tensor(res_b[:, t, :], psb[:, XB, P * t:P * t + P], cw[:, t, e:e + 1],
                                                 (res_b if e else x3)[:, t, :], ALU.mult, ALU.add).then_inc(y_added, 1)
                if kind == "ln1":
                    if i == 0:
                        dve.wait_ge(y_added, units(b, TT * E, TT * E) + 1)
                    if i == LN_PARTS - 1:
                        dve.wait_ge(y_free, 16 * b + 16)
                    layer_norm(b, 1, norm_b, res_b, y, y_ready, i)

            run_turns(dve, step_a, step_b, VECTOR_ORDER)


def kernel(L0_attn_x, L0_attn_W_q, L0_attn_W_k, L0_attn_W_v, L0_attn_W_o, L0_attn_b_o, L0_attn_rel_k, L0_attn_rel_v,
           L0_ffn_W_r, L0_ffn_W_k, L0_ffn_W_v, L0_ffn_mu_r, L0_ffn_mu_k, L1_attn_Wq, L1_attn_Wk, L1_attn_Wv, L1_attn_Wo,
           L1_ffn_Wg, L1_ffn_W1, L1_ffn_W2, L1_ffn_W3):
    import concourse.bacc as bacc
    from concourse.bass_utils import run_bass_kernel_spmd

    i = np.arange(P)[:, None]
    back = i + R - np.arange(WIN)[None, :]
    near = ((back >= 0) & (back < CLIP)).astype(np.float32)
    causal = np.where(np.arange(P)[None, :] > i, np.float32(NEG), np.float32(0)).astype(np.float32)
    head = (i // D0 % HH == np.arange(HH)[None, :]).astype(np.float32)
    inv = np.exp(-np.log(np.float32(10000.0)) * (np.arange(0, C, 2, dtype=np.float32) / np.float32(C))).astype(np.float32)
    ang = (np.arange(N, dtype=np.float32)[:, None] * inv[None, :]).astype(np.float32)
    pe = np.zeros((N, C), np.float32)
    pe[:, 0::2], pe[:, 1::2] = np.sin(ang), np.cos(ang)
    rel = [np.tile(t[0:R + 1].T, (H0, 1)) for t in (L0_attn_rel_k, L0_attn_rel_v)]
    fields = {
        "ident": np.eye(P, dtype=np.float32), "near": near, "causal": causal, "head": head,
        "wq": L0_attn_W_q, "wk": L0_attn_W_k, "wv": L0_attn_W_v, "wo": L0_attn_W_o,
        "bo": np.tile(L0_attn_b_o[None, :], (P, 1)), "rel": np.concatenate(rel, axis=1),
        "wr": L0_ffn_W_r.T, "wkf": L0_ffn_W_k.T, "wvf": L0_ffn_W_v.T, "mu": np.stack([L0_ffn_mu_r, L0_ffn_mu_k], axis=1),
    }
    given = {
        "x": L0_attn_x,
        "first": np.concatenate([fields[n] for n, _ in FIRST], axis=1),
        "second": np.concatenate([fields[n] for n, _ in SECOND], axis=1),
        "wq1": L1_attn_Wq.T.reshape(C, H1, C), "wk1": L1_attn_Wk.T, "wv1": L1_attn_Wv.T,
        "wo1": L1_attn_Wo.reshape(C, H1, C).transpose(2, 1, 0), "wg": L1_ffn_Wg.T,
        "w1": L1_ffn_W1.transpose(2, 0, 1), "w2": L1_ffn_W2.transpose(2, 0, 1), "w3": L1_ffn_W3.transpose(2, 0, 1),
        "c_pe": pe.T * np.float32(SC1), "c_pe0": pe[0][:, None],
    }
    nc = bacc.Bacc("TRN2", target_bir_lowering=False, num_devices=1)
    arrays, args = {}, []
    for name, a in given.items():
        a = np.ascontiguousarray(a)
        arrays[f"in_{name}"] = a
        args.append(nc.dram_tensor(f"in_{name}", a.shape, mybir.dt.from_np(a.dtype), kind="ExternalInput").ap())
    out = nc.dram_tensor("out", (NB, N, C), F32, kind="ExternalOutput").ap()
    build(nc, *args, out)
    r = run_bass_kernel_spmd(nc, [arrays], core_ids=[0])
    return r.results[0]["out"]
```
